# Optimizing a Trainium2 kernel written in Bass

```python
import numpy as np
import jax
import jax.numpy as jnp

def _softmax(x, axis=-1):
    return jax.nn.softmax(x, axis=axis)

def _gelu(x):
    return jax.nn.gelu(x, approximate=True)

def _silu(x):
    return jax.nn.silu(x)

def _sigmoid(x):
    return jax.nn.sigmoid(x)

def _layernorm(x, axis=-1, eps=1e-05):
    m = jnp.mean(x, axis=axis, keepdims=True)
    v = jnp.var(x, axis=axis, keepdims=True)
    return (x - m) / jnp.sqrt(v + eps)

def _scatter_add(tgt, idx, src, axis=0):
    return tgt.at[idx].add(src)

def _segment_sum(src, seg, n):
    return jax.ops.segment_sum(src, seg, n)
kernel_name = 'mk_conv_attn_hybrid_d2_conv_nchw256_r4_4fe627'

def setup_inputs(seed: int=0):
    np.random.seed(seed)
    _w = jnp.asarray

    def _rec_inputs():
        import jax
        import jax.numpy as jnp
        _gk = jax.random.key(seed)
        x = -0.0002928 + 1 * jax.random.normal(jax.random.fold_in(_gk, 1), (4, 64, 16, 16), jnp.float32)
        return x
    x = _rec_inputs()

    def _L0_conv_setup():
        import jax, jax.numpy as jnp
        import numpy as np
        CH = 64
        K = 8
        INNER = CH // K
        key = jax.random.key(seed)
        ks = jax.random.split(key, 9)
        B, C, H, W = (4, CH, 16, 16)
        s = 0.02
        return {'x': jax.random.normal(ks[0], (B, C, H, W), dtype=jnp.float32), 'wq': jax.random.normal(ks[1], (INNER, C), dtype=jnp.float32) * s, 'bq': jnp.zeros((INNER,), dtype=jnp.float32), 'wk': jax.random.normal(ks[2], (INNER, C), dtype=jnp.float32) * s, 'bk': jnp.zeros((INNER,), dtype=jnp.float32), 'wv': jax.random.normal(ks[3], (INNER, C), dtype=jnp.float32) * s, 'bv': jnp.zeros((INNER,), dtype=jnp.float32), 'wo': jax.random.normal(ks[4], (C, INNER), dtype=jnp.float32) * s, 'bo': jnp.zeros((C,), dtype=jnp.float32)}
    _L0_conv_all = _L0_conv_setup()
    _L0_conv_in = {k: v for k, v in _L0_conv_all.items() if k in ('wq', 'bq', 'wk', 'bk', 'wv', 'bv', 'wo', 'bo')}
    del _L0_conv_all

    def _L1_attn_setup():
        import jax, jax.numpy as jnp
        import numpy as np
        N_HEAD = 16
        NOPE = 32
        ROPE = 16
        VDIM = 32
        HD = NOPE + ROPE
        WINDOW = 32
        KEEP = 128
        EPS = 1e-06

        def _freqs(T, dim=ROPE, theta=10000.0):
            f = 1.0 / theta ** (np.arange(0, dim, 2, dtype=np.float32) / dim)
            ang = np.outer(np.arange(T, dtype=np.float32), f)
            return (jnp.asarray(np.cos(ang)), jnp.asarray(np.sin(ang)))

        def _rms(x, w):
            return x * jax.lax.rsqrt(jnp.mean(x * x, -1, keepdims=True) + EPS) * w

        def _rope(x, cos, sin):
            T = x.shape[-2]
            c = cos[:T][None, None]
            s = sin[:T][None, None]
            xr, xi = jnp.split(x, 2, -1)
            return jnp.concatenate([xr * c - xi * s, xr * s + xi * c], -1)

        def _attn(q, k, v, mask=None):
            s = jnp.einsum('bhqd,bhkd->bhqk', q, k) / np.float32(np.sqrt(HD))
            if mask is not None:
                s = jnp.where(mask, s, jnp.float32(-1000000000.0))
            return jnp.einsum('bhqk,bhkd->bhqd', jax.nn.softmax(s, -1), v)
        key = jax.random.key(seed)
        ks = jax.random.split(key, 16)
        w = lambda k, shape: jax.random.normal(k, shape, jnp.float32) * 0.02
        B, T, C = (2, 512, 64)
        return {'x': jax.random.normal(ks[0], (B, T, C), jnp.float32), 'Wcq': w(ks[1], (C, 24)), 'q_norm_w': jnp.ones((24,), jnp.float32), 'Wq_nope': w(ks[2], (24, N_HEAD * NOPE)), 'Wq_rope': w(ks[3], (24, N_HEAD * ROPE)), 'Wckv': w(ks[4], (C, 32)), 'kv_norm_w': jnp.ones((32,), jnp.float32), 'Wk_nope': w(ks[5], (32, N_HEAD * NOPE)), 'Wv': w(ks[6], (32, N_HEAD * VDIM)), 'Wk_rope': w(ks[7], (C, ROPE)), 'W_imp': w(ks[8], (C, 1)), 'Wsel_k': w(ks[9], (C, N_HEAD * HD)), 'Wsel_v': w(ks[10], (C, N_HEAD * VDIM)), 'Wwin_k': w(ks[11], (C, N_HEAD * HD)), 'Wwin_v': w(ks[12], (C, N_HEAD * VDIM)), 'Wgate': w(ks[13], (C, 3)), 'Wproj': w(ks[14], (N_HEAD * VDIM, C))}
    _L1_attn_all = _L1_attn_setup()
    _L1_attn_in = {k: v for k, v in _L1_attn_all.items() if k in ('Wcq', 'q_norm_w', 'Wq_nope', 'Wq_rope', 'Wckv', 'kv_norm_w', 'Wk_nope', 'Wv', 'Wk_rope', 'W_imp', 'Wsel_k', 'Wsel_v', 'Wwin_k', 'Wwin_v', 'Wgate', 'Wproj')}
    del _L1_attn_all

    def _L1_ffn_setup():
        import jax, jax.numpy as jnp
        import numpy as np
        from jax import lax
        key = jax.random.key(seed)
        B, T, I, H = (16, 512, 64, 64)
        ks = jax.random.split(key, 13)
        s = 1.0 / np.sqrt(H)

        def w(k, shape):
            return jax.random.uniform(k, shape, jnp.float32, -s, s)
        return {'x': jax.random.normal(ks[0], (B, T, I), jnp.float32), 'U_i': w(ks[1], (I, H)), 'V_i': w(ks[2], (H, H)), 'b_i': w(ks[3], (H,)), 'U_f': w(ks[4], (I, H)), 'V_f': w(ks[5], (H, H)), 'b_f': w(ks[6], (H,)), 'U_c': w(ks[7], (I, H)), 'V_c': w(ks[8], (H, H)), 'b_c': w(ks[9], (H,)), 'U_o': w(ks[10], (I, H)), 'V_o': w(ks[11], (H, H)), 'b_o': w(ks[12], (H,))}
    _L1_ffn_all = _L1_ffn_setup()
    _L1_ffn_in = {k: v for k, v in _L1_ffn_all.items() if k in ('U_i', 'V_i', 'b_i', 'U_f', 'V_f', 'b_f', 'U_c', 'V_c', 'b_c', 'U_o', 'V_o', 'b_o')}
    del _L1_ffn_all
    return {'x': x, 'L0_conv_wq': _L0_conv_in['wq'], 'L0_conv_bq': _L0_conv_in['bq'], 'L0_conv_wk': _L0_conv_in['wk'], 'L0_conv_bk': _L0_conv_in['bk'], 'L0_conv_wv': _L0_conv_in['wv'], 'L0_conv_bv': _L0_conv_in['bv'], 'L0_conv_wo': _L0_conv_in['wo'], 'L0_conv_bo': _L0_conv_in['bo'], 'L1_attn_Wcq': _L1_attn_in['Wcq'], 'L1_attn_q_norm_w': _L1_attn_in['q_norm_w'], 'L1_attn_Wq_nope': _L1_attn_in['Wq_nope'], 'L1_attn_Wq_rope': _L1_attn_in['Wq_rope'], 'L1_attn_Wckv': _L1_attn_in['Wckv'], 'L1_attn_kv_norm_w': _L1_attn_in['kv_norm_w'], 'L1_attn_Wk_nope': _L1_attn_in['Wk_nope'], 'L1_attn_Wv': _L1_attn_in['Wv'], 'L1_attn_Wk_rope': _L1_attn_in['Wk_rope'], 'L1_attn_W_imp': _L1_attn_in['W_imp'], 'L1_attn_Wsel_k': _L1_attn_in['Wsel_k'], 'L1_attn_Wsel_v': _L1_attn_in['Wsel_v'], 'L1_attn_Wwin_k': _L1_attn_in['Wwin_k'], 'L1_attn_Wwin_v': _L1_attn_in['Wwin_v'], 'L1_attn_Wgate': _L1_attn_in['Wgate'], 'L1_attn_Wproj': _L1_attn_in['Wproj'], 'L1_ffn_U_i': _L1_ffn_in['U_i'], 'L1_ffn_V_i': _L1_ffn_in['V_i'], 'L1_ffn_b_i': _L1_ffn_in['b_i'], 'L1_ffn_U_f': _L1_ffn_in['U_f'], 'L1_ffn_V_f': _L1_ffn_in['V_f'], 'L1_ffn_b_f': _L1_ffn_in['b_f'], 'L1_ffn_U_c': _L1_ffn_in['U_c'], 'L1_ffn_V_c': _L1_ffn_in['V_c'], 'L1_ffn_b_c': _L1_ffn_in['b_c'], 'L1_ffn_U_o': _L1_ffn_in['U_o'], 'L1_ffn_V_o': _L1_ffn_in['V_o'], 'L1_ffn_b_o': _L1_ffn_in['b_o']}

def reference(x, L0_conv_wq, L0_conv_bq, L0_conv_wk, L0_conv_bk, L0_conv_wv, L0_conv_bv, L0_conv_wo, L0_conv_bo, L1_attn_Wcq, L1_attn_q_norm_w, L1_attn_Wq_nope, L1_attn_Wq_rope, L1_attn_Wckv, L1_attn_kv_norm_w, L1_attn_Wk_nope, L1_attn_Wv, L1_attn_Wk_rope, L1_attn_W_imp, L1_attn_Wsel_k, L1_attn_Wsel_v, L1_attn_Wwin_k, L1_attn_Wwin_v, L1_attn_Wgate, L1_attn_Wproj, L1_ffn_U_i, L1_ffn_V_i, L1_ffn_b_i, L1_ffn_U_f, L1_ffn_V_f, L1_ffn_b_f, L1_ffn_U_c, L1_ffn_V_c, L1_ffn_b_c, L1_ffn_U_o, L1_ffn_V_o, L1_ffn_b_o):
    import jax
    import jax.numpy as jnp

    def _L0_conv_ref(x, wq, bq, wk, bk, wv, bv, wo, bo):
        import jax, jax.numpy as jnp
        import numpy as np
        CH = 64
        K = 8
        INNER = CH // K
        B, C, H, W = x.shape
        N = H * W
        xf = x.reshape(B, C, N)
        q = jnp.einsum('oc,bcn->bon', wq, xf) + bq[None, :, None]
        k = jnp.einsum('oc,bcn->bon', wk, xf) + bk[None, :, None]
        v = jnp.einsum('oc,bcn->bon', wv, xf) + bv[None, :, None]
        energy = jnp.einsum('bci,bcj->bij', q, k)
        attn = jax.nn.softmax(energy, axis=-1)
        out = jnp.einsum('bcj,bij->bci', v, attn)
        out = jnp.einsum('oc,bcn->bon', wo, out) + bo[None, :, None]
        return out.reshape(B, C, H, W)

    def _L1_attn_ref(x, Wcq, q_norm_w, Wq_nope, Wq_rope, Wckv, kv_norm_w, Wk_nope, Wv, Wk_rope, W_imp, Wsel_k, Wsel_v, Wwin_k, Wwin_v, Wgate, Wproj):
        import jax, jax.numpy as jnp
        import numpy as np
        N_HEAD = 16
        NOPE = 32
        ROPE = 16
        VDIM = 32
        HD = NOPE + ROPE
        WINDOW = 32
        KEEP = 128
        EPS = 1e-06

        def _freqs(T, dim=ROPE, theta=10000.0):
            f = 1.0 / theta ** (np.arange(0, dim, 2, dtype=np.float32) / dim)
            ang = np.outer(np.arange(T, dtype=np.float32), f)
            return (jnp.asarray(np.cos(ang)), jnp.asarray(np.sin(ang)))

        def _rms(x, w):
            return x * jax.lax.rsqrt(jnp.mean(x * x, -1, keepdims=True) + EPS) * w

        def _rope(x, cos, sin):
            T = x.shape[-2]
            c = cos[:T][None, None]
            s = sin[:T][None, None]
            xr, xi = jnp.split(x, 2, -1)
            return jnp.concatenate([xr * c - xi * s, xr * s + xi * c], -1)

        def _attn(q, k, v, mask=None):
            s = jnp.einsum('bhqd,bhkd->bhqk', q, k) / np.float32(np.sqrt(HD))
            if mask is not None:
                s = jnp.where(mask, s, jnp.float32(-1000000000.0))
            return jnp.einsum('bhqk,bhkd->bhqd', jax.nn.softmax(s, -1), v)
        B, T, C = x.shape
        cos, sin = _freqs(T)
        cq = _rms(x @ Wcq, q_norm_w)
        qn = (cq @ Wq_nope).reshape(B, T, N_HEAD, NOPE).transpose(0, 2, 1, 3)
        qr = _rope((cq @ Wq_rope).reshape(B, T, N_HEAD, ROPE).transpose(0, 2, 1, 3), cos, sin)
        q = jnp.concatenate([qn, qr], -1)
        gate = jax.nn.softmax((x @ Wgate).mean(1), -1)
        ckv = _rms(x @ Wckv, kv_norm_w)
        kn = (ckv @ Wk_nope).reshape(B, T, N_HEAD, NOPE).transpose(0, 2, 1, 3)
        v1 = (ckv @ Wv).reshape(B, T, N_HEAD, VDIM).transpose(0, 2, 1, 3)
        kr = (x @ Wk_rope / N_HEAD).reshape(B, T, 1, ROPE).transpose(0, 2, 1, 3)
        kr = _rope(kr, cos, sin)
        k1 = jnp.concatenate([kn, jnp.broadcast_to(kr, (B, N_HEAD, T, ROPE))], -1)
        ii = jnp.arange(T)
        causal = ii[:, None] >= ii[None, :]
        o1 = _attn(q, k1, v1, causal[None, None])
        scores = (x @ W_imp)[..., 0]
        _, idx = jax.lax.top_k(scores, KEEP)
        idx = jnp.sort(idx, 1)
        sel = jnp.take_along_axis(x, idx[..., None], 1)
        ks = (sel @ Wsel_k).reshape(B, KEEP, N_HEAD, HD).transpose(0, 2, 1, 3)
        vs = (sel @ Wsel_v).reshape(B, KEEP, N_HEAD, VDIM).transpose(0, 2, 1, 3)
        ks = jnp.concatenate([ks[..., :NOPE], _rope(ks[..., NOPE:], cos, sin)], -1)
        o2 = _attn(q, ks, vs)
        kw = (x @ Wwin_k).reshape(B, T, N_HEAD, HD).transpose(0, 2, 1, 3)
        vw = (x @ Wwin_v).reshape(B, T, N_HEAD, VDIM).transpose(0, 2, 1, 3)
        kw = jnp.concatenate([kw[..., :NOPE], _rope(kw[..., NOPE:], cos, sin)], -1)
        winmask = causal & (ii[:, None] - ii[None, :] < WINDOW)
        o3 = _attn(q, kw, vw, winmask[None, None])
        g = gate[:, :, None, None, None]
        o = g[:, 0] * o1 + g[:, 1] * o2 + g[:, 2] * o3
        o = o.transpose(0, 2, 1, 3).reshape(B, T, N_HEAD * VDIM)
        return o @ Wproj

    def _L1_ffn_ref(x, U_i, V_i, b_i, U_f, V_f, b_f, U_c, V_c, b_c, U_o, V_o, b_o):
        import jax, jax.numpy as jnp
        import numpy as np
        from jax import lax
        B, T, _ = x.shape
        H = U_i.shape[1]
        xt = jnp.swapaxes(x, 0, 1)
        xi = xt @ U_i + b_i
        xf = xt @ U_f + b_f
        xg = xt @ U_c + b_c
        xo = xt @ U_o + b_o
        h0 = jnp.zeros((B, H), x.dtype)
        c0 = jnp.zeros((B, H), x.dtype)

        def step(carry, xs):
            h, c = carry
            xi_t, xf_t, xg_t, xo_t = xs
            i_t = jax.nn.sigmoid(xi_t + h @ V_i)
            f_t = jax.nn.sigmoid(xf_t + h @ V_f)
            g_t = jnp.tanh(xg_t + h @ V_c)
            o_t = jax.nn.sigmoid(xo_t + h @ V_o)
            c_new = h * c + i_t * g_t
            h_new = o_t * jnp.tanh(c_new)
            return ((h_new, c_new), h_new)
        (_, _), hs = lax.scan(step, (h0, c0), (xi, xf, xg, xo))
        return jnp.swapaxes(hs, 0, 1)

    def _gn(v, G=32, eps=1e-05):
        B_, C_, H_, W_ = v.shape
        g = v.reshape(B_, G, C_ // G, H_, W_)
        m = jnp.mean(g, axis=(2, 3, 4), keepdims=True)
        s = jnp.var(g, axis=(2, 3, 4), keepdims=True)
        return ((g - m) / jnp.sqrt(s + eps)).reshape(v.shape)

    def _ln_c(v, eps=1e-06):
        m = jnp.mean(v, axis=1, keepdims=True)
        s = jnp.var(v, axis=1, keepdims=True)
        return (v - m) / jnp.sqrt(s + eps)

    def _ln_t(v, eps=1e-05):
        m = jnp.mean(v, axis=-1, keepdims=True)
        s = jnp.var(v, axis=-1, keepdims=True)
        return (v - m) / jnp.sqrt(s + eps)

    def _to_tokens(v):
        B_, C_, H_, W_ = v.shape
        return v.reshape(B_, C_, H_ * W_).transpose(0, 2, 1)

    def _from_tokens(t, like):
        B_, C_, H_, W_ = like.shape
        return t.transpose(0, 2, 1).reshape(B_, C_, H_, W_)
    x = x + _L0_conv_ref(_gn(x), L0_conv_wq, L0_conv_bq, L0_conv_wk, L0_conv_bk, L0_conv_wv, L0_conv_bv, L0_conv_wo, L0_conv_bo)
    t = _to_tokens(x)
    t = t + _L1_attn_ref(_ln_t(t), L1_attn_Wcq, L1_attn_q_norm_w, L1_attn_Wq_nope, L1_attn_Wq_rope, L1_attn_Wckv, L1_attn_kv_norm_w, L1_attn_Wk_nope, L1_attn_Wv, L1_attn_Wk_rope, L1_attn_W_imp, L1_attn_Wsel_k, L1_attn_Wsel_v, L1_attn_Wwin_k, L1_attn_Wwin_v, L1_attn_Wgate, L1_attn_Wproj)
    t = t + _L1_ffn_ref(_ln_t(t), L1_ffn_U_i, L1_ffn_V_i, L1_ffn_b_i, L1_ffn_U_f, L1_ffn_V_f, L1_ffn_b_f, L1_ffn_U_c, L1_ffn_V_c, L1_ffn_b_c, L1_ffn_U_o, L1_ffn_V_o, L1_ffn_b_o)
    x = _from_tokens(t, x)
    return x

_drawn_inputs = setup_inputs


def setup_inputs(seed=0):
    import zlib

    import numpy as np

    out = dict(_drawn_inputs(seed))
    spreads = {'L0_conv_bq': (0.0, 0.8),
     'L0_conv_bk': (0.0, 2.0),
     'L0_conv_bv': (0.0, 0.8),
     'L0_conv_bo': (0.0, 0.1),
     'L1_attn_q_norm_w': (1.0, 0.6),
     'L1_attn_kv_norm_w': (1.0, 0.6)}
    factors = {'L0_conv_wq': 8.0,
     'L0_conv_wk': 8.0,
     'L0_conv_wv': 8.0,
     'L0_conv_wo': 8.0,
     'L1_attn_Wcq': 8.0,
     'L1_attn_Wq_nope': 8.0,
     'L1_attn_Wq_rope': 8.0,
     'L1_attn_Wckv': 8.0,
     'L1_attn_Wk_nope': 8.0,
     'L1_attn_Wv': 8.0,
     'L1_attn_Wk_rope': 34.592,
     'L1_attn_W_imp': 8.0,
     'L1_attn_Wsel_k': 8.0,
     'L1_attn_Wsel_v': 8.0,
     'L1_attn_Wwin_k': 8.0,
     'L1_attn_Wwin_v': 8.0,
     'L1_attn_Wgate': 8.0,
     'L1_attn_Wproj': 7.676,
     'L1_ffn_V_i': 8.0,
     'L1_ffn_b_i': 8.0,
     'L1_ffn_V_c': 3.767,
     'L1_ffn_b_c': 3.175,
     'L1_ffn_V_o': 8.0,
     'L1_ffn_b_o': 8.0}
    for name, (base, spread) in spreads.items():
        noise = np.random.default_rng([zlib.crc32(name.encode()), seed]).standard_normal(out[name].shape)
        drawn = base * np.exp(spread * noise) if base else spread * noise
        out[name] = jnp.asarray(drawn.astype(out[name].dtype))
    for name, factor in factors.items():
        out[name] = (out[name] * factor).astype(out[name].dtype)
    return out
```

```python
from contextlib import ExitStack

import concourse.bass as bass
from concourse import mybir

F32 = mybir.dt.float32
BF16 = mybir.dt.bfloat16
ALU = mybir.AluOpType
ACT = mybir.ActivationFunctionType
AX = mybir.AxisListType

NB, CH, T = 4, 64, 256
INNER = 8
NH, NOPE, ROPE, VD = 16, 32, 16, 32
HD = NOPE + ROPE
RQ, RKV = 24, 32
WINDOW, KEEP = 32, 128
NP = NH // 2
TB = T // 128
MAXROW, ROPEROW = 32, 48
NGRP = NH // 4
CQ, CKV, IMP, GATE = 0, RQ, RQ + RKV, RQ + RKV + 1
NCAT = GATE + 3
SCALE = float(HD) ** -0.5
STEPS = 8


def conv_attn_lstm(nc, d, out):
    with ExitStack() as ctx:
        def sb(name, shape, dt=F32):
            return ctx.enter_context(nc.sbuf_tensor(name, shape, dt))

        def sem(name):
            return ctx.enter_context(nc.semaphore(name))

        c = {k: sb("w_" + k, list(d[k].shape)) for k in d if k != "x"}
        ident, ones = c["ident"], c["ones"]
        ident16 = sb("ident16", [128, 128], BF16)
        masks16 = sb("masks16", [128, 4, 128], BF16)
        corner16 = sb("corner16", [128, 2, 32], BF16)
        krw = sb("krw", [CH + 1, 2, 128])
        u_half = sb("u_half", [CH + 1, 3, CH])
        v_half = sb("v_half", [128, 3, CH])

        xc = sb("xc", [128, 2, T])
        yc = sb("yc", [128, 2, T])
        qc, kc = sb("qc", [CH, 2, T]), sb("kc", [CH, 2, T])
        bnc = sb("bnc", [128, 2, 6])
        mvc = sb("mvc", [128, 2, 2])
        gsum = sb("gsum", [128, 4])
        grp = sb("grp", [128, 4])
        gtmp = sb("gtmp", [128, 2])
        grstd = sb("grstd", [128, 2])
        wvo = sb("wvo", [128, CH])
        cst = sb("cst", [128, CH])
        vw = sb("vw", [128, NB * TB, CH])
        cmax = sb("cmax", [128, NB * TB])
        csum = sb("csum", [128, NB * TB])
        crec = sb("crec", [128, NB * TB])
        cp = sb("cp", [128, NB * TB, T])
        cpt = sb("cpt", [128, NB * TB, TB, 128])
        x1 = sb("x1", [128, NB * TB, CH])
        x2 = sb("x2", [128, NB * TB, CH])
        tmp = sb("tmp", [128, NB * TB, CH])
        xn = sb("xn", [128, NB * TB, CH])
        bn = sb("bn", [128, NB * TB, 6])
        mv = sb("mv", [128, NB * TB, 2])
        rstd = sb("rstd", [128, NB * TB])
        xnT = sb("xnT", [CH + 1, NB, T])
        cat = sb("cat", [128, NB * TB, NCAT])
        sq = sb("sq", [128, NB * TB, RQ + RKV])
        ssq, rms = sb("ssq", [128, 2, NB * TB]), sb("rms", [128, 2, NB * TB])
        vare = sb("vare", [128, NB * TB])
        rtmp, rint = sb("rtmp", [128, 16]), sb("rint", [128, 16], mybir.dt.int32)
        cqn = sb("cqn", [128, NB * TB, RQ])
        ckn = sb("ckn", [128, NB * TB, RKV])
        cqT, ckT = sb("cqT", [RQ, NB, T]), sb("ckT", [RKV, NB, T])
        gsm = sb("gsm", [128, NB, 3])
        gm1 = sb("gm1", [128, NB])
        gate = sb("gate", [128, NB, 3])
        diag = sb("diag", [128, NB * TB, 128])
        eqs = sb("eqs", [128, T])
        rank = sb("rank", [128, NB * TB])
        sel = sb("sel", [128, NB, TB])
        pos = sb("pos", [128, TB, NB])
        xsT = sb("xsT", [CH + 1, NB, KEEP])

        cq_b, ck_b = sb("cq_b", [RQ, T]), sb("ck_b", [RKV, T])
        xn_b, xs_b = sb("xn_b", [CH + 1, T]), sb("xs_b", [CH + 1, KEEP])
        gate_b = sb("gate_b", [128, 3])
        QT = sb("QT", [128, NP, 2, T])
        K1, KW = (sb(n, [128, NP, T]) for n in ("K1", "KW"))
        KS = sb("KS", [128, NP, KEEP])
        krp = sb("krp", [128, T])
        V1, VW = (sb(n, [128, TB, NH, VD + 1]) for n in ("V1", "VW"))
        VS = sb("VS", [128, NH, VD + 1])
        ra, rb = sb("ra", [128, 3, T]), sb("rb", [128, 3, T])
        nm = sb("nm", [128, NH, 4])
        cm = sb("cm", [32, NH])
        mx = sb("mx", [128, NP, 128])
        et = sb("et", [128, 3, 512])
        etc = sb("etc", [128, NH, 32])
        orec, ow = sb("orec", [128, 2, 12]), sb("ow", [128, 2, 12])
        oprod = sb("oprod", [128, 2, 12, VD])
        osum = sb("osum", [128, 2, 2, 128])
        oT = sb("oT", [128, NGRP, 128])

        xn2T = sb("xn2T", [CH + 1, T + STEPS, NB])
        x2T = sb("x2T", [CH, NB, T])
        y = sb("y", [CH, NB, T])
        hh = sb("hh", [128, 2 * STEPS, NB])
        hs = sb("hs", [CH, 2, STEPS, NB])
        half = sb("half", [CH, STEPS, NB])
        scan = sb("scan", [CH, 56])
        bank = [ctx.enter_context(nc.psum_tensor(f"bank{i}", [128, 512], F32)) for i in range(8)]

        names = """w_ready x_ready dve act pe pool pool_c iter_ready staged pjd_ready pjd_free pja_ready pja_free
            rp_ready rp_done sm_ready sm_free cn_ready cn_free mx_ready mt_ready mtv_done mta_done
            x2_done q_low hs_ready st_ready ex_done ec_ready ec_done pv_done o_ready o_free oc_ready ot_ready ot_done y_ready
            const_ready h_ready g_in t_gate c_new t_cell hc_ready y_done out_done tail tail_done""".split()
        S = {n: sem(n) for n in names}
        block = ctx.enter_context(nc.Block())
        nw = len(c)
        D = {}
        A_ = {"exp": 0, "cpt1": 9, "cpt3": 10, "gate": 11}
        E_BANK, P_BANK = (6, 7, 0, 1), (2, 3, 4, 5)
        dve_units = [(krp[:, :], "rope", 1)]
        pe_units = [(krw[:, 0, :], krw[:, 1, :], xn_b[:, :])]
        for p in range(NP):
            dve_units.append((QT[:, p, :, :], "rope", 1))
            pe_units.append((c["wqa"][:, p, :], c["wqb"][:, p, :], cq_b[:, :]))
        for p in range(NP):
            dve_units.append((KW[:, p, :], "rope", 1))
            pe_units.append((c["wwa"][:, p, :], c["wwb"][:, p, :], xn_b[:, :]))
        for p in range(0, NP, 2):
            dve_units.append((KS[:, p:p + 2, :], "rope", 2))
            pe_units.append((c["wsa"][:, p:p + 2, :], c["wsb"][:, p:p + 2, :], xs_b[:, :]))
        rope_units = list(dve_units)
        for p in range(0, NP, 2):
            dve_units.append((K1[:, p:p + 2, :], "k1", 1))
        K1_FIRST, ND, NR = len(rope_units), len(dve_units), len(rope_units)

        @block.sync
        def _(sp):
            xv = d["x"].rearrange("(j h) c n -> h c j n", h=2)
            for h in range(2):
                sp.dma_start(xc[64 * h:64 * h + 64, :, :], xv[h]).then_inc(S["x_ready"], 16)
            for k in c:
                sp.dma_start(c[k][...], d[k][...]).then_inc(S["w_ready"], 16)
            sp.wait_ge(S["y_done"], T // STEPS)
            sp.dma_start(out.rearrange("b c n -> c b n"), y[:, :, :]).then_inc(S["out_done"], 16)
            sp.wait_ge(S["out_done"], 16)


        PE = {n: i + 1 for i, n in enumerate(
            "gsum qk wvo vw energy0 energy1 energy2 energy3 ptr0 ptr1 ptr2 ptr3 pv xnT0 xnT1 cat cqT0 cqT1 ckT0 ckT1 "
            "gate srow pos selT".split())}
        TL = {n: i + 1 for i, n in enumerate("xn2a xn2b x2a x2b".split())}

        @block.gpsimd
        def _(pool):
            made = [0]

            def const(ins):
                made[0] += 1
                ins.then_inc(S["pool_c"], 1)
                pool.wait_ge(S["pool_c"], made[0])

            const(nc.gpsimd.memset(xnT[CH:CH + 1, :, :], 1.0))
            const(nc.gpsimd.memset(xsT[CH:CH + 1, :, :], 1.0))
            const(nc.gpsimd.memset(xn2T[CH:CH + 1, :, :], 1.0))
            const(nc.gpsimd.memset(mx[:, :, :], 0.0))
            const(nc.gpsimd.memset(QT[64:128, :, 0, :], 0.0))
            const(nc.gpsimd.memset(QT[0:64, :, 1, :], 0.0))
            const(nc.gpsimd.memset(V1[:, :, :, VD:VD + 1], 1.0))
            const(nc.gpsimd.memset(VW[:, :, :, VD:VD + 1], 1.0))
            const(nc.gpsimd.memset(VS[:, :, VD:VD + 1], 1.0))
            const(nc.gpsimd.memset(hh[:, :, :], 0.0))
            const(nc.gpsimd.memset(scan[:, :], 0.0))
            const(nc.gpsimd.memset(xn2T[0:CH, T:T + STEPS, :], 0.0))
            const(nc.gpsimd.memset(half[:, :, :], 0.5))
            nc.gpsimd.memset(hs[:, 0, :, :], 0.0).then_inc(S["hs_ready"], 1)
            nc.gpsimd.memset(hs[:, 1, :, :], 0.0).then_inc(S["hs_ready"], 1)
            const(nc.gpsimd.memset(scan[:, 1:13:3], 1.0))
            const(nc.gpsimd.memset(scan[:, 17:29:3], 1.0))

            with pool.Fori(0, NB) as b:
                pool.wait_ge(S["iter_ready"], b + 1)
                nc.gpsimd.tensor_copy(cq_b[:, :], cqT[:, b, :]).then_inc(S["staged"], 1)
                nc.gpsimd.tensor_copy(ck_b[:, :], ckT[:, b, :]).then_inc(S["staged"], 1)
                nc.gpsimd.tensor_copy(xn_b[:, :], xnT[:, b, :]).then_inc(S["staged"], 1)
                nc.gpsimd.tensor_copy(xs_b[:, :], xsT[:, b, :]).then_inc(S["staged"], 1)
                nc.gpsimd.tensor_copy(gate_b[:, :], gate[:, b, :]).then_inc(S["staged"], 1)
                for u, (dst, _, n) in enumerate(rope_units):
                    pool.wait_ge(S["pjd_free"], b * ND + u + 1)
                    src = [t[:, u % 3, 0:T] for t in (ra, rb)]
                    if n == 2:
                        src = [t.rearrange("p (g n) -> p g n", g=2) for t in src]
                    if 1 <= u <= NP:
                        for r in range(2):
                            rows = slice(64 * r, 64 * r + 64)
                            if r == 1:
                                pool.wait_ge(S["q_low"], b * NP + u)
                            last = nc.gpsimd.tensor_tensor(dst[rows, r, :], src[0][rows], src[1][rows], ALU.add)
                            if r == 0:
                                last.then_inc(S["q_low"], 1)
                        last.then_inc(S["rp_done"], 1)
                        pool.wait_ge(S["rp_done"], b * NR + u + 1)
                        continue
                    nc.gpsimd.tensor_tensor(dst, src[0], src[1], ALU.add).then_inc(S["rp_done"], 1)
                for qb in range(TB):
                    for g in range(NGRP):
                        n = qb * NGRP + g
                        pool.wait_ge(S["o_free"], b * 8 + n + 1)
                        if g >= 2:
                            pool.wait_ge(S["ot_ready"], b * 8 + n - 1)
                        part = [oprod[:, n % 2, 4 * j:4 * j + 4, :].rearrange("p h v -> p (h v)") for j in range(3)]
                        nc.gpsimd.tensor_tensor(osum[:, n % 2, 0, :], part[0], part[1], ALU.add).then_inc(S["pool"], 1)
                        pool.wait_ge(S["pool"], b * 8 + n + 1)
                        nc.gpsimd.tensor_tensor(osum[:, n % 2, 1, :], osum[:, n % 2, 0, :], part[2],
                                                ALU.add).then_inc(S["oc_ready"], 1)

            pool.wait_ge(S["tail_done"], 4)
            with pool.Fori(0, T // STEPS // 2) as kk:
                k = kk * 2
                for u in range(2):
                    pool.wait_ge(S["h_ready"], (k + u + 1) * STEPS + 1)
                    nc.gpsimd.tensor_tensor(hs[:, u, :, :], hh[0:CH, u * STEPS:(u + 1) * STEPS, :],
                                            half[:, :, :], ALU.mult).then_inc(S["hs_ready"], 1)
                    pool.wait_ge(S["hs_ready"], k + u + 3)
                    cols = bass.ds((k + u) * STEPS, STEPS)
                    nc.gpsimd.tensor_tensor(y[:, :, cols], x2T[:, :, cols],
                                            hs[:, u, :, :].rearrange("p t b -> p b t"),
                                            ALU.add).then_inc(S["y_done"], 1)

        @block.vector
        def _(dve):
            count = [0]

            def inc(ins):
                ins.then_inc(S["dve"], 1)
                count[0] += 1
                return count[0]

            def after(value):
                dve.wait_ge(S["dve"], value)

            def link(ins):
                after(inc(ins))

            v = nc.vector

            def rsqrt(y, x, n):
                i, t = rint[:, 0:n], rtmp[:, 0:n]
                link(v.tensor_scalar(i, x.bitcast(mybir.dt.int32), 1, None, ALU.logical_shift_right))
                link(v.tensor_scalar(y.bitcast(mybir.dt.int32), i, -1.0, float(0x5F3759DF), ALU.mult, ALU.add))
                for _ in range(3):
                    link(v.scalar_tensor_tensor(out=t, in0=y, scalar=-0.5, in1=y, op0=ALU.mult, op1=ALU.mult))
                    link(v.tensor_tensor(t, t, x, ALU.mult))
                    link(v.scalar_tensor_tensor(out=y, in0=t, scalar=1.5, in1=y, op0=ALU.add, op1=ALU.mult))

            dve.wait_ge(S["x_ready"], 32)
            for j in range(2):
                n = inc(v.bn_stats(bnc[:, j, :], xc[:, j, :]))
            after(n)
            for j in range(2):
                n = inc(v.bn_aggr(mvc[:, j, :], bnc[:, j, :]))
            after(n)
            inc(v.tensor_copy(gsum[:, 0:2], mvc[:, :, 0]))
            link(v.tensor_tensor(gtmp[:, :], mvc[:, :, 0], mvc[:, :, 0], ALU.mult))
            D["gsum"] = inc(v.tensor_tensor(gsum[:, 2:4], mvc[:, :, 1], gtmp[:, :], ALU.add))
            dve.wait_ge(S["w_ready"], 16 * nw)
            inc(v.tensor_copy(ident16[:, :], ident[:, :]))
            inc(v.tensor_copy(masks16[:, :, :], c["masks"][:, :, :]))
            inc(v.tensor_copy(corner16[:, :, :], c["corner"][:, :, :]))
            inc(v.tensor_copy(krw[:, :, :], c["wkr"][:, :, :]))
            inc(v.tensor_scalar(u_half[:, 1:3, :], c["u3"][:, 1:3, :], 0.5, None, ALU.mult))
            inc(v.tensor_copy(u_half[:, 0, :], c["u3"][:, 0, :]))
            inc(v.tensor_scalar(v_half[:, 1:3, :], c["v3"][:, 1:3, :], 0.25, None, ALU.mult))
            n = inc(v.tensor_scalar(v_half[:, 0, :], c["v3"][:, 0, :], 0.5, None, ALU.mult))
            after(n)
            link(v.tensor_scalar(krw[0:CH, :, :], c["wkr"][0:CH, :, :], 1.0 / NH, None, ALU.mult))
            dve.wait_ge(S["pe"], PE["gsum"])
            link(v.tensor_copy(grp[:, :], bank[0][:, 0:4]))
            link(v.tensor_tensor(gtmp[:, :], grp[:, 0:2], grp[:, 0:2], ALU.mult))
            link(v.tensor_tensor(gtmp[:, :], grp[:, 2:4], gtmp[:, :], ALU.subtract))
            link(v.tensor_scalar(gtmp[:, :], gtmp[:, :], 1e-5, None, ALU.add))
            rsqrt(grstd[:, :], gtmp[:, :], 2)
            for j in range(2):
                D["yc"] = inc(v.tensor_scalar(yc[:, j, :], xc[:, j, :], grp[:, j:j + 1], grstd[:, j:j + 1],
                                              ALU.subtract, ALU.mult))
            dve.wait_ge(S["pe"], PE["wvo"])
            D["wvo"] = inc(v.tensor_copy(wvo[:, :], bank[2][:, 0:CH]))
            dve.wait_ge(S["pe"], PE["qk"])
            inc(v.tensor_scalar(qc[:, :, :], bank[0][0:CH, :].rearrange("p (j n) -> p j n", j=2), c["bqk"][:, 0:1],
                                None, ALU.add))
            D["qk"] = inc(v.tensor_scalar(kc[:, :, :], bank[1][0:CH, :].rearrange("p (j n) -> p j n", j=2),
                                          c["bqk"][:, 1:2], None, ALU.add))
            dve.wait_ge(S["pe"], PE["vw"])
            for h in range(2):
                inc(v.tensor_copy(vw[:, :, :].rearrange("p (j h k) n -> p j h k n", j=2, h=2)[:, :, h],
                                  bank[3 + h][:, 0:4 * CH].rearrange("p (j k n) -> p j k n", j=2, n=CH)))
            link(v.tensor_copy(cst[:, :], bank[6][:, 0:CH]))
            for j in range(2):
                for t in range(TB):
                    src = bank[5][:, 256 * j + 128 * t:256 * j + 128 * t + 128].rearrange("p (h c) -> p h c", h=2)
                    D["xtok"] = inc(v.tensor_tensor(
                        x1[:, 4 * j + t:4 * j + t + 3:2, :], src,
                        cst[:, :].unsqueeze(1).broadcast_to([128, 2, CH]), ALU.add))
            for e in range(4):
                dve.wait_ge(S["pe"], PE[f"energy{e}"])
                src = bank[E_BANK[e]][:, :].rearrange("p (a n) -> p a n", a=2)
                D[f"cmax{e}"] = inc(v.tensor_reduce(cmax[:, 2 * e:2 * e + 2], src, AX.X, ALU.max, negate=True))
            for e in range(2):
                dve.wait_ge(S["pe"], PE[f"ptr{2 * e}"])
                D[f"cpt{2 * e}"] = inc(v.tensor_copy(
                    cpt[:, 4 * e:4 * e + 2, :, :],
                    bank[P_BANK[2 * e]][:, :].rearrange("p (a k n) -> p a k n", a=2, k=2)))
            dve.wait_ge(S["act"], A_["exp"] + 4 * 2)
            link(v.reciprocal(crec[:, :], csum[:, :]))
            dve.wait_ge(S["pe"], PE["pv"])
            link(v.tensor_tensor(tmp[:, :, :], bank[2][:, :].rearrange("p (a n) -> p a n", n=CH),
                                 crec[:, :].unsqueeze(2).broadcast_to([128, NB * TB, CH]), ALU.mult))
            link(v.tensor_tensor(x1[:, :, :], x1[:, :, :], tmp[:, :, :], ALU.add))

            def layer_norm(dst, src):
                for a in range(NB * TB):
                    n = inc(v.bn_stats(bn[:, a, :], src[:, a, :]))
                after(n)
                for a in range(NB * TB):
                    n = inc(v.bn_aggr(mv[:, a, :], bn[:, a, :]))
                after(n)
                link(v.tensor_scalar(vare[:, :], mv[:, :, 1], 1e-5, None, ALU.add))
                rsqrt(rstd[:, :], vare[:, :], NB * TB)
                for a in range(NB * TB):
                    n = inc(v.tensor_scalar(dst[:, a, :], src[:, a, :], mv[:, a, 0:1], rstd[:, a:a + 1],
                                            ALU.subtract, ALU.mult))
                return n

            D["xn"] = layer_norm(xn, x1)
            for e in range(2):
                dve.wait_ge(S["pe"], PE[f"xnT{e}"])
                D["xnT"] = inc(v.tensor_copy(xnT[0:CH, 2 * e:2 * e + 2, :],
                                             bank[e][0:CH, :].rearrange("p (a n) -> p a n", a=2)))
            dve.wait_ge(S["pe"], PE["cat"])
            link(v.tensor_copy(cat[:, :, :], bank[2][:, 0:8 * NCAT].rearrange("p (a n) -> p a n", n=NCAT)))
            D["cat"] = count[0]
            link(v.tensor_tensor(sq[:, :, :], cat[:, :, 0:IMP], cat[:, :, 0:IMP], ALU.mult))
            inc(v.tensor_reduce(ssq[:, 0, :], sq[:, :, 0:RQ], AX.X, ALU.add))
            link(v.tensor_reduce(ssq[:, 1, :], sq[:, :, RQ:IMP], AX.X, ALU.add))
            inc(v.tensor_scalar(ssq[:, 0, :], ssq[:, 0, :], 1.0 / RQ, 1e-6, ALU.mult, ALU.add))
            link(v.tensor_scalar(ssq[:, 1, :], ssq[:, 1, :], 1.0 / RKV, 1e-6, ALU.mult, ALU.add))
            rsqrt(rms[:, :, :].rearrange("p k a -> p (k a)"), ssq[:, :, :].rearrange("p k a -> p (k a)"), 16)
            inc(v.tensor_tensor(cqn[:, :, :], cat[:, :, CQ:CKV],
                                rms[:, 0, :].unsqueeze(2).broadcast_to([128, 8, RQ]), ALU.mult))
            D["cqn"] = inc(v.tensor_tensor(ckn[:, :, :], cat[:, :, CKV:IMP],
                                           rms[:, 1, :].unsqueeze(2).broadcast_to([128, 8, RKV]), ALU.mult))
            for a in range(8):
                D["diag"] = inc(v.tensor_scalar(diag[:, a, :], ident[:, :], cat[:, a, IMP:IMP + 1], None, ALU.mult))
            for e in range(2):
                dve.wait_ge(S["pe"], PE[f"cqT{e}"])
                inc(v.tensor_scalar(cqT[:, 2 * e:2 * e + 2, :], bank[3 + e][0:RQ, :].rearrange("p (a n) -> p a n", a=2),
                                    c["qn"][:, 0:1], None, ALU.mult))
            for e in range(2):
                dve.wait_ge(S["pe"], PE[f"ckT{e}"])
                inc(v.tensor_scalar(ckT[:, 2 * e:2 * e + 2, :], bank[5 + e][0:RKV, :].rearrange("p (a n) -> p a n", a=2),
                                    c["kvn"][:, 0:1], None, ALU.mult))
            dve.wait_ge(S["pe"], PE["gate"])
            link(v.tensor_copy(gsm[:, :, :], bank[7][:, 0:3 * NB].rearrange("p (b g) -> p b g", g=3)))
            link(v.tensor_reduce(gm1[:, :], gsm[:, :, :], AX.X, ALU.max))
            D["gsm"] = inc(v.tensor_tensor(gsm[:, :, :], gsm[:, :, :],
                                           gm1[:, :].unsqueeze(2).broadcast_to([128, NB, 3]), ALU.subtract))
            dve.wait_ge(S["pe"], PE["srow"])
            for a in range(8):
                row = bank[a // 4][:, 256 * ((a // 2) % 2):256 * ((a // 2) % 2) + 256]
                s = cat[:, a, IMP:IMP + 1]
                link(v.scalar_tensor_tensor(out=eqs[:, :], in0=row, scalar=s, in1=c["tie"][:, a % 2, :],
                                            op0=ALU.is_equal, op1=ALU.mult))
                link(v.scalar_tensor_tensor(out=eqs[:, :], in0=row, scalar=s, in1=eqs[:, :],
                                            op0=ALU.is_gt, op1=ALU.add, accum_out=rank[:, a:a + 1]))
            D["sel"] = inc(v.tensor_scalar(sel[:, :, :], rank[:, :].rearrange("p (b t) -> p b t", t=TB), KEEP - 0.5,
                                           None, ALU.is_lt))
            after(D["sel"])
            dve.wait_ge(S["act"], A_["gate"])
            link(v.tensor_reduce(gm1[:, :], gate[:, :, :], AX.X, ALU.add))
            link(v.reciprocal(gm1[:, :], gm1[:, :]))
            link(v.tensor_tensor(gate[:, :, :], gate[:, :, :], gm1[:, :].unsqueeze(2).broadcast_to([128, NB, 3]),
                                 ALU.mult))
            dve.wait_ge(S["pe"], PE["pos"])
            link(v.tensor_copy(pos[:, :, :], bank[2][:, 0:8].rearrange("p (t b) -> p t b", t=TB)))
            for a in range(8):
                D["psel"] = inc(v.tensor_scalar(diag[:, a, :], c["iota"][:, :], pos[:, a % 2, a // 2:a // 2 + 1],
                                                sel[:, a // 2, a % 2:a % 2 + 1], ALU.is_equal, ALU.mult))
            dve.wait_ge(S["pe"], PE["selT"])
            dve.wait_ge(S["pool_c"], 15)
            v.tensor_copy(xsT[0:CH, :, :], bank[3][0:CH, :].rearrange("p (b n) -> p b n", b=NB)
                          ).then_inc(S["iter_ready"], 1)
            D["phase1"] = count[0]

            with dve.Fori(0, NB) as b:
                u = 0
                for n, (dst, kind, cols) in enumerate(dve_units):
                    src = bank[n % 4]
                    dve.wait_ge(S["pjd_ready"], b * ND + n + 1)
                    if kind == "rope":
                        if u >= 3:
                            dve.wait_ge(S["rp_done"], b * NR + u - 2)
                        C, R = c["cos"][:, :], c["sin"][:, :]
                        A, B = src[:, 0:T], src[:, T:2 * T]
                        a_, b_ = ra[:, u % 3, :], rb[:, u % 3, :]
                        if cols == 2:
                            A, B, a_, b_ = (t.rearrange("p (g n) -> p g n", g=2) for t in (A, B, a_, b_))
                            C, R = (t[:, 0:KEEP].unsqueeze(1).broadcast_to([128, 2, KEEP]) for t in (C, R))
                        v.tensor_tensor(a_, A, C, ALU.mult)
                        v.tensor_tensor(b_, B, R, ALU.mult).then_inc(S["pjd_free"], 1)
                        u += 1
                    else:
                        if n == K1_FIRST:
                            dve.wait_ge(S["rp_done"], b * NR + 1)
                        v.tensor_tensor(dst, src[:, :].rearrange("p (g n) -> p g n", g=2),
                                        krp[:, :].unsqueeze(1).broadcast_to([128, 2, T]),
                                        ALU.add).then_inc(S["pjd_free"], 1)
                for qb in range(TB):
                    nseg = 3 + qb
                    for h in range(NH):
                        n = qb * NH + h
                        dve.wait_ge(S["sm_ready"], b * 32 + n + 1)
                        if h == 0 and qb == 1:
                            dve.wait_ge(S["mt_ready"], b * 2 + 1)
                        v.tensor_reduce(nm[:, h, 0:nseg], bank[n % 4][:, 0:128 * nseg].rearrange(
                            "p (s n) -> p s n", s=nseg), AX.X, ALU.max).then_inc(S["sm_free"], 1)
                    dve.wait_ge(S["sm_free"], b * 32 + qb * 16 + 16)
                    if qb == 1:
                        dve.wait_ge(S["cn_ready"], b + 1)
                        for f in range(2):
                            v.tensor_reduce(cm[:, f:NH:2], bank[4 + f][0:32, 0:32 * NP].rearrange(
                                "p (h n) -> p h n", n=32), AX.X, ALU.max).then_inc(S["cn_free"], 1)
                        dve.wait_ge(S["cn_free"], b * 4 + 2)
                        v.tensor_tensor(nm[:, :, 1], nm[:, :, 0], nm[:, :, 1], ALU.max).then_inc(S["cn_free"], 1)
                        v.tensor_tensor(nm[0:32, :, 3], nm[0:32, :, 3], cm[:, :], ALU.max).then_inc(S["cn_free"], 1)
                        dve.wait_ge(S["cn_free"], b * 4 + 4)
                    v.tensor_scalar(mx[:, :, :].rearrange("p g (f r) -> p (g f) r", f=2)[:, :, MAXROW:MAXROW + 3],
                                    nm[:, :, nseg - 3:nseg], -1.0, None, ALU.mult).then_inc(S["mx_ready"], 1)
                    dve.wait_ge(S["mt_ready"], b * 2 + qb + 1)
                    for e in range(2):
                        v.tensor_copy(QT[MAXROW:MAXROW + 3, 4 * e:4 * e + 4, 0, 128 * qb:128 * qb + 128],
                                      bank[4 + e][MAXROW:MAXROW + 3, :].rearrange("p (g n) -> p g n", g=4)
                                      ).then_inc(S["mtv_done"], 1)
                    for g in range(NGRP):
                        n = qb * NGRP + g
                        dve.wait_ge(S["pv_done"], b * 32 + 4 * n + 4)
                        O = bank[6 + n % 2][:, 0:12 * (VD + 1)].rearrange("p (a n) -> p a n", n=VD + 1)
                        v.reciprocal(orec[:, n % 2, :], O[:, :, VD]).then_inc(S["dve"], 1)
                        dve.wait_ge(S["dve"], D["phase1"] + b * 16 + 2 * n + 1)
                        v.tensor_tensor(ow[:, n % 2, :].rearrange("p (j h) -> p j h", j=3),
                                        orec[:, n % 2, :].rearrange("p (j h) -> p j h", j=3),
                                        gate_b[:, :].unsqueeze(2).broadcast_to([128, 3, 4]),
                                        ALU.mult).then_inc(S["dve"], 1)
                        dve.wait_ge(S["dve"], D["phase1"] + b * 16 + 2 * n + 2)
                        if n >= 2:
                            dve.wait_ge(S["oc_ready"], b * 8 + n - 1)
                        v.tensor_tensor(oprod[:, n % 2, :, :], O[:, :, 0:VD],
                                        ow[:, n % 2, :].unsqueeze(2).broadcast_to([128, 12, VD]),
                                        ALU.mult).then_inc(S["o_free"], 1)
                    dve.wait_ge(S["y_ready"], b * 2 + qb + 1)
                    v.tensor_tensor(x2[:, 2 * b + qb, :], x1[:, 2 * b + qb, :], bank[4][:, 0:CH],
                                    ALU.add).then_inc(S["iter_ready"] if qb == 1 else S["x2_done"], 1)

            dve.wait_ge(S["iter_ready"], NB + 1)
            count[0] = D["phase1"] + NB * 16
            D["xn2"] = layer_norm(xn, x2)
            for e in range(2):
                dve.wait_ge(S["tail"], TL[f"xn2{'ab'[e]}"])
                v.tensor_copy(xn2T[0:CH, 0:T, 2 * e:2 * e + 2].rearrange("p t b -> p b t"),
                              bank[e][0:CH, :].rearrange("p (b n) -> p b n", b=2)).then_inc(S["tail_done"], 1)
            for e in range(2):
                dve.wait_ge(S["tail"], TL[f"x2{'ab'[e]}"])
                v.tensor_copy(x2T[:, 2 * e:2 * e + 2, :],
                              bank[2 + e][0:CH, :].rearrange("p (b n) -> p b n", b=2)).then_inc(S["tail_done"], 1)

            dve.wait_ge(S["pool_c"], 15)
            v.memset(bank[7][0:CH, 0:12], 0.0).then_inc(S["h_ready"], 1)
            with dve.Fori(0, T // STEPS // 2) as kk:
                k = kk * 2
                for s in range(2 * STEPS):
                    prev, slot, t = (s - 1) % (2 * STEPS), s, k * STEPS
                    dve.wait_ge(S["h_ready"], t + s + 1)
                    cell = bank[7][0:CH, 2:12:3]
                    v.scalar_tensor_tensor(out=scan[:, 18:30:3], in0=hh[0:CH, prev, :], scalar=0.5, in1=cell,
                                           op0=ALU.mult, op1=ALU.mult).then_inc(S["hc_ready"], 1)
                    dve.wait_ge(S["hc_ready"], t + s + 1)
                    dve.wait_ge(S["t_gate"], t + s + 1)
                    v.tensor_tensor_scan(bank[7][0:CH, 0:12], scan[:, 0:12], scan[:, 16:28], 0.0, ALU.mult,
                                         ALU.add).then_inc(S["c_new"], 1)
                    dve.wait_ge(S["t_cell"], t + s + 1)
                    if s % STEPS == 0:
                        dve.wait_ge(S["hs_ready"], k + s // STEPS + 1)
                    v.scalar_tensor_tensor(out=hh[0:CH, slot, :], in0=scan[:, 30:42:3], scalar=1.0,
                                           in1=bank[6][0:CH, 0:4], op0=ALU.add, op1=ALU.mult).then_inc(S["h_ready"], 1)

        @block.scalar
        def _(act):
            a_ = nc.scalar

            def ot_copy(b, qb, g):
                n = qb * NGRP + g
                act.wait_ge(S["ot_ready"], b * 8 + n + 1)
                a_.activation(oT[:, g, :], bank[4 + g % 2][:, 0:128], ACT.Copy).then_inc(S["ot_done"], 1)

            for e in range(4):
                act.wait_ge(S["dve"], D[f"cmax{e}"])
                for i in range(2):
                    a = 2 * e + i
                    a_.activation(cp[:, a, :], bank[E_BANK[e]][:, 256 * i:256 * i + 256], ACT.Exp,
                                  bias=cmax[:, a:a + 1], accum_out=csum[:, a:a + 1]).then_inc(S["act"], 1)
            for e in range(2):
                act.wait_ge(S["pe"], PE[f"ptr{2 * e + 1}"])
                a_.activation(cpt[:, 4 * e + 2:4 * e + 4, :, :],
                              bank[P_BANK[2 * e + 1]][:, :].rearrange("p (a k n) -> p a k n", a=2, k=2),
                              ACT.Copy).then_inc(S["act"], 1)
            act.wait_ge(S["dve"], D["gsm"])
            a_.activation(gate[:, :, :], gsm[:, :, :], ACT.Exp, scale=1.0 / T).then_inc(S["act"], 1)
            with act.Fori(0, NB) as b:
                act.wait_ge(S["iter_ready"], b + 1)
                for n, dst in enumerate((V1[:, 0], V1[:, 1], VW[:, 0], VW[:, 1], VS[:, :, :])):
                    act.wait_ge(S["pja_ready"], b * 5 + n + 1)
                    a_.activation(dst[:, :, 0:VD], bank[4 + n % 2][:, :].rearrange("p (h v) -> p h v", v=VD),
                                  ACT.Copy).then_inc(S["pja_free"], 1)
                for qb in range(TB):
                    act.wait_ge(S["mtv_done"], b * 4 + 2 * qb + 2)
                    for e in range(2):
                        a_.activation(QT[64 + MAXROW:64 + MAXROW + 3, 4 * e:4 * e + 4, 1, 128 * qb:128 * qb + 128],
                                      bank[4 + e][64 + MAXROW:64 + MAXROW + 3, :].rearrange("p (g n) -> p g n", g=4),
                                      ACT.Copy).then_inc(S["mta_done"], 1)
                    cols = 128 * (3 + qb)
                    for h in range(NH):
                        n = qb * NH + h
                        act.wait_ge(S["st_ready"], b * 32 + n + 1)
                        if n >= 3:
                            act.wait_ge(S["pv_done"], b * 32 + n - 2)
                        a_.activation(et[:, n % 3, 0:cols], bank[n % 4][:, 0:cols], ACT.Exp,
                                      scale=SCALE).then_inc(S["ex_done"], 1)
                        if h == 0 and qb == 1:
                            act.wait_ge(S["ec_ready"], b + 1)
                            for f in range(2):
                                a_.activation(etc[96:128, f:NH:2, :], bank[4 + f][96:128, 0:32 * NP].rearrange(
                                    "p (h n) -> p h n", n=32), ACT.Exp, scale=SCALE).then_inc(S["ec_done"], 1)
                        if h >= 10 and h % 4 == 2:
                            ot_copy(b, qb, h // 4 - 2)
                    ot_copy(b, qb, NGRP - 2)
                    ot_copy(b, qb, NGRP - 1)
            with act.Fori(0, T // STEPS // 2) as kk:
                k = kk * 2
                for s in range(2 * STEPS):
                    t = k * STEPS
                    act.wait_ge(S["g_in"], t + s + 1)
                    src = bank[s // STEPS][0:CH, 12 * (s % STEPS):12 * (s % STEPS) + 12]
                    dst = scan[:, 2:44].rearrange("p (g x) -> p g x", g=3)[:, :, 0:12:3]
                    a_.activation(dst, src.rearrange("p (g b) -> p g b", g=3), ACT.Tanh).then_inc(S["t_gate"], 1)
                    act.wait_ge(S["c_new"], t + s + 1)
                    a_.activation(bank[6][0:CH, 0:4], bank[7][0:CH, 2:12:3], ACT.Tanh,
                                  scale=0.5).then_inc(S["t_cell"], 1)

        @block.tensor
        def _(pe):
            mm, tr = nc.tensor.matmul, nc.tensor.transpose

            def part(out, lhsT, rhs, start):
                return mm(out, lhsT, rhs, start=start, stop=True, skip_group_check=True)

            def done(name, ins):
                ins.then_inc(S["pe"], 1)
                order.append(name)
                assert len(order) == PE[name], name

            order = []
            pe.wait_ge(S["w_ready"], 16 * nw)
            pe.wait_ge(S["dve"], D["gsum"])
            done("gsum", mm(bank[0][:, 0:4], c["pair"][:, :], gsum[:, :], start=True, stop=True))
            pe.wait_ge(S["dve"], D["yc"])
            for i in range(2):
                n = mm(bank[i][0:CH, :], c["wqk"][:, i, :], yc[:, :, :].rearrange("p j n -> p (j n)"),
                       start=True, stop=True)
            done("qk", n)
            done("wvo", mm(bank[2][:, 0:CH], c["wv2"][:, :], c["wo9"][0:INNER, :], start=True, stop=True))
            pe.wait_ge(S["dve"], D["wvo"])
            for a in range(8):
                b, kb = a // 2, a % 2
                r = 64 * (b % 2)
                part(bank[3 + b % 2][:, CH * (a // 4 * 2 + kb):CH * (a // 4 * 2 + kb) + CH],
                     yc[r:r + 64, b // 2, 128 * kb:128 * kb + 128], wvo[r:r + 64, :], a % 4 == 0 and a < 4 or a == 2)
            mm(bank[6][:, 0:CH], c["bv9"][:, :], c["wo9"][:, :], start=True, stop=True)
            for a in range(4):
                n = tr(bank[5][:, 128 * a:128 * a + 128], xc[:, a // 2, 128 * (a % 2):128 * (a % 2) + 128], ident[:, :])
            done("vw", n)
            pe.wait_ge(S["dve"], D["xtok"])
            for b in range(NB):
                r, j = 32 * (b % 2), b // 2
                for i in range(TB):
                    n = part(bank[E_BANK[b]][:, 256 * i:256 * i + 256], qc[r:r + INNER, j, 128 * i:128 * i + 128],
                             kc[r:r + INNER, j, :], i == 0)
                done(f"energy{b}", n)
            for b in range(NB):
                pe.wait_ge(S["act"], 2 * b + 2)
                for i in range(4):
                    n = tr(bank[P_BANK[b]][:, 128 * i:128 * i + 128],
                           cp[:, 2 * b + i // 2, 128 * (i % 2):128 * (i % 2) + 128], ident[:, :])
                done(f"ptr{b}", n)
            pe.wait_ge(S["dve"], D["cpt2"])
            pe.wait_ge(S["act"], A_["cpt3"])
            for a in range(8):
                for kb in range(TB):
                    n = part(bank[2][:, CH * a:CH * a + CH], cpt[:, a, kb, :], vw[:, a // 2 * 2 + kb, :],
                             a == 0 and kb == 0)
            done("pv", n)

            def token_transposes(src, rows, banks, names, sem_done):
                for e in range(2):
                    for i in range(4):
                        n = tr(bank[banks[e]][0:rows, 128 * i:128 * i + 128], src[:, 4 * e + i, :], ident[:, :])
                    if sem_done is None:
                        done(names[e], n)
                    else:
                        n.then_inc(sem_done, 1)

            pe.wait_ge(S["dve"], D["xn"])
            token_transposes(xn, CH, (0, 1), ("xnT0", "xnT1"), None)
            pe.wait_ge(S["dve"], D["xnT"])
            for a in range(8):
                n = part(bank[2][:, NCAT * a:NCAT * a + NCAT], xnT[0:CH, a // 2, 128 * (a % 2):128 * (a % 2) + 128],
                         c["wcat"][:, :], a == 0)
            done("cat", n)
            pe.wait_ge(S["dve"], D["cqn"])
            token_transposes(cqn, RQ, (3, 4), ("cqT0", "cqT1"), None)
            token_transposes(ckn, RKV, (5, 6), ("ckT0", "ckT1"), None)
            for t in range(TB):
                n = mm(bank[7][:, 0:3 * NB], ones[:, :], cat[:, t:8:2, GATE:GATE + 3], start=t == 0, stop=t == 1)
            done("gate", n)
            pe.wait_ge(S["dve"], D["diag"])
            for a in range(8):
                n = part(bank[a // 4][:, 128 * (a % 4):128 * (a % 4) + 128], ones[:, :], diag[:, a, :], a % 4 == 0)
            done("srow", n)
            pe.wait_ge(S["dve"], D["sel"])
            part(bank[2][:, 0:NB], c["lt"][:, :], sel[:, :, 0], True)
            part(bank[2][:, NB:2 * NB], c["lt"][:, :], sel[:, :, 1], False)
            done("pos", part(bank[2][:, NB:2 * NB], ones[:, :], sel[:, :, 0], False))
            pe.wait_ge(S["dve"], D["psel"])
            for a in range(8):
                n = part(bank[3][0:CH, KEEP * (a // 2):KEEP * (a // 2) + KEEP], xn[:, a, :], diag[:, a, :], a == 0)
            done("selT", n)

            with pe.Fori(0, NB) as b:
                pe.wait_ge(S["staged"], b * 5 + 5)
                for n in range(ND):
                    o = bank[n % 4]
                    if n >= 4:
                        pe.wait_ge(S["pjd_free"], b * ND + n - 3)
                    if n < K1_FIRST and dve_units[n][2] == 1:
                        wa, wb, x = pe_units[n]
                        part(o[:, 0:T], wa, x, True)
                        last = part(o[:, T:2 * T], wb, x, False)
                    elif n < K1_FIRST:
                        wa, wb, x = pe_units[n]
                        for i in range(4):
                            last = part(o[:, KEEP * i:KEEP * i + KEEP], (wa, wb)[i // 2][:, i % 2, :], x, i == 0)
                    else:
                        p = 2 * (n - K1_FIRST)
                        for i in range(2):
                            last = part(o[:, T * i:T * i + T], c["wk1"][:, p + i, :], ck_b[:, :], i == 0)
                    last.then_inc(S["pjd_ready"], 1)
                    if n % 5 == 4:
                        m = n // 5
                        if m >= 2:
                            pe.wait_ge(S["pja_free"], b * 5 + m - 1)
                        x, w = ((ck_b[:, 0:128], c["wv1"]), (ck_b[:, 128:256], c["wv1"]), (xn_b[0:CH, 0:128], c["wwv"]),
                                (xn_b[0:CH, 128:256], c["wwv"]), (xs_b[0:CH, :], c["wsv"]))[m]
                        mm(bank[4 + m % 2][:, :], x, w[:, :], start=True, stop=True).then_inc(S["pja_ready"], 1)
                pe.wait_ge(S["rp_done"], b * NR + NR)
                pe.wait_ge(S["pjd_free"], b * ND + ND)
                pe.wait_ge(S["pja_free"], b * 5 + 5)
                for qb in range(TB):
                    q = slice(128 * qb, 128 * qb + 128)
                    for h in range(NH):
                        n, p, f = qb * NH + h, h // 2, h % 2
                        o = bank[n % 4]
                        if h >= 4:
                            pe.wait_ge(S["sm_free"], b * 32 + n - 3)
                        if n == 2 * NH - 1:
                            pe.wait_ge(S["x2_done"], b + 1)
                        nk = 128 * (qb + 1)
                        part(o[:, 0:nk], QT[:, p, f, q], K1[:, p, 0:nk], True)
                        part(o[:, nk:nk + 128], QT[:, p, f, q], KS[:, p, :], False)
                        part(o[:, nk + 128:nk + 256], QT[:, p, f, q], KW[:, p, q], False)
                        part(o[:, nk - 128:nk], ident16[:, :], masks16[:, 0, :], False)
                        part(o[:, nk + 128:nk + 256], ident16[:, :], masks16[:, 2, :], False).then_inc(S["sm_ready"], 1)
                    if qb == 1:
                        for h in range(NH):
                            p, f = h // 2, h % 2
                            o = bank[4 + h % 2][0:32, 32 * p:32 * p + 32]
                            part(o, QT[:, p, f, 128:160], KW[:, p, 96:128], p == 0)
                            last = part(o, ident16[0:32, 0:32], corner16[0:32, 0, :], False)
                        last.then_inc(S["cn_ready"], 1)
                    pe.wait_ge(S["mx_ready"], b * 2 + qb + 1)
                    for p in range(NP):
                        last = tr(bank[4 + p // 4][:, 128 * (p % 4):128 * (p % 4) + 128], mx[:, p, :], ident[:, :])
                    last.then_inc(S["mt_ready"], 1)
                    pe.wait_ge(S["mtv_done"], b * 4 + 2 * qb + 2)
                    pe.wait_ge(S["mta_done"], b * 4 + 2 * qb + 2)

                    def scores_t(h):
                        n, p, f = qb * NH + h, h // 2, h % 2
                        o = bank[n % 4]
                        if h >= 4:
                            pe.wait_ge(S["ex_done"], b * 32 + n - 3)
                        for kb in range(qb + 1):
                            part(o[:, 128 * kb:128 * kb + 128], K1[:, p, 128 * kb:128 * kb + 128], QT[:, p, f, q], kb == 0)
                        nk = 128 * (qb + 1)
                        part(o[:, nk:nk + 128], KS[:, p, :], QT[:, p, f, q], False)
                        part(o[:, nk + 128:nk + 256], KW[:, p, q], QT[:, p, f, q], False)
                        part(o[:, nk - 128:nk], ident16[:, :], masks16[:, 1, :], False)
                        part(o[:, nk + 128:nk + 256], ident16[:, :], masks16[:, 3, :], False).then_inc(S["st_ready"], 1)

                    def corner_t():
                        for h in range(NH):
                            p, f = h // 2, h % 2
                            o = bank[4 + h % 2][96:128, 32 * p:32 * p + 32]
                            part(o, KW[:, p, 96:128], QT[:, p, f, 128:160], p == 0)
                            last = part(o, ident16[96:128, 96:128], corner16[96:128, 1, :], False)
                        last.then_inc(S["ec_ready"], 1)

                    def values(h):
                        n, g = qb * NH + h, qb * NGRP + h // 4
                        pe.wait_ge(S["ex_done"], b * 32 + n + 1)
                        if qb == 1 and h == 0:
                            pe.wait_ge(S["ec_done"], b * 2 + 2)
                        if h % 4 == 0 and g >= 2:
                            pe.wait_ge(S["o_free"], b * 8 + g - 1)
                        o = [bank[6 + g % 2][:, (4 * j + h % 4) * (VD + 1):(4 * j + h % 4 + 1) * (VD + 1)] for j in range(3)]
                        e = [et[:, n % 3, 128 * i:128 * i + 128] for i in range(4)]
                        for kb in range(qb + 1):
                            part(o[0], e[kb], V1[:, kb, h, :], kb == 0)
                        part(o[1], e[qb + 1], VS[:, h, :], True)
                        last = part(o[2], e[qb + 2], VW[:, qb, h, :], True)
                        if qb == 1:
                            last = part(o[2][0:32, :], etc[96:128, h, :], VW[96:128, 0, h, :], False)
                        last.then_inc(S["pv_done"], 1)

                    def out_t(g):
                        n = qb * NGRP + g
                        pe.wait_ge(S["oc_ready"], b * 8 + n + 1)
                        if g >= 2:
                            pe.wait_ge(S["ot_done"], b * 8 + n - 1)
                        tr(bank[4 + g % 2][:, 0:128], osum[:, n % 2, 1, :], ident[:, :]).then_inc(S["ot_ready"], 1)

                    for h in range(NH + 2):
                        if h < NH:
                            scores_t(h)
                        if h == 0 and qb == 1:
                            corner_t()
                        if h >= 2:
                            values(h - 2)
                        if 8 <= h < NH and h % 4 == 0:
                            out_t(h // 4 - 2)
                    out_t(NGRP - 2)
                    out_t(NGRP - 1)
                    pe.wait_ge(S["ot_done"], b * 8 + 4 * qb + 4)
                    for g in range(NGRP):
                        last = mm(bank[4][:, 0:CH], oT[:, g, :], c["wproj"][:, g, :], start=g == 0, stop=g == NGRP - 1)
                    last.then_inc(S["y_ready"], 1)

            pe.wait_ge(S["dve"], D["xn2"])
            token_transposes(xn, CH, (0, 1), None, S["tail"])
            token_transposes(x2, CH, (2, 3), None, S["tail"])
            pe.wait_ge(S["tail_done"], 4)

            def gate_inputs(u, first):
                for g in range(3):
                    o = bank[u][0:CH, 0:12 * STEPS].rearrange("p (t g b) -> p t g b", g=3, b=NB)[:, :, g, :]
                    part(o, u_half[:, g, :], xn2T[:, bass.ds(first, STEPS), :], g == 0)

            gate_inputs(0, 0)
            with pe.Fori(0, T // STEPS // 2) as kk:
                k = kk * 2
                for s in range(2 * STEPS):
                    pe.wait_ge(S["h_ready"], k * STEPS + s + 1)
                    o = bank[s // STEPS][0:CH, 12 * (s % STEPS):12 * (s % STEPS) + 12]
                    for g in range(3):
                        last = part(o[:, 4 * g:4 * g + 4], v_half[:, g, :], hh[:, (s - 1) % (2 * STEPS), :], False)
                    last.then_inc(S["g_in"], 1)
                    if s % STEPS == 0:
                        u = s // STEPS
                        gate_inputs(1 - u, (k + u + 1) * STEPS)


def _host(inputs):
    import numpy as np
    i = {k: np.asarray(v) for k, v in inputs.items()}
    f = np.float32
    a = {"x": i["x"].reshape(NB, CH, T)}
    wqk = np.zeros((2, CH, 2, 2, 32), f)
    bqk = np.zeros((2, 32, 2), f)
    for n, (w, b) in enumerate((("wq", "bq"), ("wk", "bk"))):
        for h in range(2):
            wqk[h, :, n, h, :INNER] = i["L0_conv_" + w].T
            bqk[h, :INNER, n] = i["L0_conv_" + b]
    a["wqk"] = wqk.reshape(128, 2, 64)
    a["bqk"] = bqk.reshape(64, 2)
    a["wv2"] = np.concatenate([i["L0_conv_wv"]] * 2, 1)
    a["wo9"] = np.concatenate([i["L0_conv_wo"].T, i["L0_conv_bo"][None]], 0)
    a["bv9"] = np.concatenate([np.repeat(i["L0_conv_bv"][:, None], 128, 1), np.ones((1, 128), f)], 0)
    a["wcat"] = np.concatenate([i["L1_attn_" + n] for n in ("Wcq", "Wckv", "W_imp", "Wgate")], 1)
    a["qn"] = i["L1_attn_q_norm_w"][:, None]
    a["kvn"] = i["L1_attn_kv_norm_w"][:, None]

    def heads(rows, nope, rope, one):
        w = np.zeros((2, rows, NP, 2, 64), f)
        if nope is not None:
            w[0, :len(nope), :, :, 0:NOPE] = nope.reshape(-1, NP, 2, NOPE)
        if rope is not None:
            r = rope.reshape(-1, NP, 2, 2, ROPE // 2)
            w[0, :len(rope), :, :, ROPEROW:] = r.reshape(-1, NP, 2, ROPE)
            w[1, :len(rope), :, :, ROPEROW:] = r[:, :, :, ::-1].reshape(-1, NP, 2, ROPE)
        if one is not None:
            w[0, -1, :, :, MAXROW + one] = 1.0
        return w.reshape(2, rows, NP, 128)

    a["wqa"], a["wqb"] = heads(RQ, i["L1_attn_Wq_nope"], i["L1_attn_Wq_rope"], None)
    a["wk1"] = heads(RKV, i["L1_attn_Wk_nope"], None, None)[0]
    kr = heads(CH + 1, None, np.repeat(i["L1_attn_Wk_rope"][:, None], NH, 1), 0)
    a["wkr"] = np.ascontiguousarray(kr[:, :, 0, :].transpose(1, 0, 2))
    for n, src, one in (("ww", "Wwin_k", 2), ("ws", "Wsel_k", 1)):
        w = i["L1_attn_" + src].reshape(CH, NH, HD)
        a[n + "a"], a[n + "b"] = heads(CH + 1, w[..., :NOPE], w[..., NOPE:], one)
    a["wv1"], a["wwv"], a["wsv"] = (i["L1_attn_" + n] for n in ("Wv", "Wwin_v", "Wsel_v"))
    a["wproj"] = i["L1_attn_Wproj"].reshape(NGRP, 128, CH).transpose(1, 0, 2)
    a["u3"] = np.stack([np.concatenate([i["L1_ffn_U_" + g], i["L1_ffn_b_" + g][None]], 0) for g in "cio"], 1)
    a["v3"] = np.stack([np.concatenate([i["L1_ffn_V_" + g], np.zeros((128 - CH, CH), f)], 0) for g in "cio"], 1)

    p = np.arange(128)
    a["ident"], a["ones"] = np.eye(128, dtype=f), np.ones((128, 128), f)
    a["pair"] = np.where(p[:, None] // 2 == p[None] // 2, 0.5, 0.0).astype(f)
    a["lt"] = (p[:, None] < p[None]).astype(f)
    j = np.arange(T)
    a["tie"] = (j[None, None] < (128 * np.arange(TB)[None, :, None] + p[:, None, None])).astype(f)
    a["iota"] = np.broadcast_to(p.astype(f)[None], (128, 128))
    freq = 1.0 / 10000.0 ** (np.arange(0, ROPE, 2, dtype=np.float32) / ROPE)
    ang = np.outer(np.arange(T, dtype=np.float32), freq)
    cos, sin = np.ones((2, 64, T), f), np.zeros((2, 64, T), f)
    half = ROPE // 2
    for k in range(2):
        cos[:, ROPEROW + half * k:ROPEROW + half * k + half] = np.cos(ang).T
        sin[:, ROPEROW + half * k:ROPEROW + half * k + half] = (-1, 1)[k] * np.sin(ang).T
    a["cos"], a["sin"] = cos.reshape(128, T), sin.reshape(128, T)
    low = f(-1e30)
    d = p[:, None] - p[None]
    causal, window = np.where(d >= 0, f(0), low), np.where((d >= 0) & (d < WINDOW), f(0), low)
    a["masks"] = np.stack([causal, causal.T, window, window.T], 1)
    r = np.arange(32)
    corner = np.where(r[None] > r[:, None], f(0), low)
    a["corner"] = np.zeros((128, 2, 32), f)
    a["corner"][0:32, 0] = corner
    a["corner"][96:128, 1] = corner.T
    return {k: np.ascontiguousarray(v, dtype=v.dtype) for k, v in a.items()}


def kernel(**inputs):
    import concourse.bacc as _bacc
    from concourse.bass_utils import run_bass_kernel_spmd as _run

    arrays = _host(inputs)
    nc = _bacc.Bacc("TRN2", target_bir_lowering=False, num_devices=1)
    d = {k: nc.dram_tensor(k + "_dram", v.shape, mybir.dt.from_np(v.dtype), kind="ExternalInput").ap()
         for k, v in arrays.items()}
    out = nc.dram_tensor("out_dram", (NB, CH, T), F32, kind="ExternalOutput").ap()
    conv_attn_lstm(nc, d, out)
    r = _run(nc, [{k + "_dram": v for k, v in arrays.items()}], core_ids=[0])
    return r.results[0]["out_dram"].reshape(NB, CH, 16, 16)
```

```python
from contextlib import ExitStack

import concourse.bass as bass
from concourse import mybir

F32 = mybir.dt.float32
BF16 = mybir.dt.bfloat16
ALU = mybir.AluOpType
ACT = mybir.ActivationFunctionType
AX = mybir.AxisListType

NB, CH, T = 4, 64, 256
INNER = 8
NH, NOPE, ROPE, VD = 16, 32, 16, 32
HD = NOPE + ROPE
RQ, RKV = 24, 32
WINDOW, KEEP = 32, 128
NP = NH // 2
TB = T // 128
MAXROW, ROPEROW = 32, 48
NGRP = NH // 4
CQ, CKV, IMP, GATE = 0, RQ, RQ + RKV, RQ + RKV + 1
NCAT = GATE + 3
QROW, ONEROW, KROW = CH, CH + RQ, CH + 32
SCALE = float(HD) ** -0.5
PLACED = {"wqa": (QROW, KROW), "wqb": (QROW, KROW), "wk1": (KROW, 128), "wwa": (0, KROW), "wwb": (0, KROW),
          "wsa": (0, KROW), "wsb": (0, KROW), "wkr": (0, KROW), "wv1": (KROW, 128), "wwv": (0, CH), "wsv": (0, CH)}
FIRST = ("pair", "ident", "wqk", "bqk", "wv2", "wo9", "bv9")
AWAKE = 4
STEPS = 8


def conv_attn_lstm(nc, d, out):
    with ExitStack() as ctx:
        def sb(name, shape, dt=F32):
            return ctx.enter_context(nc.sbuf_tensor(name, shape, dt))

        def sem(name):
            return ctx.enter_context(nc.semaphore(name))

        c = {k: sb("w_" + k, [128 if k in PLACED else d[k].shape[0], *d[k].shape[1:]]) for k in d if k != "x"}
        ident, ones = c["ident"], c["ones"]
        ident16 = sb("ident16", [128, 128], BF16)
        masks16 = sb("masks16", [128, 4, 128], BF16)
        corner16 = sb("corner16", [128, 2, 32], BF16)
        krw = sb("krw", [128, 2, 128])
        u_half = sb("u_half", [CH + 1, 3, CH])
        v_half = sb("v_half", [128, 3, CH])

        xc = sb("xc", [128, 2, T])
        yc = sb("yc", [128, 2, T])
        qc, kc = sb("qc", [CH, 2, T]), sb("kc", [CH, 2, T])
        bnc = sb("bnc", [128, 2, 6])
        mvc = sb("mvc", [128, 2, 2])
        gsum = sb("gsum", [128, 4])
        grp = sb("grp", [128, 4])
        gtmp = sb("gtmp", [128, 2])
        grstd = sb("grstd", [128, 2])
        wvo = sb("wvo", [128, CH])
        cst = sb("cst", [128, CH])
        vw = sb("vw", [128, NB * TB, CH])
        cmax = sb("cmax", [128, NB * TB])
        csum = sb("csum", [128, NB * TB])
        crec = sb("crec", [128, NB * TB])
        cp = sb("cp", [128, NB * TB, T])
        cpt = sb("cpt", [128, NB * TB, TB, 128])
        x1 = sb("x1", [128, NB * TB, CH])
        x2 = sb("x2", [128, NB * TB, CH])
        tmp = sb("tmp", [128, NB * TB, CH])
        tok = sb("tok", [128, NB * TB, 128])
        xn = tok[:, :, 0:CH]
        bn = sb("bn", [128, NB * TB, 6])
        mv = sb("mv", [128, NB * TB, 2])
        rstd = sb("rstd", [128, NB * TB])
        tokT = sb("tokT", [128, NB + 1, T])
        cat = sb("cat", [128, NB * TB, NCAT])
        sq = sb("sq", [128, NB * TB, RQ + RKV])
        ssq, rms = sb("ssq", [128, 2, NB * TB]), sb("rms", [128, 2, NB * TB])
        vare = sb("vare", [128, NB * TB])
        rtmp, rint = sb("rtmp", [128, 16]), sb("rint", [128, 16], mybir.dt.int32)
        gsm = sb("gsm", [128, NB, 3])
        gm1 = sb("gm1", [128, NB])
        gate = sb("gate", [128, NB, 3])
        diag = sb("diag", [128, NB * TB, 128])
        eqs = cpt[:, :, :, :].rearrange("p a k n -> p a (k n)")
        rank = sb("rank", [128, NB * TB])
        sel = sb("sel", [128, NB, TB])
        pos = sb("pos", [128, TB, NB])
        xsT = sb("xsT", [128, NB + 1, KEEP])

        tok_b, xs_b = sb("tok_b", [128, T]), sb("xs_b", [128, KEEP])
        QT = sb("QT", [128, NP, 2, T])
        K1, KW = (sb(n, [128, NP, T]) for n in ("K1", "KW"))
        KS = sb("KS", [128, NP, KEEP])
        krp = sb("krp", [128, T])
        V1, VW = (sb(n, [128, TB, NH, VD + 1]) for n in ("V1", "VW"))
        VS = sb("VS", [128, NH, VD + 1])
        ra, rb = sb("ra", [128, 3, T]), sb("rb", [128, 3, T])
        nm = sb("nm", [128, TB, NH, 4])
        cm = sb("cm", [32, NH])
        mx = sb("mx", [128, TB, NP, 128])
        et = sb("et", [128, 3, 512])
        etc = sb("etc", [128, NH, 32])
        orec, ow = sb("orec", [128, 2, 12]), sb("ow", [128, 2, 12])
        oprod = sb("oprod", [128, 2, 12, VD])
        osum = sb("osum", [128, 2, 2, 128])
        oT = sb("oT", [128, NGRP, 128])

        xn2T = sb("xn2T", [CH + 1, T + STEPS, NB])
        x2T = sb("x2T", [CH, NB, T])
        y = cp[0:CH, 0:NB, :]
        hh = sb("hh", [128, 2 * STEPS, NB])
        hs = sb("hs", [CH, 2, STEPS, NB])
        half = sb("half", [CH, STEPS, NB])
        scan = sb("scan", [CH, 56])
        bank = [ctx.enter_context(nc.psum_tensor(f"bank{i}", [128, 512], F32)) for i in range(8)]

        names = """w_first w_ready x_ready dve act pe pool pool_c staged pjd_ready pjd_free pja_ready pja_free
            rp_ready rp_done sm_ready sm_free cn_ready cn_free mx_ready mt_ready mtv_done mta_done
            x2_done q_low hs_ready st_ready ex_done ec_ready ec_done pv_done o_ready o_free oc_ready ot_ready ot_done y_ready
            xs_ready h_ready g_in t_gate c_new t_cell hc_ready y_done out_done tail tail_done""".split()
        S = {n: sem(n) for n in names}
        block = ctx.enter_context(nc.Block())
        later = [k for k in c if k not in FIRST]
        nf, nw = len(FIRST), len(later)
        D = {}
        A_ = {"exp": 0, "cpt1": 9, "cpt3": 10, "gate": 11}
        E_BANK, P_BANK = (6, 7, 0, 1), (2, 3, 4, 5)
        units = [(krp[:, :], "rope", 1, krw[:, 0, :], krw[:, 1, :], tok_b[:, :])]
        for p in range(0, NP, 2):
            for i in (p, p + 1):
                units.append((QT[:, i, :, :], "query", 1, c["wqa"][:, i, :], c["wqb"][:, i, :], tok_b[:, :]))
            for i in (p, p + 1):
                units.append((KW[:, i, :], "rope", 1, c["wwa"][:, i, :], c["wwb"][:, i, :], tok_b[:, :]))
            units.append((KS[:, p:p + 2, :], "rope", 2, c["wsa"][:, p:p + 2, :], c["wsb"][:, p:p + 2, :], xs_b[:, :]))
            units.append((K1[:, p:p + 2, :], "plain", 2, c["wk1"][:, p, :], c["wk1"][:, p + 1, :], tok_b[:, :]))
        ND, NR = len(units), sum(u[1] != "plain" for u in units)
        UG, RG = (ND - 1) // NGRP, (NR - 1) // NGRP
        P_RING = 4 - ND % 4
        NU = TB * NH
        NO = TB * NGRP
        MT = (23, 4)
        OT_LAG = 9
        CORNER = 15
        Y_LAG = NH + 7

        @block.sync
        def _(sp):
            xv = d["x"].rearrange("(j h) c n -> h c j n", h=2)
            for h in range(2):
                sp.dma_start(xc[64 * h:64 * h + 64, :, :], xv[h]).then_inc(S["x_ready"], 16)
            for k in FIRST:
                sp.dma_start(c[k][...], d[k][...]).then_inc(S["w_first"], 16)
            sp.wait_ge(S["y_done"], T // STEPS)
            sp.dma_start(out.rearrange("b c n -> c b n"), y[:, :, :]).then_inc(S["out_done"], 16)
            sp.wait_ge(S["out_done"], 16)


        PE = {n: i + 1 for i, n in enumerate(
            "gsum qk wvo vw energy0 energy1 energy2 energy3 ptr0 ptr1 ptr2 ptr3 pv xnT0 xnT1 cat tokT0 tokT1 "
            "gate srow pos selT".split())}
        TL = {n: i + 1 for i, n in enumerate("xn2a xn2b x2a x2b".split())}

        @block.gpsimd
        def _(pool):
            made = [0]

            def const(ins):
                made[0] += 1
                ins.then_inc(S["pool_c"], 1)
                pool.wait_ge(S["pool_c"], made[0])

            for k, (r0, r1) in PLACED.items():
                t = krw if k == "wkr" else c[k]
                if r0 > 0:
                    const(nc.gpsimd.memset(t[0:r0], 0.0))
                if r1 < 128:
                    const(nc.gpsimd.memset(t[r1:128], 0.0))
            const(nc.gpsimd.memset(tok[:, :, ONEROW:KROW], 1.0))
            const(nc.gpsimd.memset(xsT[CH:128, :, :], 1.0))
            const(nc.gpsimd.memset(xn2T[CH:CH + 1, :, :], 1.0))
            const(nc.gpsimd.memset(mx[:, :, :, :], 0.0))
            const(nc.gpsimd.memset(QT[64:128, :, 0, :], 0.0))
            const(nc.gpsimd.memset(QT[0:64, :, 1, :], 0.0))
            const(nc.gpsimd.memset(V1[:, :, :, VD:VD + 1], 1.0))
            const(nc.gpsimd.memset(VW[:, :, :, VD:VD + 1], 1.0))
            const(nc.gpsimd.memset(VS[:, :, VD:VD + 1], 1.0))
            const(nc.gpsimd.memset(hh[:, :, :], 0.0))
            const(nc.gpsimd.memset(scan[:, :], 0.0))
            const(nc.gpsimd.memset(xn2T[0:CH, T:T + STEPS, :], 0.0))
            const(nc.gpsimd.memset(half[:, :, :], 0.5))
            nc.gpsimd.memset(hs[:, 0, :, :], 0.0).then_inc(S["hs_ready"], 1)
            nc.gpsimd.memset(hs[:, 1, :, :], 0.0).then_inc(S["hs_ready"], 1)
            const(nc.gpsimd.memset(scan[:, 1:13:3], 1.0))
            const(nc.gpsimd.memset(scan[:, 17:29:3], 1.0))

            const(nc.gpsimd.memset(tokT[:, NB, :], 0.0))
            const(nc.gpsimd.memset(xsT[0:CH, NB, :], 0.0))

            D["const"] = made[0]

            def stage(b):
                nc.gpsimd.tensor_copy(tok_b[:, :], tokT[:, b, :]).then_inc(S["staged"], 1)
                nc.gpsimd.tensor_copy(xs_b[:, :], xsT[:, b, :]).then_inc(S["staged"], 1)

            pool.wait_ge(S["xs_ready"], 1)
            stage(0)
            with pool.Fori(0, NB) as b:
                u = q = 0
                for n, (dst, kind, pairs, *_) in enumerate(units):
                    if kind == "plain":
                        continue
                    pool.wait_ge(S["pjd_free"], b * ND + n + 1)
                    src = [t[:, u % 3, 0:T] for t in (ra, rb)]
                    u += 1
                    if pairs == 2:
                        src = [t.rearrange("p (g n) -> p g n", g=2) for t in src]
                    if kind == "query":
                        q += 1
                        nc.gpsimd.tensor_tensor(dst[0:64, 0, :], src[0][0:64], src[1][0:64],
                                                ALU.add).then_inc(S["q_low"], 1)
                        pool.wait_ge(S["q_low"], b * NP + q)
                        nc.gpsimd.tensor_tensor(dst[64:128, 1, :], src[0][64:128], src[1][64:128],
                                                ALU.add).then_inc(S["rp_done"], 1)
                        pool.wait_ge(S["rp_done"], b * NR + u)
                    else:
                        nc.gpsimd.tensor_tensor(dst, src[0], src[1], ALU.add).then_inc(S["rp_done"], 1)
                pool.wait_ge(S["pja_ready"], b * 5 + 5)
                pool.wait_ge(S["pjd_ready"], b * ND + ND)
                stage(b + 1)
                for n in range(NO):
                    pool.wait_ge(S["o_free"], b * NO + n + 1)
                    if n >= 2:
                        pool.wait_ge(S["ot_ready"], b * NO + n - 1)
                    part = [oprod[:, n % 2, 4 * j:4 * j + 4, :].rearrange("p h v -> p (h v)") for j in range(3)]
                    nc.gpsimd.tensor_tensor(osum[:, n % 2, 0, :], part[0], part[1], ALU.add).then_inc(S["pool"], 1)
                    pool.wait_ge(S["pool"], b * NO + n + 1)
                    nc.gpsimd.tensor_tensor(osum[:, n % 2, 1, :], osum[:, n % 2, 0, :], part[2],
                                            ALU.add).then_inc(S["oc_ready"], 1)

            pool.wait_ge(S["tail_done"], 4)
            with pool.Fori(0, T // STEPS // 2) as kk:
                k = kk * 2
                for u in range(2):
                    pool.wait_ge(S["h_ready"], (k + u + 1) * STEPS + 1)
                    nc.gpsimd.tensor_tensor(hs[:, u, :, :], hh[0:CH, u * STEPS:(u + 1) * STEPS, :],
                                            half[:, :, :], ALU.mult).then_inc(S["hs_ready"], 1)
                    pool.wait_ge(S["hs_ready"], k + u + 3)
                    cols = bass.ds((k + u) * STEPS, STEPS)
                    nc.gpsimd.tensor_tensor(y[:, :, cols], x2T[:, :, cols],
                                            hs[:, u, :, :].rearrange("p t b -> p b t"),
                                            ALU.add).then_inc(S["y_done"], 1)

        @block.vector
        def _(dve):
            count = [0]

            def inc(ins):
                ins.then_inc(S["dve"], 1)
                count[0] += 1
                return count[0]

            def after(value):
                dve.wait_ge(S["dve"], value)

            def link(ins):
                after(inc(ins))

            v = nc.vector

            def rsqrt(y, x, n):
                i, t = rint[:, 0:n], rtmp[:, 0:n]
                link(v.tensor_scalar(i, x.bitcast(mybir.dt.int32), 1, None, ALU.logical_shift_right))
                link(v.tensor_scalar(y.bitcast(mybir.dt.int32), i, -1.0, float(0x5F3759DF), ALU.mult, ALU.add))
                for _ in range(3):
                    link(v.scalar_tensor_tensor(out=t, in0=y, scalar=-0.5, in1=y, op0=ALU.mult, op1=ALU.mult))
                    link(v.tensor_tensor(t, t, x, ALU.mult))
                    link(v.scalar_tensor_tensor(out=y, in0=t, scalar=1.5, in1=y, op0=ALU.add, op1=ALU.mult))

            dve.wait_ge(S["x_ready"], 32)
            for j in range(2):
                n = inc(v.bn_stats(bnc[:, j, :], xc[:, j, :]))
            after(n)
            for j in range(2):
                n = inc(v.bn_aggr(mvc[:, j, :], bnc[:, j, :]))
            after(n)
            inc(v.tensor_copy(gsum[:, 0:2], mvc[:, :, 0]))
            link(v.tensor_tensor(gtmp[:, :], mvc[:, :, 0], mvc[:, :, 0], ALU.mult))
            D["gsum"] = inc(v.tensor_tensor(gsum[:, 2:4], mvc[:, :, 1], gtmp[:, :], ALU.add))
            dve.wait_ge(S["w_first"], 16 * nf)
            inc(v.tensor_copy(ident16[:, :], ident[:, :]))
            dve.wait_ge(S["pe"], PE["gsum"])
            link(v.tensor_copy(grp[:, :], bank[0][:, 0:4]))
            link(v.tensor_tensor(gtmp[:, :], grp[:, 0:2], grp[:, 0:2], ALU.mult))
            link(v.tensor_tensor(gtmp[:, :], grp[:, 2:4], gtmp[:, :], ALU.subtract))
            link(v.tensor_scalar(gtmp[:, :], gtmp[:, :], 1e-5, None, ALU.add))
            rsqrt(grstd[:, :], gtmp[:, :], 2)
            for j in range(2):
                D["yc"] = inc(v.tensor_scalar(yc[:, j, :], xc[:, j, :], grp[:, j:j + 1], grstd[:, j:j + 1],
                                              ALU.subtract, ALU.mult))
            dve.wait_ge(S["pe"], PE["wvo"])
            D["wvo"] = inc(v.tensor_copy(wvo[:, :], bank[2][:, 0:CH]))
            dve.wait_ge(S["pe"], PE["qk"])
            inc(v.tensor_scalar(qc[:, :, :], bank[0][0:CH, :].rearrange("p (j n) -> p j n", j=2), c["bqk"][:, 0:1],
                                None, ALU.add))
            D["qk"] = inc(v.tensor_scalar(kc[:, :, :], bank[1][0:CH, :].rearrange("p (j n) -> p j n", j=2),
                                          c["bqk"][:, 1:2], None, ALU.add))
            dve.wait_ge(S["pe"], PE["vw"])
            for h in range(2):
                inc(v.tensor_copy(vw[:, :, :].rearrange("p (j h k) n -> p j h k n", j=2, h=2)[:, :, h],
                                  bank[3 + h][:, 0:4 * CH].rearrange("p (j k n) -> p j k n", j=2, n=CH)))
            link(v.tensor_copy(cst[:, :], bank[6][:, 0:CH]))
            for j in range(2):
                for t in range(TB):
                    src = bank[5][:, 256 * j + 128 * t:256 * j + 128 * t + 128].rearrange("p (h c) -> p h c", h=2)
                    D["xtok"] = inc(v.tensor_tensor(
                        x1[:, 4 * j + t:4 * j + t + 3:2, :], src,
                        cst[:, :].unsqueeze(1).broadcast_to([128, 2, CH]), ALU.add))
            for e in range(4):
                dve.wait_ge(S["pe"], PE[f"energy{e}"])
                src = bank[E_BANK[e]][:, :].rearrange("p (a n) -> p a n", a=2)
                D[f"cmax{e}"] = inc(v.tensor_reduce(cmax[:, 2 * e:2 * e + 2], src, AX.X, ALU.max, negate=True))
            for e in range(2):
                dve.wait_ge(S["pe"], PE[f"ptr{2 * e}"])
                D[f"cpt{2 * e}"] = inc(v.tensor_copy(
                    cpt[:, 4 * e:4 * e + 2, :, :],
                    bank[P_BANK[2 * e]][:, :].rearrange("p (a k n) -> p a k n", a=2, k=2)))
            dve.wait_ge(S["w_ready"], 16 * nw)
            inc(v.tensor_copy(masks16[:, :, :], c["masks"][:, :, :]))
            inc(v.tensor_copy(corner16[:, :, :], c["corner"][:, :, :]))
            inc(v.tensor_scalar(u_half[:, 1:3, :], c["u3"][:, 1:3, :], 0.5, None, ALU.mult))
            inc(v.tensor_copy(u_half[:, 0, :], c["u3"][:, 0, :]))
            inc(v.tensor_scalar(v_half[:, 1:3, :], c["v3"][:, 1:3, :], 0.25, None, ALU.mult))
            inc(v.tensor_scalar(v_half[:, 0, :], c["v3"][:, 0, :], 0.5, None, ALU.mult))
            inc(v.tensor_copy(krw[CH:KROW, :, :], c["wkr"][CH:KROW, :, :]))
            inc(v.tensor_scalar(krw[0:CH, :, :], c["wkr"][0:CH, :, :], 1.0 / NH, None, ALU.mult))
            dve.wait_ge(S["act"], A_["exp"] + 4 * 2)
            link(v.reciprocal(crec[:, :], csum[:, :]))
            dve.wait_ge(S["pe"], PE["pv"])
            link(v.tensor_tensor(tmp[:, :, :], bank[2][:, :].rearrange("p (a n) -> p a n", n=CH),
                                 crec[:, :].unsqueeze(2).broadcast_to([128, NB * TB, CH]), ALU.mult))
            link(v.tensor_tensor(x1[:, :, :], x1[:, :, :], tmp[:, :, :], ALU.add))

            def layer_norm(dst, src):
                for a in range(NB * TB):
                    n = inc(v.bn_stats(bn[:, a, :], src[:, a, :]))
                after(n)
                for a in range(NB * TB):
                    n = inc(v.bn_aggr(mv[:, a, :], bn[:, a, :]))
                after(n)
                link(v.tensor_scalar(vare[:, :], mv[:, :, 1], 1e-5, None, ALU.add))
                rsqrt(rstd[:, :], vare[:, :], NB * TB)
                for a in range(NB * TB):
                    n = inc(v.tensor_scalar(dst[:, a, :], src[:, a, :], mv[:, a, 0:1], rstd[:, a:a + 1],
                                            ALU.subtract, ALU.mult))
                return n

            D["xn"] = layer_norm(xn, x1)
            for e in range(2):
                dve.wait_ge(S["pe"], PE[f"xnT{e}"])
                D["xnT"] = inc(v.tensor_copy(tokT[0:CH, 2 * e:2 * e + 2, :],
                                             bank[e][0:CH, :].rearrange("p (a n) -> p a n", a=2)))
            dve.wait_ge(S["pe"], PE["cat"])
            link(v.tensor_copy(cat[:, :, :], bank[2][:, 0:8 * NCAT].rearrange("p (a n) -> p a n", n=NCAT)))
            D["cat"] = count[0]
            link(v.tensor_tensor(sq[:, :, :], cat[:, :, 0:IMP], cat[:, :, 0:IMP], ALU.mult))
            inc(v.tensor_reduce(ssq[:, 0, :], sq[:, :, 0:RQ], AX.X, ALU.add))
            link(v.tensor_reduce(ssq[:, 1, :], sq[:, :, RQ:IMP], AX.X, ALU.add))
            inc(v.tensor_scalar(ssq[:, 0, :], ssq[:, 0, :], 1.0 / RQ, 1e-6, ALU.mult, ALU.add))
            link(v.tensor_scalar(ssq[:, 1, :], ssq[:, 1, :], 1.0 / RKV, 1e-6, ALU.mult, ALU.add))
            rsqrt(rms[:, :, :].rearrange("p k a -> p (k a)"), ssq[:, :, :].rearrange("p k a -> p (k a)"), 16)
            inc(v.tensor_tensor(tok[:, :, QROW:ONEROW], cat[:, :, CQ:CKV],
                                rms[:, 0, :].unsqueeze(2).broadcast_to([128, 8, RQ]), ALU.mult))
            D["cqn"] = inc(v.tensor_tensor(tok[:, :, KROW:128], cat[:, :, CKV:IMP],
                                           rms[:, 1, :].unsqueeze(2).broadcast_to([128, 8, RKV]), ALU.mult))
            for a in range(8):
                D["diag"] = inc(v.tensor_scalar(diag[:, a, :], ident[:, :], cat[:, a, IMP:IMP + 1], None, ALU.mult))
            for e in range(2):
                dve.wait_ge(S["pe"], PE[f"tokT{e}"])
                inc(v.tensor_scalar(tokT[CH:128, 2 * e:2 * e + 2, :],
                                    bank[3 + e][CH:128, :].rearrange("p (a n) -> p a n", a=2),
                                    c["qkn"][CH:128, 0:1], None, ALU.mult))
            dve.wait_ge(S["pe"], PE["gate"])
            link(v.tensor_copy(gsm[:, :, :], bank[7][:, 0:3 * NB].rearrange("p (b g) -> p b g", g=3)))
            link(v.tensor_reduce(gm1[:, :], gsm[:, :, :], AX.X, ALU.max))
            D["gsm"] = inc(v.tensor_tensor(gsm[:, :, :], gsm[:, :, :],
                                           gm1[:, :].unsqueeze(2).broadcast_to([128, NB, 3]), ALU.subtract))
            dve.wait_ge(S["pe"], PE["srow"])
            def row(a):
                return bank[a // 4][:, 256 * ((a // 2) % 2):256 * ((a // 2) % 2) + 256]

            for a in range(8):
                n = inc(v.scalar_tensor_tensor(out=eqs[:, a, :], in0=row(a), scalar=cat[:, a, IMP:IMP + 1],
                                               in1=c["tie"][:, a % 2, :], op0=ALU.is_equal, op1=ALU.mult))
            after(n)
            for a in range(8):
                n = inc(v.scalar_tensor_tensor(out=eqs[:, a, :], in0=row(a), scalar=cat[:, a, IMP:IMP + 1],
                                               in1=eqs[:, a, :], op0=ALU.is_gt, op1=ALU.add,
                                               accum_out=rank[:, a:a + 1]))
            after(n)
            D["sel"] = inc(v.tensor_scalar(sel[:, :, :], rank[:, :].rearrange("p (b t) -> p b t", t=TB), KEEP - 0.5,
                                           None, ALU.is_lt))
            after(D["sel"])
            dve.wait_ge(S["act"], A_["gate"])
            link(v.tensor_reduce(gm1[:, :], gate[:, :, :], AX.X, ALU.add))
            link(v.reciprocal(gm1[:, :], gm1[:, :]))
            link(v.tensor_tensor(gate[:, :, :], gate[:, :, :], gm1[:, :].unsqueeze(2).broadcast_to([128, NB, 3]),
                                 ALU.mult))
            dve.wait_ge(S["pe"], PE["pos"])
            link(v.tensor_copy(pos[:, :, :], bank[2][:, 0:8].rearrange("p (t b) -> p t b", t=TB)))
            for a in range(8):
                D["psel"] = inc(v.tensor_scalar(diag[:, a, :], c["iota"][:, :], pos[:, a % 2, a // 2:a // 2 + 1],
                                                sel[:, a // 2, a % 2:a % 2 + 1], ALU.is_equal, ALU.mult))
            dve.wait_ge(S["pe"], PE["selT"])
            dve.wait_ge(S["pool_c"], D["const"])
            v.tensor_copy(xsT[0:CH, 0:NB, :], bank[3][0:CH, :].rearrange("p (b n) -> p b n", b=NB)
                          ).then_inc(S["xs_ready"], 1)
            D["phase1"] = count[0]

            v.memset(bank[4][:, 0:1], 0.0).then_inc(S["x2_done"], 1)
            with dve.Fori(0, NB) as b:
                u = 0
                for n, (dst, kind, pairs, *_) in enumerate(units):
                    src = bank[(n + P_RING) % 4]
                    dve.wait_ge(S["pjd_ready"], b * ND + n + 1)
                    if kind != "plain":
                        if u >= 3:
                            dve.wait_ge(S["rp_done"], b * NR + u - 2)
                        C, R = c["cos"][:, :], c["sin"][:, :]
                        A, B = src[:, 0:T], src[:, T:2 * T]
                        a_, b_ = ra[:, u % 3, :], rb[:, u % 3, :]
                        if pairs == 2:
                            A, B, a_, b_ = (t.rearrange("p (g n) -> p g n", g=2) for t in (A, B, a_, b_))
                            C, R = (t[:, 0:KEEP].unsqueeze(1).broadcast_to([128, 2, KEEP]) for t in (C, R))
                        v.tensor_tensor(a_, A, C, ALU.mult)
                        v.tensor_tensor(b_, B, R, ALU.mult).then_inc(S["pjd_free"], 1)
                        u += 1
                    else:
                        if n == UG:
                            dve.wait_ge(S["rp_done"], b * NR + 1)
                        v.tensor_tensor(dst, src[:, :].rearrange("p (g n) -> p g n", g=2),
                                        krp[:, :].unsqueeze(1).broadcast_to([128, 2, T]),
                                        ALU.add).then_inc(S["pjd_free"], 1)

                def minus_max(qb, first):
                    v.tensor_scalar(mx[:, qb, :, :].rearrange("p g (f r) -> p (g f) r", f=2)[:, :, MAXROW:MAXROW + 3],
                                    nm[:, qb, :, first:first + 3], -1.0, None, ALU.mult).then_inc(S["mx_ready"], 1)

                def max_rows(qb):
                    dve.wait_ge(S["mt_ready"], b * 2 + qb + 1)
                    for e in range(2):
                        v.tensor_copy(QT[MAXROW:MAXROW + 3, 4 * e:4 * e + 4, 0, 128 * qb:128 * qb + 128],
                                      bank[4 + e][MAXROW:MAXROW + 3, :].rearrange("p (g n) -> p g n", g=4)
                                      ).then_inc(S["mtv_done"], 1)

                for n in range(NU):
                    qb, h = n // NH, n % NH
                    nseg = 3 + qb
                    dve.wait_ge(S["sm_ready"], b * NU + n + 1)
                    v.tensor_reduce(nm[:, qb, h, 0:nseg], bank[n % 4][:, 0:128 * nseg].rearrange(
                        "p (s n) -> p s n", s=nseg), AX.X, ALU.max).then_inc(S["sm_free"], 1)
                    if n == NH - 1:
                        dve.wait_ge(S["sm_free"], b * NU + NH)
                        minus_max(0, 0)
                        dve.wait_ge(S["cn_ready"], b + 1)
                        for f in range(2):
                            v.tensor_reduce(cm[:, f:NH:2], bank[4 + f][0:32, 0:32 * NP].rearrange(
                                "p (h n) -> p h n", n=32), AX.X, ALU.max).then_inc(S["cn_free"], 1)
                    if n == MT[0] + 1:
                        max_rows(0)
                dve.wait_ge(S["sm_free"], b * NU + NU)
                v.tensor_tensor(nm[:, 1, :, 1], nm[:, 1, :, 0], nm[:, 1, :, 1], ALU.max).then_inc(S["cn_free"], 1)
                v.tensor_tensor(nm[0:32, 1, :, 3], nm[0:32, 1, :, 3], cm[:, :], ALU.max).then_inc(S["cn_free"], 1)
                dve.wait_ge(S["cn_free"], b * 4 + 4)
                minus_max(1, 1)
                max_rows(1)
                for n in range(NO):
                    dve.wait_ge(S["pv_done"], b * NU + 4 * n + 4)
                    O = bank[6 + n % 2][:, 0:12 * (VD + 1)].rearrange("p (a n) -> p a n", n=VD + 1)
                    v.reciprocal(orec[:, n % 2, :], O[:, :, VD]).then_inc(S["dve"], 1)
                    dve.wait_ge(S["dve"], D["phase1"] + b * 2 * NO + 2 * n + 1)
                    v.tensor_tensor(ow[:, n % 2, :].rearrange("p (j h) -> p j h", j=3),
                                    orec[:, n % 2, :].rearrange("p (j h) -> p j h", j=3),
                                    gate[:, b, :].unsqueeze(2).broadcast_to([128, 3, 4]),
                                    ALU.mult).then_inc(S["dve"], 1)
                    dve.wait_ge(S["dve"], D["phase1"] + b * 2 * NO + 2 * n + 2)
                    if n >= 2:
                        dve.wait_ge(S["oc_ready"], b * NO + n - 1)
                    v.tensor_tensor(oprod[:, n % 2, :, :], O[:, :, 0:VD],
                                    ow[:, n % 2, :].unsqueeze(2).broadcast_to([128, 12, VD]),
                                    ALU.mult).then_inc(S["o_free"], 1)
                    if n in (NGRP, NO - 1):
                        qb = n // (NO - 1)
                        dve.wait_ge(S["y_ready"], b * 2 + qb + 1)
                        v.tensor_tensor(x2[:, 2 * b + qb, :], x1[:, 2 * b + qb, :], bank[4][:, 0:CH],
                                        ALU.add).then_inc(S["x2_done"], 1)

            dve.wait_ge(S["x2_done"], 2 * NB + 1)
            count[0] = D["phase1"] + NB * 2 * NO
            D["xn2"] = layer_norm(xn, x2)
            for e in range(2):
                dve.wait_ge(S["tail"], TL[f"xn2{'ab'[e]}"])
                v.tensor_copy(xn2T[0:CH, 0:T, 2 * e:2 * e + 2].rearrange("p t b -> p b t"),
                              bank[e][0:CH, :].rearrange("p (b n) -> p b n", b=2)).then_inc(S["tail_done"], 1)
            for e in range(2):
                dve.wait_ge(S["tail"], TL[f"x2{'ab'[e]}"])
                v.tensor_copy(x2T[:, 2 * e:2 * e + 2, :],
                              bank[2 + e][0:CH, :].rearrange("p (b n) -> p b n", b=2)).then_inc(S["tail_done"], 1)

            dve.wait_ge(S["pool_c"], D["const"])
            v.memset(bank[7][0:CH, 0:12], 0.0).then_inc(S["h_ready"], 1)
            with dve.Fori(0, T // STEPS // 2) as kk:
                k = kk * 2
                for s in range(2 * STEPS):
                    prev, slot, t = (s - 1) % (2 * STEPS), s, k * STEPS
                    dve.wait_ge(S["h_ready"], t + s + 1)
                    cell = bank[7][0:CH, 2:12:3]
                    v.scalar_tensor_tensor(out=scan[:, 18:30:3], in0=hh[0:CH, prev, :], scalar=0.5, in1=cell,
                                           op0=ALU.mult, op1=ALU.mult).then_inc(S["hc_ready"], 1)
                    dve.wait_ge(S["hc_ready"], t + s + 1)
                    dve.wait_ge(S["t_gate"], t + s + 1)
                    v.tensor_tensor_scan(bank[7][0:CH, 0:12], scan[:, 0:12], scan[:, 16:28], 0.0, ALU.mult,
                                         ALU.add).then_inc(S["c_new"], 1)
                    dve.wait_ge(S["t_cell"], t + s + 1)
                    if s % STEPS == 0:
                        dve.wait_ge(S["hs_ready"], k + s // STEPS + 1)
                    v.scalar_tensor_tensor(out=hh[0:CH, slot, :], in0=scan[:, 30:42:3], scalar=1.0,
                                           in1=bank[6][0:CH, 0:4], op0=ALU.add, op1=ALU.mult).then_inc(S["h_ready"], 1)

        @block.scalar
        def _(act):
            a_ = nc.scalar
            for k in later:
                r0, r1 = PLACED.get(k, (0, d[k].shape[0]))
                act.dma_start(c[k][r0:r1], d[k][...]).then_inc(S["w_ready"], 16)

            def ot_copy(b, n):
                act.wait_ge(S["ot_ready"], b * NO + n + 1)
                a_.activation(oT[:, n % NGRP, :], bank[4 + n % 2][:, 0:128], ACT.Copy).then_inc(S["ot_done"], 1)

            def max_rows(b, qb):
                act.wait_ge(S["mtv_done"], b * 4 + 2 * qb + 2)
                for e in range(2):
                    a_.activation(QT[64 + MAXROW:64 + MAXROW + 3, 4 * e:4 * e + 4, 1, 128 * qb:128 * qb + 128],
                                  bank[4 + e][64 + MAXROW:64 + MAXROW + 3, :].rearrange("p (g n) -> p g n", g=4),
                                  ACT.Copy).then_inc(S["mta_done"], 1)

            for e in range(4):
                act.wait_ge(S["dve"], D[f"cmax{e}"])
                for i in range(2):
                    a = 2 * e + i
                    a_.activation(cp[:, a, :], bank[E_BANK[e]][:, 256 * i:256 * i + 256], ACT.Exp,
                                  bias=cmax[:, a:a + 1], accum_out=csum[:, a:a + 1]).then_inc(S["act"], 1)
            for e in range(2):
                act.wait_ge(S["pe"], PE[f"ptr{2 * e + 1}"])
                a_.activation(cpt[:, 4 * e + 2:4 * e + 4, :, :],
                              bank[P_BANK[2 * e + 1]][:, :].rearrange("p (a k n) -> p a k n", a=2, k=2),
                              ACT.Copy).then_inc(S["act"], 1)
            act.wait_ge(S["dve"], D["gsm"])
            a_.activation(gate[:, :, :], gsm[:, :, :], ACT.Exp, scale=1.0 / T).then_inc(S["act"], 1)
            with act.Fori(0, NB) as b:
                for n, dst in enumerate((V1[:, 0], V1[:, 1], VW[:, 0], VW[:, 1], VS[:, :, :])):
                    act.wait_ge(S["pja_ready"], b * 5 + n + 1)
                    a_.activation(dst[:, :, 0:VD], bank[4 + n % 2][:, :].rearrange("p (h v) -> p h v", v=VD),
                                  ACT.Copy).then_inc(S["pja_free"], 1)
                max_rows(b, 0)
                for n in range(NU):
                    cols = 128 * (3 + n // NH)
                    act.wait_ge(S["st_ready"], b * NU + n + 1)
                    if n >= 3:
                        act.wait_ge(S["pv_done"], b * NU + n - 2)
                    a_.activation(et[:, n % 3, 0:cols], bank[n % 4][:, 0:cols], ACT.Exp,
                                  scale=SCALE).then_inc(S["ex_done"], 1)
                    if n == MT[1]:
                        max_rows(b, 1)
                    if n >= OT_LAG and (n - OT_LAG) % 4 == 0:
                        ot_copy(b, (n - OT_LAG) // 4)
                    if n == CORNER:
                        act.wait_ge(S["ec_ready"], b + 1)
                        for f in range(2):
                            a_.activation(etc[96:128, f:NH:2, :], bank[4 + f][96:128, 0:32 * NP].rearrange(
                                "p (h n) -> p h n", n=32), ACT.Exp, scale=SCALE).then_inc(S["ec_done"], 1)
                for n in (NO - 2, NO - 1):
                    ot_copy(b, n)
            with act.Fori(0, T // STEPS // 2) as kk:
                k = kk * 2
                for s in range(2 * STEPS):
                    t = k * STEPS
                    act.wait_ge(S["g_in"], t + s + 1)
                    src = bank[s // STEPS][0:CH, 12 * (s % STEPS):12 * (s % STEPS) + 12]
                    dst = scan[:, 2:44].rearrange("p (g x) -> p g x", g=3)[:, :, 0:12:3]
                    a_.activation(dst, src.rearrange("p (g b) -> p g b", g=3), ACT.Tanh).then_inc(S["t_gate"], 1)
                    act.wait_ge(S["c_new"], t + s + 1)
                    a_.activation(bank[6][0:CH, 0:4], bank[7][0:CH, 2:12:3], ACT.Tanh,
                                  scale=0.5).then_inc(S["t_cell"], 1)

        @block.tensor
        def _(pe):
            mm, tr = nc.tensor.matmul, nc.tensor.transpose

            def part(out, lhsT, rhs, start):
                return mm(out, lhsT, rhs, start=start, stop=True, skip_group_check=True)

            def done(name, ins):
                ins.then_inc(S["pe"], 1)
                order.append(name)
                assert len(order) == PE[name], name

            order = []
            pe.wait_ge(S["w_first"], 16 * nf)
            pe.wait_ge(S["dve"], D["gsum"])
            done("gsum", mm(bank[0][:, 0:4], c["pair"][:, :], gsum[:, :], start=True, stop=True))
            pe.wait_ge(S["dve"], D["yc"])
            for i in range(2):
                n = mm(bank[i][0:CH, :], c["wqk"][:, i, :], yc[:, :, :].rearrange("p j n -> p (j n)"),
                       start=True, stop=True)
            done("qk", n)
            done("wvo", mm(bank[2][:, 0:CH], c["wv2"][:, :], c["wo9"][0:INNER, :], start=True, stop=True))
            pe.wait_ge(S["dve"], D["wvo"])
            for a in range(8):
                b, kb = a // 2, a % 2
                r = 64 * (b % 2)
                part(bank[3 + b % 2][:, CH * (a // 4 * 2 + kb):CH * (a // 4 * 2 + kb) + CH],
                     yc[r:r + 64, b // 2, 128 * kb:128 * kb + 128], wvo[r:r + 64, :], a % 4 == 0 and a < 4 or a == 2)
            mm(bank[6][:, 0:CH], c["bv9"][:, :], c["wo9"][:, :], start=True, stop=True)
            for a in range(4):
                n = tr(bank[5][:, 128 * a:128 * a + 128], xc[:, a // 2, 128 * (a % 2):128 * (a % 2) + 128], ident[:, :])
            done("vw", n)
            pe.wait_ge(S["dve"], D["xtok"])
            for b in range(NB):
                r, j = 32 * (b % 2), b // 2
                for i in range(TB):
                    n = part(bank[E_BANK[b]][:, 256 * i:256 * i + 256], qc[r:r + INNER, j, 128 * i:128 * i + 128],
                             kc[r:r + INNER, j, :], i == 0)
                done(f"energy{b}", n)
            for b in range(NB):
                pe.wait_ge(S["act"], 2 * b + 2)
                for i in range(4):
                    n = tr(bank[P_BANK[b]][:, 128 * i:128 * i + 128],
                           cp[:, 2 * b + i // 2, 128 * (i % 2):128 * (i % 2) + 128], ident[:, :])
                done(f"ptr{b}", n)
            pe.wait_ge(S["dve"], D["cpt2"])
            pe.wait_ge(S["act"], A_["cpt3"])
            for a in range(8):
                for kb in range(TB):
                    n = part(bank[2][:, CH * a:CH * a + CH], cpt[:, a, kb, :], vw[:, a // 2 * 2 + kb, :],
                             a == 0 and kb == 0)
            done("pv", n)

            def token_transposes(src, rows, banks, names, sem_done):
                for e in range(2):
                    for i in range(4):
                        n = tr(bank[banks[e]][0:rows, 128 * i:128 * i + 128], src[:, 4 * e + i, :], ident[:, :])
                    if sem_done is None:
                        done(names[e], n)
                    else:
                        n.then_inc(sem_done, 1)

            pe.wait_ge(S["dve"], D["xn"])
            token_transposes(xn, CH, (0, 1), ("xnT0", "xnT1"), None)
            pe.wait_ge(S["dve"], D["xnT"])
            pe.wait_ge(S["w_ready"], 16 * nw)
            for a in range(8):
                n = part(bank[2][:, NCAT * a:NCAT * a + NCAT], tokT[0:CH, a // 2, 128 * (a % 2):128 * (a % 2) + 128],
                         c["wcat"][:, :], a == 0)
            done("cat", n)
            pe.wait_ge(S["dve"], D["cqn"])
            pe.wait_ge(S["pool_c"], D["const"])
            token_transposes(tok, 128, (3, 4), ("tokT0", "tokT1"), None)
            for t in range(TB):
                n = mm(bank[7][:, 0:3 * NB], ones[:, :], cat[:, t:8:2, GATE:GATE + 3], start=t == 0, stop=t == 1)
            done("gate", n)
            pe.wait_ge(S["dve"], D["diag"])
            for a in range(8):
                n = part(bank[a // 4][:, 128 * (a % 4):128 * (a % 4) + 128], ones[:, :], diag[:, a, :], a % 4 == 0)
            done("srow", n)
            pe.wait_ge(S["dve"], D["sel"])
            part(bank[2][:, 0:NB], c["lt"][:, :], sel[:, :, 0], True)
            part(bank[2][:, NB:2 * NB], c["lt"][:, :], sel[:, :, 1], False)
            done("pos", part(bank[2][:, NB:2 * NB], ones[:, :], sel[:, :, 0], False))
            pe.wait_ge(S["dve"], D["psel"])
            for a in range(8):
                n = part(bank[3][0:CH, KEEP * (a // 2):KEEP * (a // 2) + KEEP], xn[:, a, :], diag[:, a, :], a == 0)
            done("selT", n)

            with pe.Fori(0, NB) as b:
                pe.wait_ge(S["staged"], b * 2 + 2)
                for n, (_, kind, pairs, wa, wb, x) in enumerate(units):
                    o = bank[(n + P_RING) % 4]
                    if n >= 4:
                        pe.wait_ge(S["pjd_free"], b * ND + n - 3)
                    if kind == "plain" or pairs == 1:
                        part(o[:, 0:T], wa, x, True)
                        last = part(o[:, T:2 * T], wb, x, False)
                    else:
                        for i in range(4):
                            last = part(o[:, KEEP * i:KEEP * i + KEEP], (wa, wb)[i // 2][:, i % 2, :], x, i == 0)
                    last.then_inc(S["pjd_ready"], 1)
                    if n % 5 == 4:
                        m = n // 5
                        if m == 0:
                            pe.wait_ge(S["x2_done"], b * 2 + 1)
                        if m >= 2:
                            pe.wait_ge(S["pja_free"], b * 5 + m - 1)
                        x, w = ((tok_b[:, 0:128], c["wv1"]), (tok_b[:, 128:256], c["wv1"]), (tok_b[:, 0:128], c["wwv"]),
                                (tok_b[:, 128:256], c["wwv"]), (xs_b[:, :], c["wsv"]))[m]
                        mm(bank[4 + m % 2][:, :], x, w[:, :], start=True, stop=True).then_inc(S["pja_ready"], 1)

                def queries(n):
                    qb, p = n // NH, n % NH // 2
                    q = slice(128 * qb, 128 * qb + 128)
                    return qb, p, q, QT[:, p, n % 2, q]

                def scores(n):
                    qb, p, q, Q = queries(n)
                    o, nk = bank[n % 4], 128 * (qb + 1)
                    if n < NH and n % 4 == 0:
                        pe.wait_ge(S["rp_done"], b * NR + 1 + RG * (n // 4 + 1))
                    if n < 4:
                        pe.wait_ge(S["pjd_free"], b * ND + ND - 3 + n)
                    else:
                        pe.wait_ge(S["sm_free"], b * NU + n - 3)
                    part(o[:, 0:nk], Q, K1[:, p, 0:nk], True)
                    part(o[:, nk:nk + 128], Q, KS[:, p, :], False)
                    part(o[:, nk + 128:nk + 256], Q, KW[:, p, q], False)
                    part(o[:, nk - 128:nk], ident16[:, :], masks16[:, 0, :], False)
                    part(o[:, nk + 128:nk + 256], ident16[:, :], masks16[:, 2, :], False).then_inc(S["sm_ready"], 1)

                def corner():
                    for h in range(NH):
                        p, f = h // 2, h % 2
                        o = bank[4 + f][0:32, 32 * p:32 * p + 32]
                        part(o, QT[:, p, f, 128:160], KW[:, p, 96:128], p == 0)
                        last = part(o, ident16[0:32, 0:32], corner16[0:32, 0, :], False)
                    last.then_inc(S["cn_ready"], 1)

                def max_transposes(qb):
                    pe.wait_ge(S["mx_ready"], b * 2 + qb + 1)
                    for p in range(NP):
                        last = tr(bank[4 + p // 4][:, 128 * (p % 4):128 * (p % 4) + 128], mx[:, qb, p, :], ident[:, :])
                    last.then_inc(S["mt_ready"], 1)

                for n in range(NU):
                    scores(n)
                    if n == CORNER:
                        pe.wait_ge(S["pja_free"], b * 5 + 5)
                        corner()
                    if n == MT[0]:
                        pe.wait_ge(S["cn_free"], b * 4 + 2)
                        max_transposes(0)

                def scores_t(n):
                    qb, p, q, Q = queries(n)
                    o, nk = bank[n % 4], 128 * (qb + 1)
                    if n % NH == 0:
                        pe.wait_ge(S["mta_done"], b * 4 + 2 * qb + 2)
                    if n < 4:
                        pe.wait_ge(S["sm_free"], b * NU + NU - 3 + n)
                    else:
                        pe.wait_ge(S["ex_done"], b * NU + n - 3)
                    for kb in range(qb + 1):
                        part(o[:, 128 * kb:128 * kb + 128], K1[:, p, 128 * kb:128 * kb + 128], Q, kb == 0)
                    part(o[:, nk:nk + 128], KS[:, p, :], Q, False)
                    part(o[:, nk + 128:nk + 256], KW[:, p, q], Q, False)
                    part(o[:, nk - 128:nk], ident16[:, :], masks16[:, 1, :], False)
                    part(o[:, nk + 128:nk + 256], ident16[:, :], masks16[:, 3, :], False).then_inc(S["st_ready"], 1)

                def corner_t():
                    for h in range(NH):
                        p, f = h // 2, h % 2
                        o = bank[4 + f][96:128, 32 * p:32 * p + 32]
                        part(o, KW[:, p, 96:128], QT[:, p, f, 128:160], p == 0)
                        last = part(o, ident16[96:128, 96:128], corner16[96:128, 1, :], False)
                    last.then_inc(S["ec_ready"], 1)

                def values(n):
                    qb, h, g = n // NH, n % NH, n // 4
                    pe.wait_ge(S["ex_done"], b * NU + n + 1)
                    if n == NH:
                        pe.wait_ge(S["ec_done"], b * 2 + 2)
                    if h % 4 == 0 and g >= 2:
                        pe.wait_ge(S["o_free"], b * NO + g - 1)
                    o = [bank[6 + g % 2][:, (4 * j + h % 4) * (VD + 1):(4 * j + h % 4 + 1) * (VD + 1)] for j in range(3)]
                    e = [et[:, n % 3, 128 * i:128 * i + 128] for i in range(4)]
                    for kb in range(qb + 1):
                        part(o[0], e[kb], V1[:, kb, h, :], kb == 0)
                    part(o[1], e[qb + 1], VS[:, h, :], True)
                    last = part(o[2], e[qb + 2], VW[:, qb, h, :], True)
                    if qb == 1:
                        last = part(o[2][0:32, :], etc[96:128, h, :], VW[96:128, 0, h, :], False)
                    last.then_inc(S["pv_done"], 1)

                def out_t(n):
                    pe.wait_ge(S["oc_ready"], b * NO + n + 1)
                    if n in (2, 3):
                        pe.wait_ge(S["ec_done"], b * 2 + n - 1)
                    elif n >= 4:
                        pe.wait_ge(S["ot_done"], b * NO + n - 1)
                    if n == NGRP:
                        pe.wait_ge(S["x2_done"], b * 2 + 2)
                    tr(bank[4 + n % 2][:, 0:128], osum[:, n % 2, 1, :], ident[:, :]).then_inc(S["ot_ready"], 1)

                def project(qb):
                    pe.wait_ge(S["ot_done"], b * NO + NGRP * (qb + 1))
                    for g in range(NGRP):
                        last = mm(bank[4][:, 0:CH], oT[:, g, :], c["wproj"][:, g, :], start=g == 0, stop=g == NGRP - 1)
                    last.then_inc(S["y_ready"], 1)

                for n in range(NU + 2):
                    if n < NU:
                        scores_t(n)
                    if n >= 2:
                        values(n - 2)
                    if n == MT[1]:
                        max_transposes(1)
                    if n >= OT_LAG and (n - OT_LAG) % 4 == 0:
                        if n == OT_LAG:
                            pe.wait_ge(S["mta_done"], b * 4 + 4)
                        out_t((n - OT_LAG) // 4)
                    if n == CORNER:
                        pe.wait_ge(S["ot_done"], b * NO + 2)
                        corner_t()
                    if n == Y_LAG:
                        project(0)
                out_t(NO - 1)
                project(1)

            pe.wait_ge(S["dve"], D["xn2"])
            token_transposes(xn, CH, (0, 1), None, S["tail"])
            token_transposes(x2, CH, (2, 3), None, S["tail"])
            pe.wait_ge(S["tail_done"], 4)

            def gate_inputs(u, first):
                for g in range(3):
                    o = bank[u][0:CH, 0:12 * STEPS].rearrange("p (t g b) -> p t g b", g=3, b=NB)[:, :, g, :]
                    part(o, u_half[:, g, :], xn2T[:, bass.ds(first, STEPS), :], g == 0)

            gate_inputs(0, 0)

            def keep_awake(n):
                for _ in range(n):
                    mm(bank[5][:, :], ident16[:, :], masks16[:, :, :].rearrange("p a n -> p (a n)"), start=True, stop=True)

            with pe.Fori(0, T // STEPS // 2) as kk:
                k = kk * 2
                for s in range(2 * STEPS):
                    pe.wait_ge(S["h_ready"], k * STEPS + s + 1)
                    o = bank[s // STEPS][0:CH, 12 * (s % STEPS):12 * (s % STEPS) + 12]
                    for g in range(3):
                        last = part(o[:, 4 * g:4 * g + 4], v_half[:, g, :], hh[:, (s - 1) % (2 * STEPS), :], False)
                    last.then_inc(S["g_in"], 1)
                    if s % STEPS == 0:
                        u = s // STEPS
                        gate_inputs(1 - u, (k + u + 1) * STEPS)
                    keep_awake(AWAKE)


def _host(inputs):
    import numpy as np
    i = {k: np.asarray(v) for k, v in inputs.items()}
    f = np.float32
    a = {"x": i["x"].reshape(NB, CH, T)}
    wqk = np.zeros((2, CH, 2, 2, 32), f)
    bqk = np.zeros((2, 32, 2), f)
    for n, (w, b) in enumerate((("wq", "bq"), ("wk", "bk"))):
        for h in range(2):
            wqk[h, :, n, h, :INNER] = i["L0_conv_" + w].T
            bqk[h, :INNER, n] = i["L0_conv_" + b]
    a["wqk"] = wqk.reshape(128, 2, 64)
    a["bqk"] = bqk.reshape(64, 2)
    a["wv2"] = np.concatenate([i["L0_conv_wv"]] * 2, 1)
    a["wo9"] = np.concatenate([i["L0_conv_wo"].T, i["L0_conv_bo"][None]], 0)
    a["bv9"] = np.concatenate([np.repeat(i["L0_conv_bv"][:, None], 128, 1), np.ones((1, 128), f)], 0)
    a["wcat"] = np.concatenate([i["L1_attn_" + n] for n in ("Wcq", "Wckv", "W_imp", "Wgate")], 1)
    a["qkn"] = np.ones((128, 1), f)
    a["qkn"][QROW:ONEROW, 0], a["qkn"][KROW:, 0] = i["L1_attn_q_norm_w"], i["L1_attn_kv_norm_w"]

    def heads(rows, nope, rope, one):
        w = np.zeros((2, rows, NP, 2, 64), f)
        if nope is not None:
            w[0, :len(nope), :, :, 0:NOPE] = nope.reshape(-1, NP, 2, NOPE)
        if rope is not None:
            r = rope.reshape(-1, NP, 2, 2, ROPE // 2)
            w[0, :len(rope), :, :, ROPEROW:] = r.reshape(-1, NP, 2, ROPE)
            w[1, :len(rope), :, :, ROPEROW:] = r[:, :, :, ::-1].reshape(-1, NP, 2, ROPE)
        if one is not None:
            w[0, ONEROW, :, :, MAXROW + one] = 1.0
        return w.reshape(2, rows, NP, 128)

    a["wqa"], a["wqb"] = heads(KROW - QROW, i["L1_attn_Wq_nope"], i["L1_attn_Wq_rope"], None)
    a["wk1"] = heads(RKV, i["L1_attn_Wk_nope"], None, None)[0]
    kr = heads(KROW, None, np.repeat(i["L1_attn_Wk_rope"][:, None], NH, 1), 0)
    a["wkr"] = np.ascontiguousarray(kr[:, :, 0, :].transpose(1, 0, 2))
    for n, src, one in (("ww", "Wwin_k", 2), ("ws", "Wsel_k", 1)):
        w = i["L1_attn_" + src].reshape(CH, NH, HD)
        a[n + "a"], a[n + "b"] = heads(KROW, w[..., :NOPE], w[..., NOPE:], one)
    a["wv1"], a["wwv"], a["wsv"] = (i["L1_attn_" + n] for n in ("Wv", "Wwin_v", "Wsel_v"))
    a["wproj"] = i["L1_attn_Wproj"].reshape(NGRP, 128, CH).transpose(1, 0, 2)
    a["u3"] = np.stack([np.concatenate([i["L1_ffn_U_" + g], i["L1_ffn_b_" + g][None]], 0) for g in "cio"], 1)
    a["v3"] = np.stack([np.concatenate([i["L1_ffn_V_" + g], np.zeros((128 - CH, CH), f)], 0) for g in "cio"], 1)

    p = np.arange(128)
    a["ident"], a["ones"] = np.eye(128, dtype=f), np.ones((128, 128), f)
    a["pair"] = np.where(p[:, None] // 2 == p[None] // 2, 0.5, 0.0).astype(f)
    a["lt"] = (p[:, None] < p[None]).astype(f)
    j = np.arange(T)
    a["tie"] = (j[None, None] < (128 * np.arange(TB)[None, :, None] + p[:, None, None])).astype(f)
    a["iota"] = np.broadcast_to(p.astype(f)[None], (128, 128))
    freq = 1.0 / 10000.0 ** (np.arange(0, ROPE, 2, dtype=np.float32) / ROPE)
    ang = np.outer(np.arange(T, dtype=np.float32), freq)
    cos, sin = np.ones((2, 64, T), f), np.zeros((2, 64, T), f)
    half = ROPE // 2
    for k in range(2):
        cos[:, ROPEROW + half * k:ROPEROW + half * k + half] = np.cos(ang).T
        sin[:, ROPEROW + half * k:ROPEROW + half * k + half] = (-1, 1)[k] * np.sin(ang).T
    a["cos"], a["sin"] = cos.reshape(128, T), sin.reshape(128, T)
    low = f(-1e30)
    d = p[:, None] - p[None]
    causal, window = np.where(d >= 0, f(0), low), np.where((d >= 0) & (d < WINDOW), f(0), low)
    a["masks"] = np.stack([causal, causal.T, window, window.T], 1)
    r = np.arange(32)
    corner = np.where(r[None] > r[:, None], f(0), low)
    a["corner"] = np.zeros((128, 2, 32), f)
    a["corner"][0:32, 0] = corner
    a["corner"][96:128, 1] = corner.T
    return {k: np.ascontiguousarray(v, dtype=v.dtype) for k, v in a.items()}


def kernel(**inputs):
    import concourse.bacc as _bacc
    from concourse.bass_utils import run_bass_kernel_spmd as _run

    arrays = _host(inputs)
    nc = _bacc.Bacc("TRN2", target_bir_lowering=False, num_devices=1)
    d = {k: nc.dram_tensor(k + "_dram", v.shape, mybir.dt.from_np(v.dtype), kind="ExternalInput").ap()
         for k, v in arrays.items()}
    out = nc.dram_tensor("out_dram", (NB, CH, T), F32, kind="ExternalOutput").ap()
    conv_attn_lstm(nc, d, out)
    r = _run(nc, [{k + "_dram": v for k, v in arrays.items()}], core_ids=[0])
    return r.results[0]["out_dram"].reshape(NB, CH, 16, 16)
```

```python
from contextlib import ExitStack

import concourse.bass as bass
from concourse import mybir

F32 = mybir.dt.float32
BF16 = mybir.dt.bfloat16
ALU = mybir.AluOpType
ACT = mybir.ActivationFunctionType
AX = mybir.AxisListType

NB, CH, T = 4, 64, 256
INNER = 8
NH, NOPE, ROPE, VD = 16, 32, 16, 32
HD = NOPE + ROPE
RQ, RKV = 24, 32
WINDOW, KEEP = 32, 128
NP = NH // 2
TB = T // 128
MAXROW, ROPEROW = 32, 48
NGRP = NH // 4
CQ, CKV, IMP, GATE = 0, RQ, RQ + RKV, RQ + RKV + 1
NCAT = GATE + 3
QROW, ONEROW, KROW = CH, CH + RQ, CH + 32
SCALE = float(HD) ** -0.5
PLACED = {"wqa": (QROW, KROW), "wqb": (QROW, KROW), "wk1": (KROW, 128), "wwa": (0, KROW), "wwb": (0, KROW),
          "wsa": (0, KROW), "wsb": (0, KROW), "wkr": (0, KROW), "wv1": (KROW, 128), "wwv": (0, CH), "wsv": (0, CH)}
FIRST = ("pair", "ident", "wqk", "bqk", "wv2", "wo9", "bv9")
AWAKE = 3
STEPS = 8


def conv_attn_lstm(nc, d, out):
    with ExitStack() as ctx:
        def sb(name, shape, dt=F32):
            return ctx.enter_context(nc.sbuf_tensor(name, shape, dt))

        def sem(name):
            return ctx.enter_context(nc.semaphore(name))

        c = {k: sb("w_" + k, [128 if k in PLACED else d[k].shape[0], *d[k].shape[1:]]) for k in d if k != "x"}
        ident, ones = c["ident"], c["ones"]
        idle16 = sb("idle16", [128, 512], BF16)
        ident16 = sb("ident16", [128, 128], BF16)
        masks16 = sb("masks16", [128, 4, 128], BF16)
        corner16 = sb("corner16", [128, 2, 32], BF16)
        krw = sb("krw", [128, 2, 128])
        u_half = sb("u_half", [CH + 1, 3, CH])
        v_half = sb("v_half", [128, 3, CH])

        xc = sb("xc", [128, 2, T])
        yc = sb("yc", [128, 2, T])
        qc, kc = sb("qc", [CH, 2, T]), sb("kc", [CH, 2, T])
        bnc = sb("bnc", [128, 2, 6])
        mvc = sb("mvc", [128, 2, 2])
        gsum = sb("gsum", [128, 4])
        grp = sb("grp", [128, 4])
        gtmp = sb("gtmp", [128, 2])
        grstd = sb("grstd", [128, 2])
        wvo = sb("wvo", [128, CH])
        cst = sb("cst", [128, CH])
        vw = sb("vw", [128, NB * TB, CH])
        cmax = sb("cmax", [128, NB * TB])
        csum = sb("csum", [128, NB * TB])
        crec = sb("crec", [128, NB * TB])
        cp = sb("cp", [128, NB * TB, T])
        cpt = sb("cpt", [128, NB * TB, TB, 128])
        x1_all, x2_all = (sb(n, [128, (NB + 1) * TB, CH]) for n in ("x1", "x2"))
        x1, x2 = x1_all[:, TB:, :], x2_all[:, TB:, :]
        tmp = sb("tmp", [128, NB * TB, CH])
        tok = sb("tok", [128, NB * TB, 128])
        xn = tok[:, :, 0:CH]
        bn = sb("bn", [128, NB * TB, 6])
        mv = sb("mv", [128, NB * TB, 2])
        rstd = sb("rstd", [128, NB * TB])
        tokT = sb("tokT", [128, NB + 1, T])
        cat = sb("cat", [128, NB * TB, NCAT])
        sq = sb("sq", [128, NB * TB, RQ + RKV])
        ssq, rms = sb("ssq", [128, 2, NB * TB]), sb("rms", [128, 2, NB * TB])
        vare = sb("vare", [128, NB * TB])
        rtmp, rint = sb("rtmp", [128, 16]), sb("rint", [128, 16], mybir.dt.int32)
        gsm = sb("gsm", [128, NB, 3])
        gm1 = sb("gm1", [128, NB])
        gate = sb("gate", [128, NB, 3])
        diag = sb("diag", [128, NB * TB, 128])
        eqs = cpt[:, :, :, :].rearrange("p a k n -> p a (k n)")
        rank = sb("rank", [128, NB * TB])
        sel = sb("sel", [128, NB, TB])
        pos = sb("pos", [128, TB, NB])
        xsT = sb("xsT", [128, NB + 1, KEEP])

        tok_b, xs_b = sb("tok_b", [128, T]), sb("xs_b", [128, KEEP])
        QT = sb("QT", [128, NP, 2, T])
        K1, KW = (sb(n, [128, NP, T]) for n in ("K1", "KW"))
        KS = sb("KS", [128, NP, KEEP])
        krp = sb("krp", [128, T])
        ks_kept = sb("ks_kept", [128, NB, NP, KEEP])
        kw_kept = sb("kw_kept", [128, NB, NP, WINDOW])
        v1_kept = cpt[:, :, :, :].rearrange("p a k n -> p (a k n)").rearrange("p (b h v) -> p b h v", b=NB, h=NH)
        vw_kept = cp[128 - WINDOW:, :, :].rearrange("p a n -> p (a n)").rearrange("p (b h v) -> p b h v", b=NB, h=NH)
        V1, VW = (sb(n, [128, TB, NH, VD + 1]) for n in ("V1", "VW"))
        VS = sb("VS", [128, NH, VD + 1])
        ra, rb = sb("ra", [128, 3, T]), sb("rb", [128, 3, T])
        nm = sb("nm", [128, NH, 4])
        cm = sb("cm", [32, NH])
        mx = sb("mx", [128, NP, 128])
        et = sb("et", [128, 3, 512])
        etc = sb("etc", [128, NH, 32])
        orec, ow = sb("orec", [128, 2, 12]), sb("ow", [128, 2, 12])
        oprod = sb("oprod", [128, 2, 12, VD])
        osum = sb("osum", [128, 2, 2, 128])
        oT = sb("oT", [128, NGRP, 128])

        xn2T = sb("xn2T", [CH + 1, T + STEPS, NB])
        x2T = diag[0:CH, :, :].rearrange("p (b t) n -> p b (t n)", b=NB)
        y = cp[0:CH, 0:NB, :]
        hh = sb("hh", [128, 2 * STEPS, NB])
        hs = sb("hs", [CH, 2, STEPS, NB])
        half = sb("half", [CH, STEPS, NB])
        scan = sb("scan", [CH, 56])
        bank = [ctx.enter_context(nc.psum_tensor(f"bank{i}", [128, 512], F32)) for i in range(8)]

        names = """w_first w_ready x_ready dve act pe pool pool_c staged pjd_ready pjd_free pja_ready pja_free rp_done
            sm_ready sm_free cn_ready cn_free mx_ready mt_ready mtv_done mta_done x2_done q_low
            hs_ready st_ready ex_done ec_ready ec_done pv_done o_free oc_ready ot_ready ot_done
            y_ready kept restored tok_ready xs_ready h_ready g_in o_in t_gate c_new t_cell hc_ready
            y_done out_done tail tail_done""".split()
        S = {n: sem(n) for n in names}
        block = ctx.enter_context(nc.Block())
        later = [k for k in c if k not in FIRST]
        nf, nw = len(FIRST), len(later)
        D = {}
        A_ = {"exp": 0, "cpt1": 9, "cpt3": 10, "gate": 11}
        E_BANK, P_BANK = (6, 7, 0, 1), (2, 3, 4, 5)
        def projections(qb):
            q, keys = slice(128 * qb, 128 * qb + 128), slice(0, 128 * qb + 128)
            w = lambda k, p, n: [c[k][:, i, :] for i in range(p, p + n)]
            units = [("rope", krp[:, keys].unsqueeze(1), [krw[:, 0, :]], [krw[:, 1, :]], tok_b[:, keys], keys)]
            n1 = 512 // keys.stop
            for p in range(0, NP, 2):
                units.append(("query", QT[:, p:p + 2, :, q], w("wqa", p, 2), w("wqb", p, 2), tok_b[:, q], q))
                units.append(("rope", KW[:, p:p + 2, q], w("wwa", p, 2), w("wwb", p, 2), tok_b[:, q], q))
                if qb == 0:
                    units.append(("rope", KS[:, p:p + 2, :], w("wsa", p, 2), w("wsb", p, 2), xs_b[:, :],
                                  slice(0, KEEP)))
                if p % n1 == 0:
                    units.append(("plain", K1[:, p:p + n1, keys], w("wk1", p, n1), [], tok_b[:, keys], keys))
            return units

        def value_units(qb):
            x = tok_b[:, 128 * qb:128 * qb + 128]
            return [(V1[:, qb], x, c["wv1"]), (VW[:, qb], x, c["wwv"]), (VS[:, :, :], xs_b[:, :], c["wsv"])]

        UNITS, VALUES = [projections(qb) for qb in range(TB)], [value_units(qb) for qb in range(TB)]
        ND = [len(u) for u in UNITS]
        NR = [sum(k != "plain" for k, *_ in u) for u in UNITS]
        NV = [len(u) for u in VALUES]
        NG = [(n - 1) // NGRP for n in NR]
        RING, AUX, OUT, CELL, GATES = 3, 3, 4, 6, 7

        def unit_bank(qb, n):
            return bank[(n - ND[qb]) % RING]

        SLOTS = T // TB // NB
        P_SLOTS, M_SLOTS = 7, 8
        E_SLOT = P_SLOTS + M_SLOTS
        MT_SLOTS, EC_SLOTS = (E_SLOT - 2, E_SLOT + 1), (E_SLOT - 1, E_SLOT + 3)

        def unit_slot(qb, n):
            return n * P_SLOTS // ND[qb]

        def max_slot(h):
            return P_SLOTS + h * M_SLOTS // NH

        def out_slot(g):
            return E_SLOT + 4 * g + 6

        FIRST_VALUES = 3
        RESTORE_SLOTS = (0, 1, 2, 6)

        def before(qb, b, per_batch):
            return b * per_batch[qb] + qb * NB * per_batch[0]

        def same(qb, b, n):
            return before(qb, b, (n, n))

        def turned(qb, b):
            return same(qb, b, NGRP) + qb

        @block.sync
        def _(sp):
            xv = d["x"].rearrange("(j h) c n -> h c j n", h=2)
            for h in range(2):
                sp.dma_start(xc[64 * h:64 * h + 64, :, :], xv[h]).then_inc(S["x_ready"], 16)
            for k in FIRST:
                sp.dma_start(c[k][...], d[k][...]).then_inc(S["w_first"], 16)
            sp.wait_ge(S["y_done"], T // STEPS)
            sp.dma_start(out.rearrange("b c n -> c b n"), y[:, :, :]).then_inc(S["out_done"], 16)
            sp.wait_ge(S["out_done"], 16)

        PE = {n: i + 1 for i, n in enumerate(
            "gsum qk wvo vw energy0 energy1 energy2 energy3 ptr0 ptr1 ptr2 ptr3 pv xnT0 xnT1 cat tokT0 tokT1 "
            "gate srow pos selT".split())}

        @block.gpsimd
        def _(pool):
            made = [0]

            def const(ins):
                made[0] += 1
                ins.then_inc(S["pool_c"], 1)
                pool.wait_ge(S["pool_c"], made[0])

            const(nc.gpsimd.memset(idle16[:, :], 0.0))
            const(nc.gpsimd.memset(oT[:, :, :], 0.0))
            const(nc.gpsimd.memset(x1_all[:, 0:TB, :], 0.0))
            nc.gpsimd.memset(osum[:, :, :, :], 0.0).then_inc(S["oc_ready"], 1)
            pool.wait_ge(S["oc_ready"], 1)
            for k, (r0, r1) in PLACED.items():
                t = krw if k == "wkr" else c[k]
                if r0 > 0:
                    const(nc.gpsimd.memset(t[0:r0], 0.0))
                if r1 < 128:
                    const(nc.gpsimd.memset(t[r1:128], 0.0))
            const(nc.gpsimd.memset(tok[:, :, ONEROW:KROW], 1.0))
            const(nc.gpsimd.memset(xsT[CH:128, :, :], 1.0))
            const(nc.gpsimd.memset(xn2T[CH:CH + 1, :, :], 1.0))
            const(nc.gpsimd.memset(mx[:, :, :], 0.0))
            const(nc.gpsimd.memset(QT[64:128, :, 0, :], 0.0))
            const(nc.gpsimd.memset(QT[0:64, :, 1, :], 0.0))
            const(nc.gpsimd.memset(V1[:, :, :, VD:VD + 1], 1.0))
            const(nc.gpsimd.memset(VW[:, :, :, VD:VD + 1], 1.0))
            const(nc.gpsimd.memset(VS[:, :, VD:VD + 1], 1.0))
            const(nc.gpsimd.memset(hh[:, :, :], 0.0))
            const(nc.gpsimd.memset(scan[:, :], 0.0))
            const(nc.gpsimd.memset(xn2T[0:CH, T:T + STEPS, :], 0.0))
            const(nc.gpsimd.memset(half[:, :, :], 0.5))
            nc.gpsimd.memset(hs[:, 0, :, :], 0.0).then_inc(S["hs_ready"], 1)
            nc.gpsimd.memset(hs[:, 1, :, :], 0.0).then_inc(S["hs_ready"], 1)
            const(nc.gpsimd.memset(scan[:, 1:13:3], 1.0))
            const(nc.gpsimd.memset(scan[:, 17:29:3], 1.0))
            D["const"] = made[0]

            def stage(b):
                nc.gpsimd.tensor_copy(tok_b[:, :], tokT[:, b, :]).then_inc(S["staged"], 1)
                nc.gpsimd.tensor_copy(xs_b[:, :], xsT[:, b, :]).then_inc(S["staged"], 1)

            def attention(b, qb, outputs=None):
                u = q = 0
                for n, (kind, dst, wa, _, x, at) in enumerate(UNITS[qb]):
                    if kind == "plain":
                        continue
                    cols = len(wa) * (at.stop - at.start)
                    pool.wait_ge(S["pjd_free"], before(qb, b, ND) + n + 1)
                    src = [t[:, u % 3, 0:cols].rearrange("p (g n) -> p g n", g=len(wa)) for t in (ra, rb)]
                    u += 1
                    if kind == "query":
                        q += 1
                        nc.gpsimd.tensor_tensor(dst[0:64, :, 0, :], src[0][0:64], src[1][0:64],
                                                ALU.add).then_inc(S["q_low"], 1)
                        pool.wait_ge(S["q_low"], same(qb, b, NGRP) + q)
                        nc.gpsimd.tensor_tensor(dst[64:128, :, 1, :], src[0][64:128], src[1][64:128],
                                                ALU.add).then_inc(S["rp_done"], 1)
                        pool.wait_ge(S["rp_done"], before(qb, b, NR) + u)
                    else:
                        nc.gpsimd.tensor_tensor(dst, src[0], src[1], ALU.add).then_inc(S["rp_done"], 1)
                if qb == 0:
                    pool.wait_ge(S["rp_done"], before(qb, b, NR) + NR[qb])
                    nc.gpsimd.tensor_copy(kw_kept[:, b, :, :], KW[:, :, 128 - WINDOW:128]).then_inc(S["kept"], 1)
                pool.wait_ge(S["pja_ready"], before(qb, b, NV) + NV[qb])
                pool.wait_ge(S["pjd_ready"], before(qb, b, ND) + ND[qb])
                if outputs:
                    outputs(b, 0)
                stage(b + 1)
                if outputs:
                    outputs(b, 1)
                for n in range(NGRP):
                    pool.wait_ge(S["o_free"], same(qb, b, NGRP) + n + 1)
                    pool.wait_ge(S["ot_ready"], turned(qb, b) + max(n, 1))
                    part = [oprod[:, n % 2, 4 * j:4 * j + 4, :].rearrange("p h v -> p (h v)") for j in range(3)]
                    nc.gpsimd.tensor_tensor(osum[:, n % 2, 0, :], part[0], part[1], ALU.add).then_inc(S["pool"], 1)
                    pool.wait_ge(S["pool"], same(qb, b, NGRP) + n + 1)
                    nc.gpsimd.tensor_tensor(osum[:, n % 2, 1, :], osum[:, n % 2, 0, :], part[2],
                                            ALU.add).then_inc(S["oc_ready"], 1)
                    if outputs and n == 1:
                        outputs(b, 2)

            def chunk_outputs(k, u):
                pool.wait_ge(S["h_ready"], (k + u + 1) * STEPS + 1)
                nc.gpsimd.tensor_tensor(hs[:, u % 2, :, :], hh[0:CH, u % 2 * STEPS:(u % 2 + 1) * STEPS, :],
                                        half[:, :, :], ALU.mult).then_inc(S["hs_ready"], 1)
                pool.wait_ge(S["hs_ready"], k + u + 3)
                cols = bass.ds((k + u) * STEPS, STEPS)
                nc.gpsimd.tensor_tensor(y[:, :, cols], x2T[:, :, cols],
                                        hs[:, u % 2, :, :].rearrange("p t b -> p b t"),
                                        ALU.add).then_inc(S["y_done"], 1)

            pool.wait_ge(S["tok_ready"], 1)
            nc.gpsimd.tensor_copy(tok_b[:, :], tokT[:, 0, :]).then_inc(S["staged"], 1)
            const(nc.gpsimd.tensor_copy(tokT[:, NB, :], tokT[:, 0, :]))
            pool.wait_ge(S["xs_ready"], 1)
            nc.gpsimd.tensor_copy(xs_b[:, :], xsT[:, 0, :]).then_inc(S["staged"], 1)
            const(nc.gpsimd.tensor_copy(xsT[:, NB, :], xsT[:, 0, :]))
            with pool.Fori(0, NB) as b:
                attention(b, 0)
            pool.wait_ge(S["tail_done"], 2)
            with pool.Fori(0, NB) as b:
                attention(b, 1, lambda b, u: chunk_outputs(b * (SLOTS // STEPS), u))
                chunk_outputs(b * (SLOTS // STEPS), 3)
            pool.wait_ge(S["tail_done"], 4)
            with pool.Fori(0, T // TB // STEPS // 2) as kk:
                for u in range(2):
                    chunk_outputs(kk * 2 + T // TB // STEPS, u)

        @block.vector
        def _(dve):
            count = [0]

            def inc(ins):
                ins.then_inc(S["dve"], 1)
                count[0] += 1
                return count[0]

            def after(value):
                dve.wait_ge(S["dve"], value)

            def link(ins):
                after(inc(ins))

            v = nc.vector

            def rsqrt(y, x, n):
                i, t = rint[:, 0:n], rtmp[:, 0:n]
                link(v.tensor_scalar(i, x.bitcast(mybir.dt.int32), 1, None, ALU.logical_shift_right))
                link(v.tensor_scalar(y.bitcast(mybir.dt.int32), i, -1.0, float(0x5F3759DF), ALU.mult, ALU.add))
                for _ in range(3):
                    link(v.scalar_tensor_tensor(out=t, in0=y, scalar=-0.5, in1=y, op0=ALU.mult, op1=ALU.mult))
                    link(v.tensor_tensor(t, t, x, ALU.mult))
                    link(v.scalar_tensor_tensor(out=y, in0=t, scalar=1.5, in1=y, op0=ALU.add, op1=ALU.mult))

            dve.wait_ge(S["x_ready"], 32)
            for j in range(2):
                n = inc(v.bn_stats(bnc[:, j, :], xc[:, j, :]))
            after(n)
            for j in range(2):
                n = inc(v.bn_aggr(mvc[:, j, :], bnc[:, j, :]))
            after(n)
            inc(v.tensor_copy(gsum[:, 0:2], mvc[:, :, 0]))
            link(v.tensor_tensor(gtmp[:, :], mvc[:, :, 0], mvc[:, :, 0], ALU.mult))
            D["gsum"] = inc(v.tensor_tensor(gsum[:, 2:4], mvc[:, :, 1], gtmp[:, :], ALU.add))
            dve.wait_ge(S["w_first"], 16 * nf)
            inc(v.tensor_copy(ident16[:, :], ident[:, :]))
            dve.wait_ge(S["pe"], PE["gsum"])
            link(v.tensor_copy(grp[:, :], bank[0][:, 0:4]))
            link(v.tensor_tensor(gtmp[:, :], grp[:, 0:2], grp[:, 0:2], ALU.mult))
            link(v.tensor_tensor(gtmp[:, :], grp[:, 2:4], gtmp[:, :], ALU.subtract))
            link(v.tensor_scalar(gtmp[:, :], gtmp[:, :], 1e-5, None, ALU.add))
            rsqrt(grstd[:, :], gtmp[:, :], 2)
            for j in range(2):
                D["yc"] = inc(v.tensor_scalar(yc[:, j, :], xc[:, j, :], grp[:, j:j + 1], grstd[:, j:j + 1],
                                              ALU.subtract, ALU.mult))
            dve.wait_ge(S["pe"], PE["wvo"])
            D["wvo"] = inc(v.tensor_copy(wvo[:, :], bank[2][:, 0:CH]))
            dve.wait_ge(S["pe"], PE["qk"])
            inc(v.tensor_scalar(qc[:, :, :], bank[0][0:CH, :].rearrange("p (j n) -> p j n", j=2), c["bqk"][:, 0:1],
                                None, ALU.add))
            D["qk"] = inc(v.tensor_scalar(kc[:, :, :], bank[1][0:CH, :].rearrange("p (j n) -> p j n", j=2),
                                          c["bqk"][:, 1:2], None, ALU.add))
            dve.wait_ge(S["pe"], PE["vw"])
            for h in range(2):
                inc(v.tensor_copy(vw[:, :, :].rearrange("p (j h k) n -> p j h k n", j=2, h=2)[:, :, h],
                                  bank[3 + h][:, 0:4 * CH].rearrange("p (j k n) -> p j k n", j=2, n=CH)))
            link(v.tensor_copy(cst[:, :], bank[6][:, 0:CH]))
            for j in range(2):
                for t in range(TB):
                    src = bank[5][:, 256 * j + 128 * t:256 * j + 128 * t + 128].rearrange("p (h c) -> p h c", h=2)
                    D["xtok"] = inc(v.tensor_tensor(
                        x1[:, 4 * j + t:4 * j + t + 3:2, :], src,
                        cst[:, :].unsqueeze(1).broadcast_to([128, 2, CH]), ALU.add))
            for e in range(4):
                dve.wait_ge(S["pe"], PE[f"energy{e}"])
                src = bank[E_BANK[e]][:, :].rearrange("p (a n) -> p a n", a=2)
                D[f"cmax{e}"] = inc(v.tensor_reduce(cmax[:, 2 * e:2 * e + 2], src, AX.X, ALU.max, negate=True))
            for e in range(2):
                dve.wait_ge(S["pe"], PE[f"ptr{2 * e}"])
                D[f"cpt{2 * e}"] = inc(v.tensor_copy(
                    cpt[:, 4 * e:4 * e + 2, :, :],
                    bank[P_BANK[2 * e]][:, :].rearrange("p (a k n) -> p a k n", a=2, k=2)))
            dve.wait_ge(S["w_ready"], 16 * nw)
            inc(v.tensor_copy(masks16[:, :, :], c["masks"][:, :, :]))
            inc(v.tensor_copy(corner16[:, :, :], c["corner"][:, :, :]))
            inc(v.tensor_scalar(u_half[:, 1:3, :], c["u3"][:, 1:3, :], 0.5, None, ALU.mult))
            inc(v.tensor_copy(u_half[:, 0, :], c["u3"][:, 0, :]))
            inc(v.tensor_scalar(v_half[:, 1:3, :], c["v3"][:, 1:3, :], 0.25, None, ALU.mult))
            inc(v.tensor_scalar(v_half[:, 0, :], c["v3"][:, 0, :], 0.5, None, ALU.mult))
            inc(v.tensor_copy(krw[CH:KROW, :, :], c["wkr"][CH:KROW, :, :]))
            inc(v.tensor_scalar(krw[0:CH, :, :], c["wkr"][0:CH, :, :], 1.0 / NH, None, ALU.mult))
            dve.wait_ge(S["act"], A_["exp"] + 4 * 2)
            link(v.reciprocal(crec[:, :], csum[:, :]))
            dve.wait_ge(S["pe"], PE["pv"])
            link(v.tensor_tensor(tmp[:, :, :], bank[2][:, :].rearrange("p (a n) -> p a n", n=CH),
                                 crec[:, :].unsqueeze(2).broadcast_to([128, NB * TB, CH]), ALU.mult))
            link(v.tensor_tensor(x1[:, :, :], x1[:, :, :], tmp[:, :, :], ALU.add))

            def layer_norm(dst, src, first, every):
                blocks = list(range(first, NB * TB, every))
                for i, a in enumerate(blocks):
                    n = inc(v.bn_stats(bn[:, i, :], src[:, a, :]))
                after(n)
                for i in range(len(blocks)):
                    n = inc(v.bn_aggr(mv[:, i, :], bn[:, i, :]))
                after(n)
                m = len(blocks)
                link(v.tensor_scalar(vare[:, 0:m], mv[:, 0:m, 1], 1e-5, None, ALU.add))
                rsqrt(rstd[:, 0:m], vare[:, 0:m], m)
                for i, a in enumerate(blocks):
                    n = inc(v.tensor_scalar(dst[:, a, :], src[:, a, :], mv[:, i, 0:1], rstd[:, i:i + 1],
                                            ALU.subtract, ALU.mult))
                return n

            D["xn"] = layer_norm(xn, x1, 0, 1)
            for e in range(2):
                dve.wait_ge(S["pe"], PE[f"xnT{e}"])
                D["xnT"] = inc(v.tensor_copy(tokT[0:CH, 2 * e:2 * e + 2, :],
                                             bank[e][0:CH, :].rearrange("p (a n) -> p a n", a=2)))
            dve.wait_ge(S["pe"], PE["cat"])
            link(v.tensor_copy(cat[:, :, :], bank[2][:, 0:8 * NCAT].rearrange("p (a n) -> p a n", n=NCAT)))
            D["cat"] = count[0]
            link(v.tensor_tensor(sq[:, :, :], cat[:, :, 0:IMP], cat[:, :, 0:IMP], ALU.mult))
            inc(v.tensor_reduce(ssq[:, 0, :], sq[:, :, 0:RQ], AX.X, ALU.add))
            link(v.tensor_reduce(ssq[:, 1, :], sq[:, :, RQ:IMP], AX.X, ALU.add))
            inc(v.tensor_scalar(ssq[:, 0, :], ssq[:, 0, :], 1.0 / RQ, 1e-6, ALU.mult, ALU.add))
            link(v.tensor_scalar(ssq[:, 1, :], ssq[:, 1, :], 1.0 / RKV, 1e-6, ALU.mult, ALU.add))
            rsqrt(rms[:, :, :].rearrange("p k a -> p (k a)"), ssq[:, :, :].rearrange("p k a -> p (k a)"), 16)
            inc(v.tensor_tensor(tok[:, :, QROW:ONEROW], cat[:, :, CQ:CKV],
                                rms[:, 0, :].unsqueeze(2).broadcast_to([128, 8, RQ]), ALU.mult))
            D["cqn"] = inc(v.tensor_tensor(tok[:, :, KROW:128], cat[:, :, CKV:IMP],
                                           rms[:, 1, :].unsqueeze(2).broadcast_to([128, 8, RKV]), ALU.mult))
            for a in range(8):
                D["diag"] = inc(v.tensor_scalar(diag[:, a, :], ident[:, :], cat[:, a, IMP:IMP + 1], None, ALU.mult))
            for e in range(2):
                dve.wait_ge(S["pe"], PE[f"tokT{e}"])
                done = v.tensor_scalar(tokT[CH:128, 2 * e:2 * e + 2, :],
                                       bank[3 + e][CH:128, :].rearrange("p (a n) -> p a n", a=2),
                                       c["qkn"][CH:128, 0:1], None, ALU.mult)
            done.then_inc(S["tok_ready"], 1)
            dve.wait_ge(S["pe"], PE["gate"])
            link(v.tensor_copy(gsm[:, :, :], bank[7][:, 0:3 * NB].rearrange("p (b g) -> p b g", g=3)))
            link(v.tensor_reduce(gm1[:, :], gsm[:, :, :], AX.X, ALU.max))
            D["gsm"] = inc(v.tensor_tensor(gsm[:, :, :], gsm[:, :, :],
                                           gm1[:, :].unsqueeze(2).broadcast_to([128, NB, 3]), ALU.subtract))
            dve.wait_ge(S["pe"], PE["srow"])
            def row(a):
                return bank[a // 4][:, 256 * ((a // 2) % 2):256 * ((a // 2) % 2) + 256]

            for a in range(8):
                n = inc(v.scalar_tensor_tensor(out=eqs[:, a, :], in0=row(a), scalar=cat[:, a, IMP:IMP + 1],
                                               in1=c["tie"][:, a % 2, :], op0=ALU.is_equal, op1=ALU.mult))
            after(n)
            for a in range(8):
                n = inc(v.scalar_tensor_tensor(out=eqs[:, a, :], in0=row(a), scalar=cat[:, a, IMP:IMP + 1],
                                               in1=eqs[:, a, :], op0=ALU.is_gt, op1=ALU.add,
                                               accum_out=rank[:, a:a + 1]))
            after(n)
            D["sel"] = inc(v.tensor_scalar(sel[:, :, :], rank[:, :].rearrange("p (b t) -> p b t", t=TB), KEEP - 0.5,
                                           None, ALU.is_lt))
            after(D["sel"])
            dve.wait_ge(S["act"], A_["gate"])
            link(v.tensor_reduce(gm1[:, :], gate[:, :, :], AX.X, ALU.add))
            link(v.reciprocal(gm1[:, :], gm1[:, :]))
            link(v.tensor_tensor(gate[:, :, :], gate[:, :, :], gm1[:, :].unsqueeze(2).broadcast_to([128, NB, 3]),
                                 ALU.mult))
            dve.wait_ge(S["pe"], PE["pos"])
            link(v.tensor_copy(pos[:, :, :], bank[2][:, 0:8].rearrange("p (t b) -> p t b", t=TB)))
            for a in range(8):
                D["psel"] = inc(v.tensor_scalar(diag[:, a, :], c["iota"][:, :], pos[:, a % 2, a // 2:a // 2 + 1],
                                                sel[:, a // 2, a % 2:a % 2 + 1], ALU.is_equal, ALU.mult))
            dve.wait_ge(S["pe"], PE["selT"])
            dve.wait_ge(S["pool_c"], D["const"])
            v.tensor_copy(xsT[0:CH, 0:NB, :], bank[3][0:CH, :].rearrange("p (b n) -> p b n", b=NB)
                          ).then_inc(S["xs_ready"], 1)
            D["phase1"] = count[0]

            def residual(b, qb):
                dve.wait_ge(S["y_ready"], same(qb, b, 1) + qb + 1)
                v.tensor_tensor(x2_all[:, TB * b + qb, :], x1_all[:, TB * b + qb, :], bank[AUX][:, 0:CH],
                                ALU.add).then_inc(S["x2_done"], 1)


            def attention(b, qb, steps):
                nseg = 3 + qb
                u = 0

                def rotate(n):
                    nonlocal u
                    kind, dst, wa, _, x, at = UNITS[qb][n]
                    g, w = len(wa), at.stop - at.start
                    src = unit_bank(qb, n)
                    dve.wait_ge(S["pjd_ready"], before(qb, b, ND) + n + 1)
                    if kind == "plain":
                        dve.wait_ge(S["rp_done"], before(qb, b, NR) + 1)
                        v.tensor_tensor(dst, src[:, :].rearrange("p (g n) -> p g n", g=g),
                                        krp[:, at].unsqueeze(1).broadcast_to([128, g, w]),
                                        ALU.add).then_inc(S["pjd_free"], 1)
                        return
                    if u >= 3:
                        dve.wait_ge(S["rp_done"], before(qb, b, NR) + u - 2)
                    A, B, a_, b_ = (t.rearrange("p (g n) -> p g n", g=g) for t in (
                        src[:, 0:g * w], src[:, T:T + g * w], ra[:, u % 3, 0:g * w], rb[:, u % 3, 0:g * w]))
                    C, R = (t[:, at].unsqueeze(1).broadcast_to([128, g, w]) for t in (c["cos"], c["sin"]))
                    v.tensor_tensor(a_, A, C, ALU.mult)
                    v.tensor_tensor(b_, B, R, ALU.mult).then_inc(S["pjd_free"], 1)
                    u += 1

                def maxima(h):
                    dve.wait_ge(S["sm_ready"], same(qb, b, NH) + h + 1)
                    v.tensor_reduce(nm[:, h, 0:nseg], bank[h % RING][:, 0:128 * nseg].rearrange(
                        "p (s n) -> p s n", s=nseg), AX.X, ALU.max).then_inc(S["sm_free"], 1)

                def minus_max(e):
                    dve.wait_ge(S["sm_free"], same(qb, b, NH) + 8 * e + 8)
                    half_nm = nm[:, 8 * e:8 * e + 8, :]
                    if qb == 1:
                        if e == 0:
                            dve.wait_ge(S["cn_ready"], b + 1)
                            v.tensor_reduce(cm[:, :], bank[AUX][0:32, :].rearrange("p (h n) -> p h n", n=32), AX.X,
                                            ALU.max).then_inc(S["cn_free"], 1)
                        v.tensor_tensor(half_nm[:, :, 1], half_nm[:, :, 0], half_nm[:, :, 1],
                                        ALU.max).then_inc(S["cn_free"], 1)
                        if e == 0:
                            dve.wait_ge(S["cn_free"], b * 5 + 1)
                        v.tensor_tensor(half_nm[0:32, :, 3], half_nm[0:32, :, 3], cm[:, 8 * e:8 * e + 8],
                                        ALU.max).then_inc(S["cn_free"], 1)
                        dve.wait_ge(S["cn_free"], b * 5 + 3 + 2 * e)
                    v.tensor_scalar(mx[:, 4 * e:4 * e + 4, :].rearrange("p g (f r) -> p (g f) r", f=2)[
                        :, :, MAXROW:MAXROW + 3], half_nm[:, :, nseg - 3:nseg], -1.0, None,
                        ALU.mult).then_inc(S["mx_ready"], 1)

                def max_rows(e):
                    dve.wait_ge(S["mt_ready"], same(qb, b, 2) + e + 1)
                    v.tensor_copy(QT[MAXROW:MAXROW + 3, 4 * e:4 * e + 4, 0, 128 * qb:128 * qb + 128],
                                  bank[AUX][MAXROW:MAXROW + 3, :].rearrange("p (g n) -> p g n", g=4)
                                  ).then_inc(S["mtv_done"], 1)

                def outputs(n):
                    dve.wait_ge(S["pv_done"], same(qb, b, NH) + 4 * n + 4)
                    O = bank[OUT + n % 2][:, 0:12 * (VD + 1)].rearrange("p (a n) -> p a n", n=VD + 1)
                    v.reciprocal(orec[:, n % 2, :], O[:, :, VD]).then_inc(S["dve"], 1)
                    dve.wait_ge(S["dve"], D["attn"][qb] + b * 2 * NGRP + 2 * n + 1)
                    v.tensor_tensor(ow[:, n % 2, :].rearrange("p (j h) -> p j h", j=3),
                                    orec[:, n % 2, :].rearrange("p (j h) -> p j h", j=3),
                                    gate[:, b, :].unsqueeze(2).broadcast_to([128, 3, 4]),
                                    ALU.mult).then_inc(S["dve"], 1)
                    dve.wait_ge(S["dve"], D["attn"][qb] + b * 2 * NGRP + 2 * n + 2)
                    if n >= 2:
                        dve.wait_ge(S["oc_ready"], same(qb, b, NGRP) + n)
                    v.tensor_tensor(oprod[:, n % 2, :, :], O[:, :, 0:VD],
                                    ow[:, n % 2, :].unsqueeze(2).broadcast_to([128, 12, VD]),
                                    ALU.mult).then_inc(S["o_free"], 1)

                def slot(t):
                    if t == 2:
                        residual(b, qb)
                    for n in range(ND[qb]):
                        if unit_slot(qb, n) == t:
                            rotate(n)
                    for h in range(NH):
                        if max_slot(h) == t:
                            maxima(h)
                            if h % 8 == 7:
                                minus_max(h // 8)
                    if t in MT_SLOTS:
                        max_rows(MT_SLOTS.index(t))
                    if t >= E_SLOT + 4 and (t - E_SLOT) % 4 == 0:
                        outputs((t - E_SLOT) // 4 - 1)

                for t in range(SLOTS):
                    if steps:
                        steps[0](b * SLOTS, t)
                    if t > 0:
                        slot(t - 1)
                    if steps:
                        steps[1](b * SLOTS, t)
                slot(SLOTS - 1)

            def tail(qb):
                residual(NB, qb)
                dve.wait_ge(S["x2_done"], (NB + 1) * (qb + 1))
                D["xn2"].append(layer_norm(xn, x2, qb, TB))
                cols = slice(128 * qb, 128 * qb + 128)
                dve.wait_ge(S["tail"], 2 * qb + 2)
                v.tensor_copy(xn2T[0:CH, cols, :].rearrange("p t b -> p b t"),
                              bank[0][0:CH, :].rearrange("p (b n) -> p b n", b=NB)).then_inc(S["tail_done"], 1)

            def step_start(t, s):
                prev = (s - 1) % (2 * STEPS)
                dve.wait_ge(S["h_ready"], t + s + 1)
                v.scalar_tensor_tensor(out=scan[:, 18:30:3], in0=hh[0:CH, prev, :], scalar=0.5,
                                       in1=bank[CELL][0:CH, 2:12:3], op0=ALU.mult,
                                       op1=ALU.mult).then_inc(S["hc_ready"], 1)

            def step_end(t, s):
                slot = s % (2 * STEPS)
                dve.wait_ge(S["hc_ready"], t + s + 1)
                dve.wait_ge(S["t_gate"], t + s + 1)
                v.tensor_tensor_scan(bank[CELL][0:CH, 0:12], scan[:, 0:12], scan[:, 16:28], 0.0, ALU.mult,
                                     ALU.add).then_inc(S["c_new"], 1)
                dve.wait_ge(S["t_cell"], t + s + 1)
                if s % STEPS == 0:
                    dve.wait_ge(S["hs_ready"], chunk(t) + s // STEPS + 1)
                v.scalar_tensor_tensor(out=hh[0:CH, slot, :], in0=scan[:, 30:42:3], scalar=1.0,
                                       in1=bank[CELL][0:CH, 16:20], op0=ALU.add, op1=ALU.mult).then_inc(S["h_ready"], 1)

            D["attn"], D["xn2"] = [count[0]], []
            with dve.Fori(0, NB) as b:
                attention(b, 0, None)
            count[0] += NB * 2 * NGRP
            tail(0)
            D["attn"].append(count[0])
            dve.wait_ge(S["pool_c"], D["const"])
            v.memset(bank[CELL][0:CH, 0:12], 0.0).then_inc(S["h_ready"], 1)
            with dve.Fori(0, NB) as b:
                chunk = lambda t: b * (SLOTS // STEPS)
                attention(b, 1, (step_start, step_end))
            count[0] += NB * 2 * NGRP
            tail(1)
            with dve.Fori(0, T // TB // STEPS // 2) as kk:
                k = kk * 2 + T // TB // STEPS
                chunk = lambda t: k
                for s in range(2 * STEPS):
                    step_start(k * STEPS, s)
                    step_end(k * STEPS, s)

        @block.scalar
        def _(act):
            a_ = nc.scalar
            for k in later:
                r0, r1 = PLACED.get(k, (0, d[k].shape[0]))
                act.dma_start(c[k][r0:r1], d[k][...]).then_inc(S["w_ready"], 16)

            for e in range(4):
                act.wait_ge(S["dve"], D[f"cmax{e}"])
                for i in range(2):
                    a = 2 * e + i
                    a_.activation(cp[:, a, :], bank[E_BANK[e]][:, 256 * i:256 * i + 256], ACT.Exp,
                                  bias=cmax[:, a:a + 1], accum_out=csum[:, a:a + 1]).then_inc(S["act"], 1)
            for e in range(2):
                act.wait_ge(S["pe"], PE[f"ptr{2 * e + 1}"])
                a_.activation(cpt[:, 4 * e + 2:4 * e + 4, :, :],
                              bank[P_BANK[2 * e + 1]][:, :].rearrange("p (a k n) -> p a k n", a=2, k=2),
                              ACT.Copy).then_inc(S["act"], 1)
            act.wait_ge(S["dve"], D["gsm"])
            a_.activation(gate[:, :, :], gsm[:, :, :], ACT.Exp, scale=1.0 / T).then_inc(S["act"], 1)

            def ot_copy(b, qb, g):
                act.wait_ge(S["ot_ready"], turned(qb, b) + g + 2)
                a_.activation(oT[:, g % NGRP, :], bank[AUX][:, 0:128], ACT.Copy).then_inc(S["ot_done"], 1)

            def attention(b, qb, step):
                def keep():
                    act.wait_ge(S["rp_done"], before(qb, b, NR) + NR[qb])
                    a_.activation(ks_kept[:, b, :, :], KS[:, :, :], ACT.Copy).then_inc(S["kept"], 1)

                def restore(t):
                    if t == 0:
                        act.wait_ge(S["pjd_ready"], before(qb, b, ND) + 1)
                        act.wait_ge(S["kept"], NB * 4)
                    dst, src = ((KS[:, :, :], ks_kept[:, b, :, :]),
                                (KW[:, :, 128 - WINDOW:128], kw_kept[:, b, :, :]),
                                (V1[:, 0, :, 0:VD], v1_kept[:, b]),
                                (VW[128 - WINDOW:, 0, :, 0:VD], vw_kept[:, b]))[RESTORE_SLOTS.index(t)]
                    a_.activation(dst, src, ACT.Copy).then_inc(S["restored"], 1)

                def values(m):
                    act.wait_ge(S["pja_ready"], before(qb, b, NV) + m + 1)
                    if qb == 0 and m < 2:
                        r, kept = ((0, v1_kept), (128 - WINDOW, vw_kept))[m]
                        a_.activation(kept[:, b], bank[AUX][r:, :].rearrange("p (h v) -> p h v", v=VD),
                                      ACT.Copy).then_inc(S["kept"], 1)
                    a_.activation(VALUES[qb][m][0][:, :, 0:VD], bank[AUX][:, :].rearrange("p (h v) -> p h v", v=VD),
                                  ACT.Copy).then_inc(S["pja_free"], 1)

                def max_rows(e):
                    act.wait_ge(S["mtv_done"], same(qb, b, 2) + e + 1)
                    a_.activation(QT[64 + MAXROW:64 + MAXROW + 3, 4 * e:4 * e + 4, 1, 128 * qb:128 * qb + 128],
                                  bank[AUX][64 + MAXROW:64 + MAXROW + 3, :].rearrange("p (g n) -> p g n", g=4),
                                  ACT.Copy).then_inc(S["mta_done"], 1)

                def exponentials(h):
                    cols = 128 * (3 + qb)
                    act.wait_ge(S["st_ready"], same(qb, b, NH) + h + 1)
                    if h >= 3:
                        act.wait_ge(S["pv_done"], same(qb, b, NH) + h - 2)
                    a_.activation(et[:, h % 3, 0:cols], bank[(h + 1) % RING][:, 0:cols], ACT.Exp,
                                  scale=SCALE).then_inc(S["ex_done"], 1)

                def corner(e):
                    act.wait_ge(S["ec_ready"], b * 2 + e + 1)
                    a_.activation(etc[96:128, 8 * e:8 * e + 8, :],
                                  bank[AUX][96:128, 0:256].rearrange("p (h n) -> p h n", n=32),
                                  ACT.Exp, scale=SCALE).then_inc(S["ec_done"], 1)

                for t in range(SLOTS):
                    if step:
                        step(b * SLOTS, t)
                    if t == 1:
                        ot_copy(b, qb, -1)
                    if 0 <= t - FIRST_VALUES < NV[qb]:
                        values(t - FIRST_VALUES)
                    if t in RESTORE_SLOTS and qb == 1:
                        restore(t)
                    if t == P_SLOTS + 2 and qb == 0:
                        keep()
                    if t in MT_SLOTS:
                        max_rows(MT_SLOTS.index(t))
                    if t in EC_SLOTS and qb == 1:
                        corner(EC_SLOTS.index(t))
                    if E_SLOT <= t < E_SLOT + NH:
                        exponentials(t - E_SLOT)
                    for g in range(NGRP - 1):
                        if out_slot(g) == t:
                            ot_copy(b, qb, g)

            def gates(src, n):
                dst = scan[:, 2:2 + 14 * n].rearrange("p (g x) -> p g x", g=n)[:, :, 0:12:3]
                a_.activation(dst, src.rearrange("p (g b) -> p g b", g=n), ACT.Tanh).then_inc(S["t_gate"], 1)

            def step(t, s):
                act.wait_ge(S["g_in"], t + s + 1)
                gates(bank[GATES][0:CH, 12 * (s % STEPS):12 * (s % STEPS) + 12], 3)
                cell(t, s)

            def step_alone(t, s, outputs_before):
                act.wait_ge(S["g_in"], t + s + 1)
                gates(bank[s // STEPS][0:CH, 8 * (s % STEPS):8 * (s % STEPS) + 8], 2)
                act.wait_ge(S["o_in"], outputs_before + s + 1)
                a_.activation(scan[:, 30:42:3], bank[2 + s // STEPS][0:CH, 4 * (s % STEPS):4 * (s % STEPS) + 4], ACT.Tanh)
                cell(t, s)

            def cell(t, s):
                act.wait_ge(S["c_new"], t + s + 1)
                a_.activation(bank[CELL][0:CH, 16:20], bank[CELL][0:CH, 2:12:3], ACT.Tanh,
                              scale=0.5).then_inc(S["t_cell"], 1)

            def tail(qb):
                ot_copy(NB, qb, -1)
                act.wait_ge(S["tail"], 2 * qb + 1)
                a_.activation(x2T[:, :, 128 * qb:128 * qb + 128],
                              bank[1][0:CH, :].rearrange("p (b n) -> p b n", b=NB), ACT.Copy
                              ).then_inc(S["tail_done"], 1)

            with act.Fori(0, NB) as b:
                attention(b, 0, None)
            tail(0)
            with act.Fori(0, NB) as b:
                attention(b, 1, step)
            tail(1)
            with act.Fori(0, T // TB // STEPS // 2) as kk:
                for s in range(2 * STEPS):
                    step_alone((kk * 2 + T // TB // STEPS) * STEPS, s, kk * 2 * STEPS)

        @block.tensor
        def _(pe):
            mm, tr = nc.tensor.matmul, nc.tensor.transpose

            def part(out, lhsT, rhs, start):
                return mm(out, lhsT, rhs, start=start, stop=True, skip_group_check=True)

            def done(name, ins):
                ins.then_inc(S["pe"], 1)
                order.append(name)
                assert len(order) == PE[name], name

            def keep_awake(n, o):
                for _ in range(n):
                    mm(o[:, :], idle16[:, 0:128], idle16[:, :], start=True, stop=True)

            order = []
            pe.wait_ge(S["pool_c"], 1)
            keep_awake(16, bank[7])
            pe.wait_ge(S["w_first"], 16 * nf)
            pe.wait_ge(S["dve"], D["gsum"])
            done("gsum", mm(bank[0][:, 0:4], c["pair"][:, :], gsum[:, :], start=True, stop=True))
            keep_awake(8, bank[7])
            pe.wait_ge(S["dve"], D["yc"])
            for i in range(2):
                n = mm(bank[i][0:CH, :], c["wqk"][:, i, :], yc[:, :, :].rearrange("p j n -> p (j n)"),
                       start=True, stop=True)
            done("qk", n)
            done("wvo", mm(bank[2][:, 0:CH], c["wv2"][:, :], c["wo9"][0:INNER, :], start=True, stop=True))
            keep_awake(2, bank[7])
            pe.wait_ge(S["dve"], D["wvo"])
            for a in range(8):
                b, kb = a // 2, a % 2
                r = 64 * (b % 2)
                part(bank[3 + b % 2][:, CH * (a // 4 * 2 + kb):CH * (a // 4 * 2 + kb) + CH],
                     yc[r:r + 64, b // 2, 128 * kb:128 * kb + 128], wvo[r:r + 64, :], a % 4 == 0 and a < 4 or a == 2)
            mm(bank[6][:, 0:CH], c["bv9"][:, :], c["wo9"][:, :], start=True, stop=True)
            for a in range(4):
                n = tr(bank[5][:, 128 * a:128 * a + 128], xc[:, a // 2, 128 * (a % 2):128 * (a % 2) + 128], ident[:, :])
            done("vw", n)
            keep_awake(6, bank[7])
            pe.wait_ge(S["dve"], D["xtok"])
            for b in range(NB):
                r, j = 32 * (b % 2), b // 2
                for i in range(TB):
                    n = part(bank[E_BANK[b]][:, 256 * i:256 * i + 256], qc[r:r + INNER, j, 128 * i:128 * i + 128],
                             kc[r:r + INNER, j, :], i == 0)
                done(f"energy{b}", n)
            for b in range(NB):
                pe.wait_ge(S["act"], 2 * b + 2)
                for i in range(4):
                    n = tr(bank[P_BANK[b]][:, 128 * i:128 * i + 128],
                           cp[:, 2 * b + i // 2, 128 * (i % 2):128 * (i % 2) + 128], ident[:, :])
                done(f"ptr{b}", n)
            keep_awake(3, bank[7])
            pe.wait_ge(S["dve"], D["cpt2"])
            pe.wait_ge(S["act"], A_["cpt3"])
            for a in range(8):
                for kb in range(TB):
                    n = part(bank[2][:, CH * a:CH * a + CH], cpt[:, a, kb, :], vw[:, a // 2 * 2 + kb, :],
                             a == 0 and kb == 0)
            done("pv", n)

            def token_transposes(src, rows, banks, names, sem_done):
                for e in range(2):
                    for i in range(4):
                        n = tr(bank[banks[e]][0:rows, 128 * i:128 * i + 128], src[:, 4 * e + i, :], ident[:, :])
                    if sem_done is None:
                        done(names[e], n)
                    else:
                        n.then_inc(sem_done, 1)

            keep_awake(26, bank[7])
            pe.wait_ge(S["dve"], D["xn"])
            token_transposes(xn, CH, (0, 1), ("xnT0", "xnT1"), None)
            keep_awake(4, bank[7])
            pe.wait_ge(S["dve"], D["xnT"])
            pe.wait_ge(S["w_ready"], 16 * nw)
            for a in range(8):
                n = part(bank[2][:, NCAT * a:NCAT * a + NCAT], tokT[0:CH, a // 2, 128 * (a % 2):128 * (a % 2) + 128],
                         c["wcat"][:, :], a == 0)
            done("cat", n)
            keep_awake(20, bank[7])
            pe.wait_ge(S["dve"], D["cqn"])
            pe.wait_ge(S["pool_c"], D["const"])
            token_transposes(tok, 128, (3, 4), ("tokT0", "tokT1"), None)
            for t in range(TB):
                n = mm(bank[7][:, 0:3 * NB], ones[:, :], cat[:, t:8:2, GATE:GATE + 3], start=t == 0, stop=t == 1)
            done("gate", n)
            pe.wait_ge(S["dve"], D["diag"])
            for a in range(8):
                n = part(bank[a // 4][:, 128 * (a % 4):128 * (a % 4) + 128], ones[:, :], diag[:, a, :], a % 4 == 0)
            done("srow", n)
            keep_awake(30, bank[6])
            pe.wait_ge(S["dve"], D["sel"])
            part(bank[2][:, 0:NB], c["lt"][:, :], sel[:, :, 0], True)
            part(bank[2][:, NB:2 * NB], c["lt"][:, :], sel[:, :, 1], False)
            done("pos", part(bank[2][:, NB:2 * NB], ones[:, :], sel[:, :, 0], False))
            keep_awake(8, bank[6])
            pe.wait_ge(S["dve"], D["psel"])
            for a in range(8):
                n = part(bank[3][0:CH, KEEP * (a // 2):KEEP * (a // 2) + KEEP], xn[:, a, :], diag[:, a, :], a == 0)
            done("selT", n)

            def out_t(b, qb, g):
                pe.wait_ge(S["oc_ready"], same(qb, b, NGRP) + g + 2)
                if g >= 1:
                    pe.wait_ge(S["ot_done"], turned(qb, b) + g + 1)
                elif g == 0 and qb == 0:
                    pe.wait_ge(S["mta_done"], same(qb, b, 2) + 2)
                tr(bank[AUX][:, 0:128], osum[:, g % 2, 1, :], ident[:, :]).then_inc(S["ot_ready"], 1)

            def project_out(b, qb):
                pe.wait_ge(S["ot_done"], turned(qb, b) + 1)
                for g in range(NGRP):
                    last = mm(bank[AUX][:, 0:CH], oT[:, g, :], c["wproj"][:, g, :], start=g == 0, stop=g == NGRP - 1)
                last.then_inc(S["y_ready"], 1)

            def attention(b, qb, step):
                q, nk = slice(128 * qb, 128 * qb + 128), 128 * (qb + 1)

                def project(n):
                    kind, _, wa, wb, x, at = UNITS[qb][n]
                    o, w = unit_bank(qb, n), at.stop - at.start
                    if n >= RING:
                        pe.wait_ge(S["pjd_free"], before(qb, b, ND) + n - RING + 1)
                    for i in range(len(wa)):
                        last = part(o[:, w * i:w * i + w], wa[i], x, i == 0)
                    for i in range(len(wb)):
                        last = part(o[:, T + w * i:T + w * i + w], wb[i], x, False)
                    last.then_inc(S["pjd_ready"], 1)

                def values_in(m):
                    if m == 0:
                        pe.wait_ge(S["x2_done"], same(qb, b, 1) + qb + 1)
                    else:
                        pe.wait_ge(S["pja_free"], before(qb, b, NV) + m)
                    _, x, w = VALUES[qb][m]
                    mm(bank[AUX][:, :], x, w[:, :], start=True, stop=True).then_inc(S["pja_ready"], 1)

                def scores(h):
                    Q, p, o = QT[:, h // 2, h % 2, q], h // 2, bank[h % RING]
                    if h % 4 == 0:
                        pe.wait_ge(S["rp_done"], before(qb, b, NR) + 1 + NG[qb] * (h // 4 + 1))
                    if h == 0 and qb == 1:
                        pe.wait_ge(S["restored"], b * 4 + 4)
                    if h < RING:
                        pe.wait_ge(S["pjd_free"], before(qb, b, ND) + ND[qb] - RING + 1 + h)
                    else:
                        pe.wait_ge(S["sm_free"], same(qb, b, NH) + h - RING + 1)
                    part(o[:, 0:nk], Q, K1[:, p, 0:nk], True)
                    part(o[:, nk:nk + 128], Q, KS[:, p, :], False)
                    part(o[:, nk + 128:nk + 256], Q, KW[:, p, q], False)
                    part(o[:, nk - 128:nk], ident16[:, :], masks16[:, 0, :], False)
                    part(o[:, nk + 128:nk + 256], ident16[:, :], masks16[:, 2, :], False).then_inc(S["sm_ready"], 1)

                def corner():
                    pe.wait_ge(S["pja_free"], before(qb, b, NV) + NV[qb])
                    pe.wait_ge(S["rp_done"], before(qb, b, NR) + NR[qb])
                    for h in range(NH):
                        o = bank[AUX][0:32, 32 * h:32 * h + 32]
                        part(o, QT[:, h // 2, h % 2, 128:160], KW[:, h // 2, 96:128], h == 0)
                    part(bank[AUX][0:32, :].rearrange("p (h n) -> p h n", n=32), ident16[0:32, 0:32],
                         corner16[0:32, 0:1, :].broadcast_to([32, NH, 32]), False).then_inc(S["cn_ready"], 1)

                def max_transposes(e):
                    pe.wait_ge(S["mx_ready"], same(qb, b, 2) + e + 1)
                    if e == 0:
                        pe.wait_ge(S["pja_free"], before(qb, b, NV) + NV[qb])
                    elif qb == 0:
                        pe.wait_ge(S["mta_done"], same(qb, b, 2) + 1)
                    else:
                        pe.wait_ge(S["ec_done"], b * 2 + 1)
                    for p in range(4):
                        last = tr(bank[AUX][:, 128 * p:128 * p + 128], mx[:, 4 * e + p, :], ident[:, :])
                    last.then_inc(S["mt_ready"], 1)

                def scores_t(h):
                    Q, p, o = QT[:, h // 2, h % 2, q], h // 2, bank[(h + 1) % RING]
                    if h % 8 == 0:
                        pe.wait_ge(S["mta_done"], same(qb, b, 2) + h // 8 + 1)
                    if h < RING:
                        pe.wait_ge(S["sm_free"], same(qb, b, NH) + NH - RING + 1 + h)
                    else:
                        pe.wait_ge(S["ex_done"], same(qb, b, NH) + h - RING + 1)
                    for kb in range(qb + 1):
                        part(o[:, 128 * kb:128 * kb + 128], K1[:, p, 128 * kb:128 * kb + 128], Q, kb == 0)
                    part(o[:, nk:nk + 128], KS[:, p, :], Q, False)
                    part(o[:, nk + 128:nk + 256], KW[:, p, q], Q, False)
                    part(o[:, nk - 128:nk], ident16[:, :], masks16[:, 1, :], False)
                    part(o[:, nk + 128:nk + 256], ident16[:, :], masks16[:, 3, :], False).then_inc(S["st_ready"], 1)

                def corner_t(e):
                    pe.wait_ge(S["mta_done"], same(qb, b, 2) + e + 1)
                    for h in range(8 * e, 8 * e + 8):
                        o = bank[AUX][96:128, 32 * (h % 8):32 * (h % 8) + 32]
                        part(o, KW[:, h // 2, 96:128], QT[:, h // 2, h % 2, 128:160], h % 8 == 0)
                    part(bank[AUX][96:128, 0:256].rearrange("p (h n) -> p h n", n=32), ident16[96:128, 96:128],
                         corner16[96:128, 1:2, :].broadcast_to([32, 8, 32]), False).then_inc(S["ec_ready"], 1)

                def values(h):
                    g = h // 4
                    pe.wait_ge(S["ex_done"], same(qb, b, NH) + h + 1)
                    if h % 8 == 0 and qb == 1:
                        pe.wait_ge(S["ec_done"], b * 2 + h // 8 + 1)
                    if h % 4 == 0 and g >= 2:
                        pe.wait_ge(S["o_free"], same(qb, b, NGRP) + g - 1)
                    o = [bank[OUT + g % 2][:, (4 * j + h % 4) * (VD + 1):(4 * j + h % 4 + 1) * (VD + 1)]
                         for j in range(3)]
                    e = [et[:, h % 3, 128 * i:128 * i + 128] for i in range(4)]
                    for kb in range(qb + 1):
                        part(o[0], e[kb], V1[:, kb, h, :], kb == 0)
                    part(o[1], e[qb + 1], VS[:, h, :], True)
                    last = part(o[2], e[qb + 2], VW[:, qb, h, :], True)
                    if qb == 1:
                        last = part(o[2][0:32, :], etc[96:128, h, :], VW[96:128, 0, h, :], False)
                    last.then_inc(S["pv_done"], 1)

                pe.wait_ge(S["staged"], same(qb, b, 2) + 2)
                for t in range(SLOTS):
                    if step:
                        step(b * SLOTS, t)
                    for n in range(ND[qb]):
                        if unit_slot(qb, n) == t:
                            project(n)
                    if t == 1:
                        out_t(b, qb, -1)
                    if t == 2:
                        project_out(b, qb)
                    if 0 <= t - FIRST_VALUES < NV[qb]:
                        values_in(t - FIRST_VALUES)
                    for h in range(NH):
                        if max_slot(h) == t:
                            scores(h)
                    if t == P_SLOTS + 2 and qb == 1:
                        corner()
                    if t in MT_SLOTS:
                        max_transposes(MT_SLOTS.index(t))
                    if t in EC_SLOTS and qb == 1:
                        corner_t(EC_SLOTS.index(t))
                    if E_SLOT <= t < E_SLOT + NH:
                        scores_t(t - E_SLOT)
                    if E_SLOT < t <= E_SLOT + NH:
                        values(t - E_SLOT - 1)
                    for g in range(NGRP - 1):
                        if out_slot(g) == t:
                            out_t(b, qb, g)
                pe.wait_ge(S["ot_done"], turned(qb, b) + NGRP)

            def tail(qb):
                out_t(NB, qb, -1)
                project_out(NB, qb)
                pe.wait_ge(S["x2_done"], (NB + 1) * (qb + 1))
                for i, src in enumerate((x2, xn)):
                    if i == 1:
                        keep_awake(22, bank[7])
                        pe.wait_ge(S["dve"], D["xn2"][qb])
                    for b in range(NB):
                        n = tr(bank[1 - i][0:CH, 128 * b:128 * b + 128], src[:, TB * b + qb, :], ident[:, :])
                    n.then_inc(S["tail"], 1)
                pe.wait_ge(S["tail_done"], 2 * qb + 2)

            def gate_inputs(o, first, gates):
                n = len(gates)
                for i, g in enumerate(gates):
                    part(o[0:CH, 0:4 * n * STEPS].rearrange("p (t g b) -> p t g b", g=n, b=NB)[:, :, i, :],
                         u_half[:, g, :], xn2T[:, bass.ds(first, STEPS), :], i == 0)

            def state_part(o, s, gates):
                for i, g in enumerate(gates):
                    at = 4 * (len(gates) * (s % STEPS) + i)
                    last = part(o[0:CH, at:at + 4], v_half[:, g, :], hh[:, (s - 1) % (2 * STEPS), :], False)
                return last

            def step_beside(t, s):
                pe.wait_ge(S["h_ready"], t + s + 1)
                if s % STEPS == 0:
                    gate_inputs(bank[GATES], t + s, (0, 1, 2))
                state_part(bank[GATES], s, (0, 1, 2)).then_inc(S["g_in"], 1)

            with pe.Fori(0, NB) as b:
                attention(b, 0, None)
            tail(0)
            with pe.Fori(0, NB) as b:
                attention(b, 1, step_beside)
            tail(1)
            gate_inputs(bank[0], T // TB, (0, 1))
            gate_inputs(bank[2], T // TB, (2,))
            with pe.Fori(0, T // TB // STEPS // 2) as kk:
                k = kk * 2 + T // TB // STEPS
                for s in range(2 * STEPS):
                    pe.wait_ge(S["h_ready"], k * STEPS + s + 1)
                    u = s // STEPS
                    state_part(bank[u], s, (0, 1)).then_inc(S["g_in"], 1)
                    state_part(bank[2 + u], s, (2,)).then_inc(S["o_in"], 1)
                    if s % STEPS == 0:
                        gate_inputs(bank[1 - u], (k + u + 1) * STEPS, (0, 1))
                        gate_inputs(bank[3 - u], (k + u + 1) * STEPS, (2,))
                    keep_awake(AWAKE, bank[5])


def _host(inputs):
    import numpy as np
    i = {k: np.asarray(v) for k, v in inputs.items()}
    f = np.float32
    a = {"x": i["x"].reshape(NB, CH, T)}
    wqk = np.zeros((2, CH, 2, 2, 32), f)
    bqk = np.zeros((2, 32, 2), f)
    for n, (w, b) in enumerate((("wq", "bq"), ("wk", "bk"))):
        for h in range(2):
            wqk[h, :, n, h, :INNER] = i["L0_conv_" + w].T
            bqk[h, :INNER, n] = i["L0_conv_" + b]
    a["wqk"] = wqk.reshape(128, 2, 64)
    a["bqk"] = bqk.reshape(64, 2)
    a["wv2"] = np.concatenate([i["L0_conv_wv"]] * 2, 1)
    a["wo9"] = np.concatenate([i["L0_conv_wo"].T, i["L0_conv_bo"][None]], 0)
    a["bv9"] = np.concatenate([np.repeat(i["L0_conv_bv"][:, None], 128, 1), np.ones((1, 128), f)], 0)
    a["wcat"] = np.concatenate([i["L1_attn_" + n] for n in ("Wcq", "Wckv", "W_imp", "Wgate")], 1)
    a["qkn"] = np.ones((128, 1), f)
    a["qkn"][QROW:ONEROW, 0], a["qkn"][KROW:, 0] = i["L1_attn_q_norm_w"], i["L1_attn_kv_norm_w"]

    def heads(rows, nope, rope, one):
        w = np.zeros((2, rows, NP, 2, 64), f)
        if nope is not None:
            w[0, :len(nope), :, :, 0:NOPE] = nope.reshape(-1, NP, 2, NOPE)
        if rope is not None:
            r = rope.reshape(-1, NP, 2, 2, ROPE // 2)
            w[0, :len(rope), :, :, ROPEROW:] = r.reshape(-1, NP, 2, ROPE)
            w[1, :len(rope), :, :, ROPEROW:] = r[:, :, :, ::-1].reshape(-1, NP, 2, ROPE)
        if one is not None:
            w[0, ONEROW, :, :, MAXROW + one] = 1.0
        return w.reshape(2, rows, NP, 128)

    a["wqa"], a["wqb"] = heads(KROW - QROW, i["L1_attn_Wq_nope"], i["L1_attn_Wq_rope"], None)
    a["wk1"] = heads(RKV, i["L1_attn_Wk_nope"], None, None)[0]
    kr = heads(KROW, None, np.repeat(i["L1_attn_Wk_rope"][:, None], NH, 1), 0)
    a["wkr"] = np.ascontiguousarray(kr[:, :, 0, :].transpose(1, 0, 2))
    for n, src, one in (("ww", "Wwin_k", 2), ("ws", "Wsel_k", 1)):
        w = i["L1_attn_" + src].reshape(CH, NH, HD)
        a[n + "a"], a[n + "b"] = heads(KROW, w[..., :NOPE], w[..., NOPE:], one)
    a["wv1"], a["wwv"], a["wsv"] = (i["L1_attn_" + n] for n in ("Wv", "Wwin_v", "Wsel_v"))
    a["wproj"] = i["L1_attn_Wproj"].reshape(NGRP, 128, CH).transpose(1, 0, 2)
    a["u3"] = np.stack([np.concatenate([i["L1_ffn_U_" + g], i["L1_ffn_b_" + g][None]], 0) for g in "cio"], 1)
    a["v3"] = np.stack([np.concatenate([i["L1_ffn_V_" + g], np.zeros((128 - CH, CH), f)], 0) for g in "cio"], 1)

    p = np.arange(128)
    a["ident"], a["ones"] = np.eye(128, dtype=f), np.ones((128, 128), f)
    a["pair"] = np.where(p[:, None] // 2 == p[None] // 2, 0.5, 0.0).astype(f)
    a["lt"] = (p[:, None] < p[None]).astype(f)
    j = np.arange(T)
    a["tie"] = (j[None, None] < (128 * np.arange(TB)[None, :, None] + p[:, None, None])).astype(f)
    a["iota"] = np.broadcast_to(p.astype(f)[None], (128, 128))
    freq = 1.0 / 10000.0 ** (np.arange(0, ROPE, 2, dtype=np.float32) / ROPE)
    ang = np.outer(np.arange(T, dtype=np.float32), freq)
    cos, sin = np.ones((2, 64, T), f), np.zeros((2, 64, T), f)
    half = ROPE // 2
    for k in range(2):
        cos[:, ROPEROW + half * k:ROPEROW + half * k + half] = np.cos(ang).T
        sin[:, ROPEROW + half * k:ROPEROW + half * k + half] = (-1, 1)[k] * np.sin(ang).T
    a["cos"], a["sin"] = cos.reshape(128, T), sin.reshape(128, T)
    low = f(-1e30)
    d = p[:, None] - p[None]
    causal, window = np.where(d >= 0, f(0), low), np.where((d >= 0) & (d < WINDOW), f(0), low)
    a["masks"] = np.stack([causal, causal.T, window, window.T], 1)
    r = np.arange(32)
    corner = np.where(r[None] > r[:, None], f(0), low)
    a["corner"] = np.zeros((128, 2, 32), f)
    a["corner"][0:32, 0] = corner
    a["corner"][96:128, 1] = corner.T
    return {k: np.ascontiguousarray(v, dtype=v.dtype) for k, v in a.items()}


def kernel(**inputs):
    import concourse.bacc as _bacc
    from concourse.bass_utils import run_bass_kernel_spmd as _run

    arrays = _host(inputs)
    nc = _bacc.Bacc("TRN2", target_bir_lowering=False, num_devices=1)
    d = {k: nc.dram_tensor(k + "_dram", v.shape, mybir.dt.from_np(v.dtype), kind="ExternalInput").ap()
         for k, v in arrays.items()}
    out = nc.dram_tensor("out_dram", (NB, CH, T), F32, kind="ExternalOutput").ap()
    conv_attn_lstm(nc, d, out)
    r = _run(nc, [{k + "_dram": v for k, v in arrays.items()}], core_ids=[0])
    return r.results[0]["out_dram"].reshape(NB, CH, 16, 16)
```
